# Optimizing a Trainium2 kernel written in Bass

```python
import numpy as np
import jax
import jax.numpy as jnp

def _softmax(x, axis=-1):
    return jax.nn.softmax(x, axis=axis)

def _gelu(x):
    return jax.nn.gelu(x, approximate=True)

def _silu(x):
    return jax.nn.silu(x)

def _sigmoid(x):
    return jax.nn.sigmoid(x)

def _layernorm(x, axis=-1, eps=1e-05):
    m = jnp.mean(x, axis=axis, keepdims=True)
    v = jnp.var(x, axis=axis, keepdims=True)
    return (x - m) / jnp.sqrt(v + eps)

def _scatter_add(tgt, idx, src, axis=0):
    return tgt.at[idx].add(src)

def _segment_sum(src, seg, n):
    return jax.ops.segment_sum(src, seg, n)
kernel_name = 'mk_gnn_resnorm_d4_gnn_r32_991eb0'

def setup_inputs(seed: int=0):
    np.random.seed(seed)
    _w = jnp.asarray

    def _rec_inputs():
        import jax
        import jax.numpy as jnp
        _gk = jax.random.key(seed)
        x = -0.000202 + 1 * jax.random.normal(jax.random.fold_in(_gk, 1), (3125, 64), jnp.float32)
        _s = jax.random.randint(jax.random.fold_in(_gk, 2), (50000,), 0, 3125, jnp.int32)
        _d = jax.random.randint(jax.random.fold_in(_gk, 3), (50000,), 0, 3125, jnp.int32)
        _loop = jnp.arange(3125, dtype=jnp.int32)
        src = jnp.concatenate([_s, _d, _loop])
        dst = jnp.concatenate([_d, _s, _loop])
        _o = jnp.argsort(dst, stable=True)
        src = src[_o]
        dst = dst[_o]
        edge_attr_10 = 0.000262864 + 0.999894 * jax.random.normal(jax.random.fold_in(_gk, 12), (103125, 10), jnp.float32)
        edge_attr_64 = 0.000189758 + 1.00013 * jax.random.normal(jax.random.fold_in(_gk, 13), (103125, 64), jnp.float32)
        node_vec = -0.00472126 + 0.997171 * jax.random.normal(jax.random.fold_in(_gk, 15), (3125,), jnp.float32)
        return (x, src, dst, edge_attr_10, edge_attr_64, node_vec)
    x, src, dst, edge_attr_10, edge_attr_64, node_vec = _rec_inputs()

    def _L0_gnn_setup():
        import jax, jax.numpy as jnp
        import numpy as np
        N = 3125
        E = 50000
        D = 64
        key = jax.random.key(seed)
        k1, k2, k3, k4, k5, k6, k7 = jax.random.split(key, 7)
        x = jax.random.normal(k1, (N, D), dtype=jnp.float32)
        edge_index = jax.random.randint(k2, (2, E), 0, N, dtype=jnp.int64)
        curvature = jax.random.normal(k3, (N,), dtype=jnp.float32)
        W_curv = jax.random.normal(k4, (D, 1), dtype=jnp.float32) / jnp.sqrt(1.0)
        b_curv = jax.random.normal(k5, (D,), dtype=jnp.float32) * 0.01
        W_lin = jax.random.normal(k6, (D, D), dtype=jnp.float32) / jnp.sqrt(D)
        b_lin = jax.random.normal(k7, (D,), dtype=jnp.float32) * 0.01
        return {'x': x, 'curvature': curvature, 'W_curv': W_curv, 'b_curv': b_curv, 'W_lin': W_lin, 'b_lin': b_lin, 'edge_index': edge_index}
    _L0_gnn_all = _L0_gnn_setup()
    _L0_gnn_in = {k: v for k, v in _L0_gnn_all.items() if k in ('W_curv', 'b_curv', 'W_lin', 'b_lin')}
    del _L0_gnn_all

    def _L1_gnn_setup():
        import jax, jax.numpy as jnp
        import numpy as np
        N_NODES = 50000
        N_EDGES = 25000
        N_GRAPHS = 128
        D = 64
        key = jax.random.key(seed)
        ks = jax.random.split(key, 8)
        x = jax.random.normal(ks[0], (N_NODES, D), dtype=jnp.float32)
        edge_index = jax.random.randint(ks[1], (2, N_EDGES), 0, N_NODES, dtype=jnp.int64)
        edge_attr = jax.random.normal(ks[2], (N_EDGES, D), dtype=jnp.float32)
        u = jax.random.normal(ks[3], (N_GRAPHS, D), dtype=jnp.float32)
        batch = jnp.sort(jax.random.randint(ks[4], (N_NODES,), 0, N_GRAPHS, dtype=jnp.int64))
        W1 = jax.random.normal(ks[5], (3 * D, D), dtype=jnp.float32) * (1.0 / np.sqrt(3 * D))
        b1 = jnp.zeros((D,), dtype=jnp.float32)
        W2 = jax.random.normal(ks[6], (D, D), dtype=jnp.float32) * (1.0 / np.sqrt(D))
        b2 = jnp.zeros((D,), dtype=jnp.float32)
        return {'x': x, 'edge_index': edge_index, 'edge_attr': edge_attr, 'u': u, 'batch': batch, 'W1': W1, 'b1': b1, 'W2': W2, 'b2': b2}
    _L1_gnn_all = _L1_gnn_setup()
    _L1_gnn_in = {k: v for k, v in _L1_gnn_all.items() if k in ('u', 'W1', 'b1', 'W2', 'b2')}
    del _L1_gnn_all

    def _L2_gnn_setup():
        import jax, jax.numpy as jnp
        import numpy as np
        N_NODES = 3125
        N_EDGES = 31250
        H = 64
        N_LAYERS = 5
        EPS = 1e-05

        def layer_norm(x, g, b):
            m = jnp.mean(x, axis=-1, keepdims=True)
            v = jnp.var(x, axis=-1, keepdims=True)
            return (x - m) * jax.lax.rsqrt(v + EPS) * g + b

        def sage_conv(x, src, dst, n_nodes, wl, bl, wr):
            xj = x[src]
            deg = jax.ops.segment_sum(jnp.ones((src.shape[0], 1), x.dtype), dst, num_segments=n_nodes)
            amax = jax.ops.segment_max(xj, dst, num_segments=n_nodes)
            amax = jnp.where(deg > 0, amax, jnp.zeros_like(amax))
            amean = jax.ops.segment_sum(xj, dst, num_segments=n_nodes) / jnp.maximum(deg, 1.0)
            agg = jnp.concatenate([amax, amean], axis=-1)
            return agg @ wl.T + bl + x @ wr.T
        key = jax.random.key(seed)
        ks = jax.random.split(key, 8)
        x = jax.random.normal(ks[0], (N_NODES, H), dtype=jnp.float32)
        edge_index = jax.random.randint(ks[1], (2, N_EDGES), 0, N_NODES, dtype=jnp.int64)
        s = 0.05
        return {'x': x, 'edge_index': edge_index, 'conv_wl': jax.random.normal(ks[2], (N_LAYERS, H, 2 * H), jnp.float32) * s, 'conv_bl': jnp.zeros((N_LAYERS, H), jnp.float32), 'conv_wr': jax.random.normal(ks[3], (N_LAYERS, H, H), jnp.float32) * s, 'ln_g': jnp.ones((N_LAYERS, H), jnp.float32), 'ln_b': jnp.zeros((N_LAYERS, H), jnp.float32), 'adapter_w': jax.random.normal(ks[4], (H, H), jnp.float32) * s, 'adapter_b': jnp.zeros((H,), jnp.float32), 'mlp_w1': jax.random.normal(ks[5], (4 * H, H), jnp.float32) * s, 'mlp_b1': jnp.zeros((4 * H,), jnp.float32), 'mlp_ln_g': jnp.ones((4 * H,), jnp.float32), 'mlp_ln_b': jnp.zeros((4 * H,), jnp.float32), 'mlp_w2': jax.random.normal(ks[6], (H, 4 * H), jnp.float32) * s, 'mlp_b2': jnp.zeros((H,), jnp.float32)}
    _L2_gnn_all = _L2_gnn_setup()
    _L2_gnn_in = {k: v for k, v in _L2_gnn_all.items() if k in ('conv_wl', 'conv_bl', 'conv_wr', 'ln_g', 'ln_b', 'adapter_w', 'adapter_b', 'mlp_w1', 'mlp_b1', 'mlp_ln_g', 'mlp_ln_b', 'mlp_w2', 'mlp_b2')}
    del _L2_gnn_all

    def _L3_gnn_setup():
        import jax, jax.numpy as jnp
        import numpy as np
        N_NODES = 3125
        N_EDGES = 1250000
        IN_DIM = 64
        HID_DIM = 64
        EDGE_DIM = 10
        BN_EPS = 1e-05
        key = jax.random.key(seed)
        ks = jax.random.split(key, 10)
        x = jax.random.normal(ks[0], (N_NODES, IN_DIM), dtype=jnp.float32)
        edge_index = jax.random.randint(ks[1], (2, N_EDGES), 0, N_NODES, dtype=jnp.int64)
        edge_attr = jax.random.normal(ks[2], (N_EDGES, EDGE_DIM), dtype=jnp.float32)
        W_edge = jax.random.normal(ks[3], (EDGE_DIM, IN_DIM), dtype=jnp.float32) * (1.0 / np.sqrt(EDGE_DIM))
        b_edge = jnp.zeros((IN_DIM,), dtype=jnp.float32)
        W1 = jax.random.normal(ks[4], (IN_DIM, HID_DIM), dtype=jnp.float32) * (1.0 / np.sqrt(IN_DIM))
        b1 = jnp.zeros((HID_DIM,), dtype=jnp.float32)
        W2 = jax.random.normal(ks[5], (HID_DIM, HID_DIM), dtype=jnp.float32) * (1.0 / np.sqrt(HID_DIM))
        b2 = jnp.zeros((HID_DIM,), dtype=jnp.float32)
        bn_gamma = jnp.ones((HID_DIM,), dtype=jnp.float32)
        bn_beta = jnp.zeros((HID_DIM,), dtype=jnp.float32)
        return {'x': x, 'edge_index': edge_index, 'edge_attr': edge_attr, 'W_edge': W_edge, 'b_edge': b_edge, 'W1': W1, 'b1': b1, 'W2': W2, 'b2': b2, 'bn_gamma': bn_gamma, 'bn_beta': bn_beta}
    _L3_gnn_all = _L3_gnn_setup()
    _L3_gnn_in = {k: v for k, v in _L3_gnn_all.items() if k in ('W_edge', 'b_edge', 'W1', 'b1', 'W2', 'b2', 'bn_gamma', 'bn_beta')}
    del _L3_gnn_all
    return {'x': x, 'src': src, 'dst': dst, 'edge_attr_10': edge_attr_10, 'edge_attr_64': edge_attr_64, 'node_vec': node_vec, 'L0_gnn_W_curv': _L0_gnn_in['W_curv'], 'L0_gnn_b_curv': _L0_gnn_in['b_curv'], 'L0_gnn_W_lin': _L0_gnn_in['W_lin'], 'L0_gnn_b_lin': _L0_gnn_in['b_lin'], 'L1_gnn_u': _L1_gnn_in['u'], 'L1_gnn_W1': _L1_gnn_in['W1'], 'L1_gnn_b1': _L1_gnn_in['b1'], 'L1_gnn_W2': _L1_gnn_in['W2'], 'L1_gnn_b2': _L1_gnn_in['b2'], 'L2_gnn_conv_wl': _L2_gnn_in['conv_wl'], 'L2_gnn_conv_bl': _L2_gnn_in['conv_bl'], 'L2_gnn_conv_wr': _L2_gnn_in['conv_wr'], 'L2_gnn_ln_g': _L2_gnn_in['ln_g'], 'L2_gnn_ln_b': _L2_gnn_in['ln_b'], 'L2_gnn_adapter_w': _L2_gnn_in['adapter_w'], 'L2_gnn_adapter_b': _L2_gnn_in['adapter_b'], 'L2_gnn_mlp_w1': _L2_gnn_in['mlp_w1'], 'L2_gnn_mlp_b1': _L2_gnn_in['mlp_b1'], 'L2_gnn_mlp_ln_g': _L2_gnn_in['mlp_ln_g'], 'L2_gnn_mlp_ln_b': _L2_gnn_in['mlp_ln_b'], 'L2_gnn_mlp_w2': _L2_gnn_in['mlp_w2'], 'L2_gnn_mlp_b2': _L2_gnn_in['mlp_b2'], 'L3_gnn_W_edge': _L3_gnn_in['W_edge'], 'L3_gnn_b_edge': _L3_gnn_in['b_edge'], 'L3_gnn_W1': _L3_gnn_in['W1'], 'L3_gnn_b1': _L3_gnn_in['b1'], 'L3_gnn_W2': _L3_gnn_in['W2'], 'L3_gnn_b2': _L3_gnn_in['b2'], 'L3_gnn_bn_gamma': _L3_gnn_in['bn_gamma'], 'L3_gnn_bn_beta': _L3_gnn_in['bn_beta']}

def reference(x, src, dst, edge_attr_10, edge_attr_64, node_vec, L0_gnn_W_curv, L0_gnn_b_curv, L0_gnn_W_lin, L0_gnn_b_lin, L1_gnn_u, L1_gnn_W1, L1_gnn_b1, L1_gnn_W2, L1_gnn_b2, L2_gnn_conv_wl, L2_gnn_conv_bl, L2_gnn_conv_wr, L2_gnn_ln_g, L2_gnn_ln_b, L2_gnn_adapter_w, L2_gnn_adapter_b, L2_gnn_mlp_w1, L2_gnn_mlp_b1, L2_gnn_mlp_ln_g, L2_gnn_mlp_ln_b, L2_gnn_mlp_w2, L2_gnn_mlp_b2, L3_gnn_W_edge, L3_gnn_b_edge, L3_gnn_W1, L3_gnn_b1, L3_gnn_W2, L3_gnn_b2, L3_gnn_bn_gamma, L3_gnn_bn_beta):
    import jax
    import jax.numpy as jnp

    def _L0_gnn_ref(x, curvature, W_curv, b_curv, W_lin, b_lin, edge_index):
        import jax, jax.numpy as jnp
        import numpy as np
        N = 3125
        E = 50000
        D = 64
        row, col = (edge_index[0], edge_index[1])
        cdiff = jnp.abs(curvature[row] - curvature[col])[:, None]
        gate = jax.nn.sigmoid(cdiff * W_curv[:, 0] + b_curv)
        msg = x[col] * gate
        summed = jax.ops.segment_sum(msg, row, num_segments=N)
        cnt = jax.ops.segment_sum(jnp.ones((msg.shape[0], 1), msg.dtype), row, num_segments=N)
        mean = summed / jnp.maximum(cnt, 1.0)
        out = jax.nn.gelu(mean @ W_lin.T + b_lin, approximate=False)
        return out

    def _L1_gnn_ref(x, edge_index, edge_attr, u, batch, W1, b1, W2, b2):
        import jax, jax.numpy as jnp
        import numpy as np
        N_NODES = 50000
        N_EDGES = 25000
        N_GRAPHS = 128
        D = 64
        n_nodes = x.shape[0]
        src = edge_index[0]
        sums = jax.ops.segment_sum(edge_attr, src, num_segments=n_nodes)
        cnt = jax.ops.segment_sum(jnp.ones((edge_attr.shape[0],), edge_attr.dtype), src, num_segments=n_nodes)
        v_e = sums / jnp.maximum(cnt, 1.0)[:, None]
        comb = jnp.concatenate([x, v_e, u[batch]], axis=1)
        h = jax.nn.relu(comb @ W1 + b1)
        out = jax.nn.relu(h @ W2 + b2)
        return out

    def _L2_gnn_ref(x, edge_index, conv_wl, conv_bl, conv_wr, ln_g, ln_b, adapter_w, adapter_b, mlp_w1, mlp_b1, mlp_ln_g, mlp_ln_b, mlp_w2, mlp_b2):
        import jax, jax.numpy as jnp
        import numpy as np
        N_NODES = 3125
        N_EDGES = 31250
        H = 64
        N_LAYERS = 5
        EPS = 1e-05

        def layer_norm(x, g, b):
            m = jnp.mean(x, axis=-1, keepdims=True)
            v = jnp.var(x, axis=-1, keepdims=True)
            return (x - m) * jax.lax.rsqrt(v + EPS) * g + b

        def sage_conv(x, src, dst, n_nodes, wl, bl, wr):
            xj = x[src]
            deg = jax.ops.segment_sum(jnp.ones((src.shape[0], 1), x.dtype), dst, num_segments=n_nodes)
            amax = jax.ops.segment_max(xj, dst, num_segments=n_nodes)
            amax = jnp.where(deg > 0, amax, jnp.zeros_like(amax))
            amean = jax.ops.segment_sum(xj, dst, num_segments=n_nodes) / jnp.maximum(deg, 1.0)
            agg = jnp.concatenate([amax, amean], axis=-1)
            return agg @ wl.T + bl + x @ wr.T
        src, dst = (edge_index[0], edge_index[1])
        n = x.shape[0]
        x_res = x @ adapter_w.T + adapter_b
        h = sage_conv(x, src, dst, n, conv_wl[0], conv_bl[0], conv_wr[0])
        h = jax.nn.silu(layer_norm(h, ln_g[0], ln_b[0]) + x_res)
        for i in range(1, N_LAYERS):
            h_res = h
            h = sage_conv(h, src, dst, n, conv_wl[i], conv_bl[i], conv_wr[i])
            h = jax.nn.silu(layer_norm(h, ln_g[i], ln_b[i]) + h_res)
        h = jax.nn.silu(h @ mlp_w1.T + mlp_b1)
        h = layer_norm(h, mlp_ln_g, mlp_ln_b)
        return h @ mlp_w2.T + mlp_b2

    def _L3_gnn_ref(x, edge_index, edge_attr, W_edge, b_edge, W1, b1, W2, b2, bn_gamma, bn_beta):
        import jax, jax.numpy as jnp
        import numpy as np
        N_NODES = 3125
        N_EDGES = 1250000
        IN_DIM = 64
        HID_DIM = 64
        EDGE_DIM = 10
        BN_EPS = 1e-05
        src, dst = (edge_index[0], edge_index[1])
        msg = jax.nn.relu(x[src] + edge_attr @ W_edge + b_edge)
        aggr = jax.ops.segment_sum(msg, dst, num_segments=N_NODES)
        h = x + aggr
        h = jax.nn.relu(h @ W1 + b1) @ W2 + b2
        h = jax.nn.relu(h)
        mean = jnp.mean(h, axis=0)
        var = jnp.var(h, axis=0)
        out = (h - mean) * jax.lax.rsqrt(var + BN_EPS) * bn_gamma + bn_beta
        return out
    edge_index = jnp.stack([src, dst])
    batch0 = jnp.zeros((3125,), jnp.int32)
    x = _layernorm(x + _L0_gnn_ref(x, node_vec, L0_gnn_W_curv, L0_gnn_b_curv, L0_gnn_W_lin, L0_gnn_b_lin, edge_index), axis=-1)
    x = _layernorm(x + _L1_gnn_ref(x, edge_index, edge_attr_64, L1_gnn_u, batch0, L1_gnn_W1, L1_gnn_b1, L1_gnn_W2, L1_gnn_b2), axis=-1)
    x = _layernorm(x + _L2_gnn_ref(x, edge_index, L2_gnn_conv_wl, L2_gnn_conv_bl, L2_gnn_conv_wr, L2_gnn_ln_g, L2_gnn_ln_b, L2_gnn_adapter_w, L2_gnn_adapter_b, L2_gnn_mlp_w1, L2_gnn_mlp_b1, L2_gnn_mlp_ln_g, L2_gnn_mlp_ln_b, L2_gnn_mlp_w2, L2_gnn_mlp_b2), axis=-1)
    x = _layernorm(x + _L3_gnn_ref(x, edge_index, edge_attr_10, L3_gnn_W_edge, L3_gnn_b_edge, L3_gnn_W1, L3_gnn_b1, L3_gnn_W2, L3_gnn_b2, L3_gnn_bn_gamma, L3_gnn_bn_beta), axis=-1)
    return x

_drawn_inputs = setup_inputs


def setup_inputs(seed=0):
    import zlib

    import numpy as np

    out = dict(_drawn_inputs(seed))
    spreads = {'L1_gnn_b1': (0.0, 0.1),
     'L1_gnn_b2': (0.0, 0.1),
     'L2_gnn_conv_bl': (0.0, 0.1),
     'L2_gnn_ln_g': (1.0, 0.2),
     'L2_gnn_ln_b': (0.0, 0.1),
     'L2_gnn_adapter_b': (0.0, 0.1),
     'L2_gnn_mlp_b1': (0.0, 0.1),
     'L2_gnn_mlp_ln_g': (1.0, 0.2),
     'L2_gnn_mlp_ln_b': (0.0, 0.1),
     'L2_gnn_mlp_b2': (0.0, 0.1),
     'L3_gnn_b_edge': (0.0, 0.1),
     'L3_gnn_b1': (0.0, 0.8),
     'L3_gnn_b2': (0.0, 0.431),
     'L3_gnn_bn_gamma': (1.0, 0.2),
     'L3_gnn_bn_beta': (0.0, 0.1)}
    factors = {'node_vec': 6.351, 'L0_gnn_W_curv': 2.816, 'L0_gnn_b_curv': 8.0, 'L0_gnn_b_lin': 8.0}
    for name, (base, spread) in spreads.items():
        noise = np.random.default_rng([zlib.crc32(name.encode()), seed]).standard_normal(out[name].shape)
        drawn = base * np.exp(spread * noise) if base else spread * noise
        out[name] = jnp.asarray(drawn.astype(out[name].dtype))
    for name, factor in factors.items():
        out[name] = (out[name] * factor).astype(out[name].dtype)
    return out
```

```python
from contextlib import ExitStack

import concourse.bass as bass
from concourse import mybir

F32 = mybir.dt.float32
BF16 = mybir.dt.bfloat16
I32 = mybir.dt.int32
ALU = mybir.AluOpType
ACT = mybir.ActivationFunctionType
AX = mybir.AxisListType.X

P = 128
D = 64
N = 3125
NB = 125
NA = N // NB
E = 103125
TC = 27
NCH = 30
T = TC * NCH
EP = P * T
W1 = TC + 1
K10 = 10
NT = 9
TROWS = N + 1 + P
GR = 3
NG = TC // GR
LAYERS = 5
EPS = 1e-5
BIG = 3.0e38
ROUND = 12582912.0
TG = 4
NGT = (NA + TG - 1) // TG
assert EP >= E and TC % GR == 0 and TC % NT == 0


def bc(ap, shape):
    return ap.to_broadcast(list(shape))


class Chain:

    def __init__(self, eng, sem, base=0):
        self.eng, self.sem, self.base, self.n = eng, sem, base, 0

    def __call__(self, ins):
        self.n += 1
        ins.then_inc(self.sem, 1)
        self.eng.wait_ge(self.sem, self.base + self.n)


def pieces(total, step):
    return [(i, min(step, total - i)) for i in range(0, total, step)]


class Linear:

    def __init__(self, shared, sources, weights, width, repeats=1):
        self.turned, self.held, self.made, self.added, self.stepped = shared["sems"]
        self.sources, self.weights, self.width = sources, weights, width
        self.nturn = NGT * len(sources)
        self.step = 512 // width if width > P else TG
        self.groups = pieces(NA, self.step)
        self.turn0, self.made0 = shared["count"]
        shared["count"] = (self.turn0 + repeats * self.nturn, self.made0 + repeats * len(self.groups))

    def pe(self, pe, nc, ps_turn, ps_out, held_tiles, ident, L=0):
        i = 0
        for src in self.sources:
            k = src.shape[2]
            for a0, n in pieces(NA, TG):
                if i >= 2:
                    pe.wait_ge(self.held, L * self.nturn + self.turn0 + i - 1)
                    pe.sem_inc(self.stepped, 1)
                for j in range(n):
                    ins = nc.tensor.transpose(ps_turn[0:k, i % 2, j * NB:(j + 1) * NB], src[:, a0 + j, :],
                                              ident[0:NB, 0:NB])
                ins.then_inc(self.turned, 1)
                i += 1
        pe.wait_ge(self.held, L * self.nturn + self.turn0 + self.nturn)
        for i, (a0, n) in enumerate(self.groups):
            if i >= 2:
                pe.wait_ge(self.added, L * len(self.groups) + self.made0 + i - 1)
            for j in range(n):
                for s, (src, w) in enumerate(zip(self.sources, self.weights)):
                    k = src.shape[2]
                    ins = nc.tensor.matmul(ps_out[0:NB, i % 2, j * self.width:(j + 1) * self.width],
                                           held_tiles[s][0:k, (a0 + j) * NB:(a0 + j + 1) * NB], w,
                                           start=(s == 0), stop=(s == len(self.sources) - 1))
            ins.then_inc(self.made, 1)

    def act(self, act, nc, ps_turn, held_tiles, L=0):
        i = 0
        for s, src in enumerate(self.sources):
            k = src.shape[2]
            for a0, n in pieces(NA, TG):
                act.wait_ge(self.turned, L * self.nturn + self.turn0 + i + 1)
                nc.scalar.activation(held_tiles[s][0:k, a0 * NB:(a0 + n) * NB], ps_turn[0:k, i % 2, 0:n * NB],
                                     ACT.Copy).then_inc(self.held, 1)
                i += 1

    def dve(self, dve, nc, ps_out, bias, out, L=0):
        for i, (a0, n) in enumerate(self.groups):
            dve.wait_ge(self.made, L * len(self.groups) + self.made0 + i + 1)
            nc.vector.tensor_tensor(out[:, a0:a0 + n, :],
                                    ps_out[0:NB, i % 2, 0:n * self.width].rearrange("p (a f) -> p a f", f=self.width),
                                    bc(bias[:, 0:self.width].unsqueeze(1), [NB, n, self.width]),
                                    ALU.add).then_inc(self.added, 1)
        dve.wait_ge(self.added, L * len(self.groups) + self.made0 + len(self.groups))


class Norm:

    def __init__(self, shared, stat, repeats=1):
        self.var_ready, self.root_ready = shared["sems"]
        self.start, self.stat = shared["count"], stat
        shared["count"] += repeats

    def dve(self, dve, nc, link, y, scratch, L=0):
        f = y.shape[2]
        mean, var, root, inv = (self.stat[:, i, :] for i in range(4))
        shape = [NB, NA, f]
        link(nc.vector.tensor_reduce(mean, y, AX, ALU.add))
        link(nc.vector.tensor_scalar(mean, mean, 1.0 / f, None, ALU.mult))
        link(nc.vector.tensor_tensor(y, y, bc(mean.unsqueeze(2), shape), ALU.subtract))
        link(nc.vector.tensor_tensor(scratch, y, y, ALU.mult))
        link(nc.vector.tensor_reduce(var, scratch, AX, ALU.add))
        nc.vector.tensor_scalar(var, var, 1.0 / f, EPS, ALU.mult, ALU.add).then_inc(self.var_ready, 1)
        dve.wait_ge(self.root_ready, L + self.start + 1)
        link(nc.vector.reciprocal(inv, root))
        link(nc.vector.tensor_tensor(y, y, bc(inv.unsqueeze(2), shape), ALU.mult))

    def act(self, act, nc, L=0):
        act.wait_ge(self.var_ready, L + self.start + 1)
        nc.scalar.activation(self.stat[:, 2, :], self.stat[:, 1, :], ACT.Sqrt).then_inc(self.root_ready, 1)

    LINKS = 7


class Gathers:

    def __init__(self, sem, name):
        self.gathered = [sem(f"{name}_gathered{k}") for k in range(2)]
        self.index_loaded = [sem(f"{name}_index_loaded{k}") for k in range(2)]
        self.used = [sem(f"{name}_used{k}") for k in range(2)]
        self.sp_done = sem(name + "_sp_done")
        self.stepped = sem(name + "_pool_stepped")

    def load_indices(self, sp, src, index, L):
        with sp.Fori(0, NCH // 2) as g:
            for k in range(2):
                sp.wait_ge(self.used[k], L * (NCH // 2) + g + 1)
                sp.dma_start(index[:, k, :], src[:, bass.ds((g * 2 + k) * TC, TC)]).then_inc(self.index_loaded[k], 16)

    def gather(self, pool, rows, index, got, L):
        with pool.Fori(0, NCH // 2) as g:
            for k in range(2):
                pool.wait_ge(self.index_loaded[k], L * (8 * NCH) + g * 16 + 16)
                pool.wait_ge(self.used[k], L * (NCH // 2) + g + 1)
                pool.sem_inc(self.stepped, 1)
                for i in range(TC):
                    pool.indirect_dma_start(got[:, k, i, :], None, rows,
                                            bass.IndirectOffsetOnAxis(ap=index[:, k, i:i + 1], axis=0)
                                            ).then_inc(self.gathered[k], 16)


class Carry:

    LINKS = 2

    def __init__(self, sem, name, reads):
        self.reads = reads
        self.turned, self.scanned = sem(name + "_tails_turned"), sem(name + "_carry_scanned")
        self.back, self.held = sem(name + "_carry_back"), sem(name + "_carry_held")
        self.brought, self.taken = sem(name + "_carry_brought"), sem(name + "_carry_taken")

    def pe(self, pe, nc, ps_carry, tails, carry_t, carry, carry_from, ident, tails_sem, tails_value, L):
        pe.wait_ge(tails_sem, tails_value)
        nc.tensor.transpose(ps_carry[:, 0, 0:P], tails[:], ident[:]).then_inc(self.turned, 1)
        pe.wait_ge(self.scanned, L * 2 + 2)
        nc.tensor.transpose(ps_carry[:, 1, 0:P], carry_t[:], ident[:]).then_inc(self.back, 1)
        pe.wait_ge(self.held, L + 1)
        for i, (a0, n) in enumerate(pieces(NA, TG)):
            if i >= 2:
                pe.wait_ge(self.taken, L * (self.reads * NGT) + self.reads * (i - 1))
            for j in range(n):
                ins = nc.tensor.matmul(ps_carry[0:NB, i % 2, j * P:(j + 1) * P], carry_from[:, a0 + j, :], carry[:],
                                       start=True, stop=True)
            ins.then_inc(self.brought, 1)

    def dve(self, dve, nc, link, ps_carry, tails_t, carry_t, carry, carry_mask, agg, no_carry, L):
        v = nc.vector
        dve.wait_ge(self.turned, L + 1)
        link(v.tensor_copy(tails_t[:], ps_carry[:, 0, 0:P]))
        v.tensor_tensor_scan(carry_t[0:D, :], carry_mask[0:D, :], tails_t[0:D, :], 0.0, ALU.min,
                             ALU.max).then_inc(self.scanned, 1)
        v.tensor_tensor_scan(carry_t[D:P, :], carry_mask[D:P, :], tails_t[D:P, :], 0.0, ALU.mult,
                             ALU.add).then_inc(self.scanned, 1)
        dve.wait_ge(self.back, L + 1)
        v.tensor_copy(carry[:], ps_carry[:, 1, 0:P]).then_inc(self.held, 1)
        for i, (a0, n) in enumerate(pieces(NA, TG)):
            dve.wait_ge(self.brought, L * NGT + i + 1)
            got = ps_carry[0:NB, i % 2, 0:n * P].rearrange("p (a f) -> p a f", f=P)
            at = slice(a0, a0 + n)
            v.tensor_tensor(agg[:, at, D:P], agg[:, at, D:P], got[:, :, D:P], ALU.add).then_inc(self.taken, 1)
            if no_carry is None:
                continue
            v.tensor_tensor(self.big[:, at, :], got[:, :, 0:D], bc(no_carry[:, at].unsqueeze(2), [NB, n, D]),
                            ALU.add).then_inc(self.taken, 1)
        dve.wait_ge(self.taken, L * (self.reads * NGT) + self.reads * NGT)
        if no_carry is not None:
            link(v.tensor_tensor(agg[:, :, 0:D], agg[:, :, 0:D], self.big[:], ALU.max))


def program(nc, t, out):
    top = ExitStack()

    def sem(name):
        return top.enter_context(nc.semaphore(name))

    def tiles(ctx, stage):
        def sb(name, shape, dt=F32):
            return ctx.enter_context(nc.sbuf_tensor(f"{stage}_{name}", list(shape), dt))

        def ps(name, shape, dt=F32):
            return ctx.enter_context(nc.psum_tensor(f"{stage}_{name}", list(shape), dt))
        return sb, ps

    def nodes(ap):
        return ap.rearrange("(b a) d -> b (a d)", a=NA)

    xc_rows = nc.dram_tensor("xc_rows", [N + 1, D + 1], F32).ap()
    first_rows = nc.dram_tensor("first_rows", [EP + NB, D + 1], F32).ap()
    tables = [nc.dram_tensor(f"table{i}", [TROWS, 2 * D], F32).ap() for i in range(NT)]
    scan_rows = nc.dram_tensor("scan_rows", [EP, 2 * D], F32).ap()
    h_rows = nc.dram_tensor("h_rows", [N + 1, D], F32).ap()

    with top:
        sb, _ = tiles(top, "all")
        sb_top = sb
        ident = sb("ident", [P, P])
        later = sb("later", [P, P])
        earlier = sb("earlier", [P, P])
        lane = sb("lane", [P, 1])
        src_f = sb("src_f", [P, T])
        curv_src = sb("curv_src", [P, T])
        keep = sb("keep", [P, NCH, W1])
        keep_big = sb("keep_big", [P, NCH, W1])
        carry_mask = sb("carry_mask", [P, P])
        carry_from = sb("carry_from", [P, NA, NB])
        no_carry = sb("no_carry", [NB, NA])
        end_row = sb("end_row", [NB, NA], I32)
        has_in = sb("has_in", [NB, NA])
        in_share = sb("in_share", [NB, NA])
        out_share = sb("out_share", [NB, NA])
        h = sb("h", [NB, NA, D])
        stat = sb("stat", [NB, 4, NA])
        products = {"sems": [sem("node_" + n) for n in ("turned", "held", "made", "added", "pe_stepped")], "count": (0, 0)}
        norms = {"sems": [sem("node_" + n) for n in ("var_ready", "root_ready")], "count": 0}

        pool_stepped = sem("pool_stepped")
        table_done = [sem(f"table_done{i}") for i in range(NT)]

        with ExitStack() as ctx:
            sb, ps = tiles(ctx, "prep")
            grid = sb("grid", [P, P], I32)
            count_i = sb("count_i", [P, P], I32)
            lane_i = sb("lane_i", [P, 1], I32)
            count_h = sb("count_h", [P, NB], BF16)
            ident_h = sb("ident_h", [P, P], BF16)
            ends_i = sb("ends_i", [P, 2, T], I32)
            dst_f = sb("dst_f", [P, T])
            hi = sb("hi", [P, 2, T], BF16)
            lo = sb("lo", [P, 2, T], BF16)
            work = sb("work", [P, T])
            work2 = sb("work2", [P, T])
            prev_last = sb("prev_last", [P, 1], I32)
            prev_f = sb("prev_f", [P, 1])
            cont = sb("cont", [P, 1])
            spans = sb("spans", [P, 1])
            curv = sb("curv", [NB, NA])
            curv_part = sb("curv_part", [NB, 3, NA], BF16)
            curv_rest = sb("curv_rest", [NB, NA])
            hot_hi = sb("hot_hi", [P, 2, TC, NB], BF16)
            hot_lo = sb("hot_lo", [P, 2, TC, NA], BF16)
            turned_hot = sb("turned_hot", [NB, 2, GR, P], BF16)
            picked = sb("picked", [P, TC, NA])
            deg = sb("deg", [NB, 2, NA])
            run = sb("run", [NB, 2, NA])
            start_f = sb("start_f", [NB, NA])
            end_f = sb("end_f", [NB, NA])
            nwork = sb("nwork", [NB, 4, NA])
            first_row = sb("first_row", [NB, NA], I32)
            xc = sb("xc", [NB, NA, D + 1])
            x0 = sb("x0", [NB, NA, D])
            zero = sb("zero", [P, TROWS])
            head = sb("head", [P, D + 1])
            zero_h = sb("zero_h", [P, P], BF16)
            ps_deg = ps("ps_deg", [P, 2, 512])
            ps_hot = ps("ps_hot", [P, 2, 1024], BF16)
            ps_pick = ps("ps_pick", [P, 2, 512])
            ps_misc = ps("ps_misc", [P, 2, 512])

            loaded, x_loaded, prev_loaded = sem("loaded"), sem("x_loaded"), sem("prev_loaded")
            iota_done, const_done, zeroed = sem("iota_done"), sem("const_done"), sem("zeroed")
            chain, digits = sem("prep_chain"), sem("digits")
            hot_ready = sem("hot_ready")
            hot_used = sem("hot_used")
            hot_turned, hot_held, looked, pick_used = (sem(n) for n in ("hot_turned", "hot_held", "looked", "pick_used"))
            deg_made, totals, offsets, keys, keyed, key_used = (
                sem(n) for n in ("deg_made", "totals", "offsets", "keys", "keyed", "key_used"))
            first_ready, xc_ready, xc_stored, placed = (sem(n) for n in ("first_ready", "xc_ready", "xc_stored", "placed"))
            zeros_stored, head_got, head_put, cont_made, cont_rows = (
                sem(n) for n in ("zeros_stored", "head_got", "head_put", "cont_made", "cont_rows"))
            FZ = T * (D + 1) // 15
            first_flat = first_rows[0:EP, :].rearrange("(p t) d -> p (t d)", t=T)
            assert FZ <= 2 * TROWS and T * (D + 1) % 30 == 0

            with nc.Block() as block:

                @block.sync
                def _(sp):
                    sp.sem_inc(hot_used, 1)
                    sp.dma_start(ends_i[:, 0, :], t["src_pad"]).then_inc(loaded, 16)
                    sp.dma_start(ends_i[:, 1, :], t["dst_pad"]).then_inc(loaded, 16)
                    sp.dma_start(x0[:].rearrange("b a d -> b (a d)"), nodes(t["x"])).then_inc(x_loaded, 16)
                    sp.dma_start(curv[:], t["node_vec"].rearrange("(b a) -> b a", a=NA)).then_inc(x_loaded, 16)
                    sp.dma_start(h[:].rearrange("b a d -> b (a d)"), nodes(t["x"])).then_inc(x_loaded, 16)
                    sp.wait_ge(const_done, 2)
                    sp.dma_start(prev_last[1:P, :], t["dst_pad"][0:P - 1, T - 1:T],
                                 allow_slow_non_contiguous=True).then_inc(prev_loaded, 16)
                    for i in range(30):
                        sp.dma_start(first_flat[:, i * (FZ // 2):(i + 1) * (FZ // 2)],
                                     zero[:, 0:FZ // 2]).then_inc(zeros_stored, 16)
                    sp.dma_start(h_rows[N:N + 1, :], zero[0:1, 0:D]).then_inc(zeros_stored, 16)
                    sp.dma_start(xc_rows[N:N + 1, :], zero[0:1, 0:D + 1]).then_inc(xc_stored, 16)
                    sp.wait_ge(xc_ready, 2)
                    sp.dma_start(nodes(xc_rows[0:N, :]), xc[:].rearrange("b a d -> b (a d)")).then_inc(xc_stored, 16)
                    sp.wait_ge(head_got, 16)
                    sp.wait_ge(placed, 16 * NA)
                    sp.dma_start(first_rows[0:EP, :].rearrange("(p t) d -> p (t d)", t=T)[:, 0:D + 1],
                                 head[:]).then_inc(head_put, 16)
                    sp.wait_ge(head_put, 16)
                    for i in range(NT):
                        sp.wait_ge(table_done[i], 16)

                @block.gpsimd
                def _(pool):
                    nc.gpsimd.iota(grid[:], [[1, P]], base=0, channel_multiplier=-1).then_inc(iota_done, 1)
                    nc.gpsimd.iota(count_i[:], [[1, P]], base=0, channel_multiplier=0).then_inc(iota_done, 1)
                    nc.gpsimd.iota(lane_i[:], [[1, 1]], base=0, channel_multiplier=1).then_inc(iota_done, 1)
                    nc.gpsimd.memset(prev_last[:], -1).then_inc(const_done, 1)
                    nc.gpsimd.memset(zero[:], 0.0).then_inc(const_done, 1)
                    pool.wait_ge(const_done, 2)
                    for i in range(NT):
                        pool.dma_start(tables[i].rearrange("r d -> (r d)").rearrange("(p k) -> p k", p=P),
                                       zero[:, 0:TROWS]).then_inc(table_done[i], 16)
                    pool.wait_ge(loaded, 32)
                    pool.wait_ge(xc_stored, 32)
                    pool.indirect_dma_start(head[:], None, xc_rows,
                                            bass.IndirectOffsetOnAxis(ap=ends_i[:, 1, 0:1], axis=0)).then_inc(head_got, 16)
                    pool.wait_ge(first_ready, 1)
                    pool.wait_ge(zeros_stored, 16 * 31)
                    for a in range(NA):
                        if a:
                            pool.wait_ge(placed, 16 * a)
                        pool.indirect_dma_start(first_rows, bass.IndirectOffsetOnAxis(ap=first_row[:, a:a + 1], axis=0),
                                                xc[:, a, :], None).then_inc(placed, 16)

                @block.vector
                def _(dve):
                    link = Chain(dve, chain)
                    v = nc.vector
                    dve.wait_ge(iota_done, 3)
                    v.tensor_scalar(ident[:], grid[:], 0.0, None, ALU.is_equal)
                    v.tensor_scalar(ident_h[:], grid[:], 0.0, None, ALU.is_equal)
                    v.tensor_scalar(later[:], grid[:], 0.0, None, ALU.is_gt)
                    v.tensor_scalar(earlier[:], grid[:], 0.0, None, ALU.is_lt)
                    v.tensor_copy(count_h[:], count_i[:, 0:NB])
                    v.tensor_copy(lane[:], lane_i[:])
                    link(v.memset(zero_h[:], 0.0))
                    dve.wait_ge(x_loaded, 48)
                    v.tensor_copy(xc[:, :, 0:D], x0[:]).then_inc(xc_ready, 1)
                    v.tensor_copy(xc[:, :, D], curv[:]).then_inc(xc_ready, 1)
                    link(v.tensor_copy(curv_part[:, 0, :], curv[:]))
                    link(v.tensor_tensor(curv_rest[:], curv[:], curv_part[:, 0, :], ALU.subtract))
                    link(v.tensor_copy(curv_part[:, 1, :], curv_rest[:]))
                    link(v.tensor_tensor(curv_part[:, 2, :], curv_rest[:], curv_part[:, 1, :], ALU.subtract))
                    dve.wait_ge(loaded, 32)
                    for i, full in enumerate((src_f, dst_f)):
                        link(v.tensor_copy(full[:], ends_i[:, i, :]))
                        link(v.tensor_scalar(work[:], full[:], 1.0 / NA, 0.5 / NA - 0.5, ALU.mult, ALU.add))
                        link(v.tensor_scalar(work[:], work[:], ROUND, ROUND, ALU.add, ALU.subtract))
                        link(v.tensor_copy(hi[:, i, :], work[:]))
                        link(v.tensor_scalar(work[:], work[:], -float(NA), None, ALU.mult))
                        link(v.tensor_tensor(lo[:, i, :], work[:], full[:], ALU.add))
                    link(v.memset(work2[:, 0:1], 0.0))
                    link(v.tensor_tensor(work2[:, 1:T], dst_f[:, 1:T], dst_f[:, 0:T - 1], ALU.is_equal))
                    link(v.memset(keep[:, :, 0:1], 0.0))
                    link(v.tensor_copy(keep[:, :, 1:W1], work2[:].rearrange("p (c t) -> p c t", t=TC)))
                    link(v.tensor_scalar(keep_big[:], keep[:], 2.0, -1.0, ALU.mult, ALU.add))
                    link(v.tensor_scalar(keep_big[:], keep_big[:], BIG, None, ALU.mult))
                    dve.wait_ge(prev_loaded, 16)
                    link(v.tensor_copy(prev_f[:], prev_last[:]))
                    link(v.tensor_tensor(cont[:], prev_f[:], dst_f[:, 0:1], ALU.is_equal))
                    link(v.tensor_tensor(spans[:], dst_f[:, 0:1], dst_f[:, T - 1:T], ALU.is_equal))
                    v.tensor_tensor(cont[:], cont[:], spans[:], ALU.mult).then_inc(cont_made, 1)
                    dve.wait_ge(cont_rows, 1)
                    link(v.tensor_copy(carry_mask[:], ps_misc[:, 0, 0:P]))
                    link(v.tensor_scalar(carry_mask[0:D, :], carry_mask[0:D, :], 2.0, -1.0, ALU.mult, ALU.add))
                    link(v.tensor_scalar(carry_mask[0:D, :], carry_mask[0:D, :], BIG, None, ALU.mult))

                    base = link.n
                    with dve.Fori(0, NCH) as c:
                        dve.wait_ge(hot_used, c + 1)
                        for i in range(2):
                            v.tensor_tensor(hot_hi[:, i, :, :], bc(count_h[:].unsqueeze(1), [P, TC, NB]),
                                            bc(hi[:, i, bass.ds(c * TC, TC)].unsqueeze(2), [P, TC, NB]),
                                            ALU.is_equal).then_inc(hot_ready, 1)
                            v.tensor_tensor(hot_lo[:, i, :, :], bc(count_h[:, 0:NA].unsqueeze(1), [P, TC, NA]),
                                            bc(lo[:, i, bass.ds(c * TC, TC)].unsqueeze(2), [P, TC, NA]),
                                            ALU.is_equal).then_inc(hot_ready, 1)
                        dve.wait_ge(hot_ready, c * 4 + 4)
                        for g in range(NG):
                            dve.wait_ge(looked, c * NG + g + 1)
                            v.tensor_tensor(picked[:, g * GR:(g + 1) * GR, :],
                                            ps_pick[:, g % 2, 0:GR * NA].rearrange("p (t a) -> p t a", a=NA),
                                            hot_lo[:, 0, g * GR:(g + 1) * GR, :], ALU.mult).then_inc(pick_used, 1)
                        dve.wait_ge(pick_used, c * NG + NG)
                        v.tensor_reduce(curv_src[:, bass.ds(c * TC, TC)], picked[:], AX, ALU.add).then_inc(chain, 1)
                        dve.wait_ge(chain, c + base + 1)
                    link.n += NCH

                    dve.wait_ge(deg_made, 1)
                    link(v.tensor_copy(deg[:], ps_deg[0:NB, :, 0:NA]))
                    link(v.memset(nwork[:, 3, :], 1.0))
                    link(v.tensor_tensor_scan(run[:, 1, :], nwork[:, 3, :], deg[:, 1, :], 0.0, ALU.mult, ALU.add))
                    v.tensor_copy(nwork[:, 0, 0:1], run[:, 1, NA - 1:NA]).then_inc(totals, 1)
                    dve.wait_ge(offsets, 1)
                    link(v.tensor_tensor(end_f[:], run[:, 1, :], bc(ps_misc[0:NB, 1, 0:1], [NB, NA]), ALU.add))
                    link(v.tensor_tensor(start_f[:], end_f[:], deg[:, 1, :], ALU.subtract))
                    link(v.tensor_scalar(has_in[:], deg[:, 1, :], 1.0, None, ALU.min))
                    link(v.tensor_scalar(nwork[:, 1, :], start_f[:], float(EP), None, ALU.subtract))
                    link(v.tensor_scalar(nwork[:, 1, :], nwork[:, 1, :], lane[0:NB, :], None, ALU.subtract))
                    link(v.tensor_tensor(nwork[:, 1, :], nwork[:, 1, :], has_in[:], ALU.mult))
                    link(v.tensor_scalar(nwork[:, 1, :], nwork[:, 1, :], lane[0:NB, :], float(EP), ALU.add, ALU.add))
                    v.tensor_copy(first_row[:], nwork[:, 1, :]).then_inc(first_ready, 1)
                    for i, share in ((1, in_share), (0, out_share)):
                        link(v.tensor_scalar(nwork[:, 2, :], deg[:, i, :], 1.0, None, ALU.max))
                        link(v.reciprocal(share[:], nwork[:, 2, :]))
                    link(v.tensor_tensor(in_share[:], in_share[:], has_in[:], ALU.mult))
                    link(v.tensor_scalar(end_f[:], end_f[:], 1.0, 0.0, ALU.subtract, ALU.max))
                    link(v.tensor_copy(end_row[:], end_f[:]))
                    link(v.tensor_scalar(nwork[:, 0, :], end_f[:], 1.0 / T, 0.5 / T - 0.5, ALU.mult, ALU.add))
                    link(v.tensor_scalar(nwork[:, 0, :], nwork[:, 0, :], ROUND, ROUND, ALU.add, ALU.subtract))
                    link(v.tensor_scalar(nwork[:, 1, :], nwork[:, 0, :], float(T), None, ALU.mult))
                    link(v.tensor_tensor(nwork[:, 1, :], start_f[:], nwork[:, 1, :], ALU.is_lt))
                    link(v.tensor_tensor(nwork[:, 1, :], nwork[:, 1, :], has_in[:], ALU.mult))
                    link(v.tensor_scalar(no_carry[:], nwork[:, 1, :], 1.0, BIG, ALU.subtract, ALU.mult))
                    link(v.tensor_tensor(nwork[:, 2, :], nwork[:, 0, :], nwork[:, 1, :], ALU.mult))
                    v.tensor_scalar(nwork[:, 2, :], nwork[:, 2, :], 1.0, None, ALU.subtract).then_inc(keys, 1)
                    for i, (a0, n) in enumerate(pieces(NA, TG)):
                        dve.wait_ge(keyed, i + 1)
                        v.tensor_scalar(carry_from[:, a0:a0 + n, :],
                                        ps_misc[:, i % 2, 0:n * NB].rearrange("p (a b) -> p a b", b=NB),
                                        lane[:], None, ALU.is_equal).then_inc(key_used, 1)

                @block.tensor
                def _(pe):
                    pe.wait_ge(chain, 1)
                    for i in range(2):
                        nc.tensor.matmul(ps_deg[0:NB, i, 0:NA], zero_h[:, 0:NB], zero_h[:, 0:NA],
                                         start=True, stop=False, skip_group_check=True)
                    pe.wait_ge(cont_made, 1)
                    nc.tensor.matmul(ps_misc[:, 0, 0:P], bc(cont[:], [P, P]), ident[:],
                                     start=True, stop=True).then_inc(cont_rows, 1)
                    with pe.Fori(0, NCH) as c:
                        pe.wait_ge(hot_ready, c * 4 + 4)
                        for g in range(NG):
                            if g >= 2:
                                pe.wait_ge(hot_held, c * NG + g - 1)
                            for j in range(GR):
                                ins = nc.tensor.transpose(ps_hot[0:NB, g % 2, j * P:(j + 1) * P],
                                                          hot_hi[:, 0, g * GR + j, :], ident_h[:])
                            ins.then_inc(hot_turned, 1)
                            for i in range(2):
                                for j in range(GR):
                                    nc.tensor.matmul(ps_deg[0:NB, i, 0:NA], hot_hi[:, i, g * GR + j, :],
                                                     hot_lo[:, i, g * GR + j, :], start=False, stop=False,
                                                     skip_group_check=True)
                            pe.wait_ge(hot_held, c * NG + g + 1)
                            if g >= 2:
                                pe.wait_ge(pick_used, c * NG + g - 1)
                            for j in range(GR):
                                for s in range(3):
                                    ins = nc.tensor.matmul(ps_pick[:, g % 2, j * NA:(j + 1) * NA],
                                                           turned_hot[:, g % 2, j, :], curv_part[:, s, :],
                                                           start=(s == 0), stop=(s == 2))
                            if g < NG - 1:
                                ins.then_inc(looked, 1)
                        ins.then_inc(looked, 1)
                        pe.wait_ge(looked, c * NG + NG)
                        pe.wait_ge(pick_used, c * NG + NG)
                        pe.sem_inc(hot_used, 1)
                    nc.tensor.matmul(ps_deg[0:NB, 1, 0:NA], zero_h[:, 0:NB], zero_h[:, 0:NA],
                                     start=False, stop=True, skip_group_check=True)
                    nc.tensor.matmul(ps_deg[0:NB, 0, 0:NA], zero_h[:, 0:NB], zero_h[:, 0:NA],
                                     start=False, stop=True, skip_group_check=True).then_inc(deg_made, 1)
                    pe.wait_ge(totals, 1)
                    nc.tensor.matmul(ps_misc[0:NB, 1, 0:1], later[0:NB, 0:NB], nwork[:, 0, 0:1],
                                     start=True, stop=True).then_inc(offsets, 1)
                    pe.wait_ge(keys, 1)
                    for i, (a0, n) in enumerate(pieces(NA, TG)):
                        if i >= 2:
                            pe.wait_ge(key_used, i - 1)
                        for j in range(n):
                            ins = nc.tensor.matmul(ps_misc[:, i % 2, j * NB:(j + 1) * NB],
                                                   bc(nwork[:, 2, a0 + j:a0 + j + 1], [NB, P]), ident[0:NB, 0:NB],
                                                   start=True, stop=True)
                        ins.then_inc(keyed, 1)

                @block.scalar
                def _(act):
                    with act.Fori(0, NCH) as c:
                        for g in range(NG):
                            act.wait_ge(hot_turned, c * NG + g + 1)
                            if g >= 2:
                                act.wait_ge(looked, c * NG + g - 1)
                            nc.scalar.activation(turned_hot[:, g % 2, :, :].rearrange("p t e -> p (t e)"),
                                                 ps_hot[0:NB, g % 2, 0:GR * P], ACT.Copy).then_inc(hot_held, 1)

        with ExitStack() as ctx:
            sb, ps = tiles(ctx, "scatter")
            CF = D + 1
            filled = sb("filled", [P, 2, TC, CF])
            fill_in = sb("fill_in", [P, CF * W1])
            fill_keep = sb("fill_keep", [P, CF * W1], BF16)
            fill_out = sb("fill_out", [P, CF * W1])
            w_curv = sb("w_curv", [P, D])
            b_curv = sb("b_curv", [P, D])
            diff = sb("diff", [P, TC])
            gate = sb("gate", [P, D, TC])
            rows = sb("rows", [P, 2, TC, 2 * D])
            same = sb("same", [P, TC, P])
            before = sb("before", [P, GR, P])
            dup = sb("dup", [P, TC])
            spare = sb("spare", [P, 1])
            to_row = sb("to_row", [P, 2, TC], I32)
            src_now = sb("src_now", [P, TC])
            sums = sb("sums", [P, 2, TC, 2 * D])
            ps_src = ps("ps_src", [P, 2, 512])
            ps_sum = ps("ps_sum", [P, 2, 512])
            in3, keep3, out3 = (a[:].rearrange("p (f t) -> p f t", t=W1) for a in (fill_in, fill_keep, fill_out))

            fill_loaded = [sem(f"fill_loaded{k}") for k in range(2)]
            edge_loaded = [sem(f"edge_loaded{k}") for k in range(2)]
            curv_loaded, fill_turned, fill_masked, fill_scanned = (
                sem(n) for n in ("curv_loaded", "fill_turned", "fill_masked", "fill_scanned"))
            wchain, arg_ready, gate_ready, rows_made = (sem(n) for n in ("wchain", "arg_ready", "gate_ready", "rows_made"))
            src_rows, same_made, summed, sums_held, same_free = (
                sem(n) for n in ("src_rows", "same_made", "summed", "sums_held", "same_free"))
            index_ready, src_copied = sem("index_ready"), sem("src_copied")
            sent = [sem(f"sent{k}") for k in range(2)]

            with nc.Block() as block:

                @block.sync
                def _(sp):
                    sp.dma_start(w_curv[:], bc(t["w_curv"], [P, D])).then_inc(curv_loaded, 16)
                    sp.dma_start(b_curv[:], bc(t["b_curv"], [P, D])).then_inc(curv_loaded, 16)
                    sp.wait_ge(curv_loaded, 32)
                    sp.sem_inc(fill_turned, 2)
                    sp.sem_inc(same_free, 2)
                    first_by_part = first_rows[0:EP, :].rearrange("(p t) d -> p t d", t=T)
                    edge_by_part = t["edge64"].rearrange("(p t) d -> p t d", t=T)
                    with sp.Fori(0, NCH // 2) as g:
                        for k in range(2):
                            sp.wait_ge(fill_turned, g * 2 + (k + 1))
                            sp.dma_start(filled[:, k, :, :], first_by_part[:, bass.ds((g * 2 + k) * TC, TC), :]
                                         ).then_inc(fill_loaded[k], 16)
                            sp.wait_ge(same_free, g * 2 + (k + 1))
                            sp.dma_start(rows[:, k, :, D:2 * D], edge_by_part[:, bass.ds((g * 2 + k) * TC, TC), :]
                                         ).then_inc(edge_loaded[k], 16)

                @block.scalar
                def _(act):
                    with act.Fori(0, NCH // 2) as g:
                        for k in range(2):
                            c = g * 2 + k
                            act.wait_ge(fill_scanned, c + 1)
                            nc.scalar.activation(keep3, bc(keep[:, bass.ds(c, 1), :], [P, CF, W1]),
                                                 ACT.Copy).then_inc(fill_masked, 1)
                            act.wait_ge(same_free, c + 2)
                            nc.scalar.activation(src_now[:], src_f[:, bass.ds(c * TC, TC)],
                                                 ACT.Copy).then_inc(src_copied, 1)
                            act.wait_ge(fill_loaded[k], g * 16 + 16)
                            nc.scalar.activation(in3[:, :, 1:W1], filled[:, k, :, :].rearrange("p t f -> p f t"),
                                                 ACT.Copy).then_inc(fill_turned, 1)
                            act.wait_ge(arg_ready, c + 1)
                            nc.scalar.activation(gate[:], gate[:], ACT.Sigmoid).then_inc(gate_ready, 1)
                            for j in range(NG):
                                act.wait_ge(summed, c * NG + (j + 1))
                                if j == 0:
                                    act.wait_ge(sent[k], g + 1)
                                nc.scalar.activation(
                                    sums[:, k, j * GR:(j + 1) * GR, :].rearrange("p t f -> p (t f)"),
                                    ps_sum[:, j % 2, 0:GR * P], ACT.Copy).then_inc(sums_held, 1)

                @block.vector
                def _(dve):
                    v = nc.vector
                    link = Chain(dve, wchain)
                    dve.wait_ge(curv_loaded, 32)
                    dve.sem_inc(fill_scanned, 1)
                    dve.sem_inc(sent[0], 1)
                    link(v.tensor_scalar(spare[:], lane[:], float(N + 1), None, ALU.add))
                    link(v.memset(fill_out[:], 0.0))
                    base, per = link.n, 2 * NG + 5
                    with dve.Fori(0, NCH // 2) as g:
                        for k in range(2):
                            c = g * 2 + k
                            link = Chain(dve, wchain, c * per + base)
                            dve.wait_ge(same_free, c + 2)
                            for j in range(NG):
                                at = slice(j * GR, (j + 1) * GR)
                                dve.wait_ge(src_rows, c * NG + (j + 1))
                                v.tensor_tensor(same[:, at, :], ps_src[:, j % 2, 0:GR * P].rearrange("p (t e) -> p t e", e=P),
                                                bc(src_f[:, bass.ds(c * TC + j * GR, GR)].unsqueeze(2), [P, GR, P]),
                                                ALU.is_equal).then_inc(same_made, 1)
                                dve.wait_ge(same_made, c * NG + (j + 1))
                                link(v.tensor_tensor(before[:], same[:, at, :], bc(earlier[:].unsqueeze(1), [P, GR, P]),
                                                     ALU.mult))
                                link(v.tensor_reduce(dup[:, at], before[:], AX, ALU.add))
                            link(v.tensor_scalar(dup[:], dup[:], 1.0, None, ALU.min))
                            link(v.scalar_tensor_tensor(out=diff[:], in0=src_f[:, bass.ds(c * TC, TC)], scalar=spare[:, 0:1],
                                                        in1=dup[:], op0=ALU.subtract, op1=ALU.mult))
                            dve.wait_ge(sent[k], g + 1)
                            v.tensor_tensor(to_row[:, k, :], src_f[:, bass.ds(c * TC, TC)], diff[:],
                                            ALU.subtract).then_inc(index_ready, 1)
                            dve.wait_ge(fill_masked, c + 1)
                            dve.wait_ge(fill_turned, c + 3)
                            link(v.tensor_copy(in3[:, :, 0:1], out3[:, :, TC:W1]))
                            v.tensor_tensor_scan(fill_out[:], fill_keep[:], fill_in[:], 0.0, ALU.mult,
                                                 ALU.add).then_inc(fill_scanned, 1)
                            dve.wait_ge(fill_scanned, c + 2)
                            dve.wait_ge(index_ready, c + 1)
                            link(v.tensor_tensor(diff[:], curv_src[:, bass.ds(c * TC, TC)], out3[:, D, 1:W1], ALU.subtract))
                            link(v.scalar_tensor_tensor(out=diff[:], in0=diff[:], scalar=-1.0, in1=diff[:], op0=ALU.mult,
                                                        op1=ALU.max))
                            v.tensor_tensor(gate[:], bc(diff[:].unsqueeze(1), [P, D, TC]),
                                            bc(w_curv[:].unsqueeze(2), [P, D, TC]), ALU.mult).then_inc(rows_made, 1)
                            dve.wait_ge(rows_made, c * 2 + 1)
                            v.tensor_tensor(gate[:], gate[:], bc(b_curv[:].unsqueeze(2), [P, D, TC]),
                                            ALU.add).then_inc(arg_ready, 1)
                            dve.wait_ge(gate_ready, c + 1)
                            v.tensor_tensor(rows[:, k, :, 0:D].rearrange("p t f -> p f t"), gate[:], out3[:, 0:D, 1:W1],
                                            ALU.mult).then_inc(rows_made, 1)
                            dve.wait_ge(rows_made, c * 2 + 2)
                            assert link.n == per, link.n

                @block.tensor
                def _(pe):
                    with pe.Fori(0, NCH // 2) as g:
                        for k in range(2):
                            c = g * 2 + k
                            pe.wait_ge(src_copied, c + 1)
                            for j in range(NG):
                                if j >= 2:
                                    pe.wait_ge(same_made, c * NG + (j - 1))
                                for i in range(GR):
                                    ins = nc.tensor.matmul(
                                        ps_src[:, j % 2, i * P:(i + 1) * P],
                                        bc(src_now[:, j * GR + i:j * GR + i + 1], [P, P]), ident[:], start=True, stop=True)
                                ins.then_inc(src_rows, 1)
                            pe.wait_ge(rows_made, c * 2 + 2)
                            pe.wait_ge(same_made, c * NG + NG)
                            pe.wait_ge(edge_loaded[k], g * 16 + 16)
                            for j in range(NG):
                                if j >= 2:
                                    pe.wait_ge(sums_held, c * NG + (j - 1))
                                for i in range(GR):
                                    ins = nc.tensor.matmul(ps_sum[:, j % 2, i * P:(i + 1) * P],
                                                           same[:, j * GR + i, :], rows[:, k, j * GR + i, :],
                                                           start=True, stop=True)
                                ins.then_inc(summed, 1)
                            pe.wait_ge(sums_held, c * NG + NG)
                            pe.sem_inc(same_free, 1)

                @block.gpsimd
                def _(pool):
                    with pool.Fori(0, NCH // 2) as g:
                        for k in range(2):
                            c = g * 2 + k
                            pool.wait_ge(index_ready, c + 1)
                            for i in range(TC):
                                if i % GR == 0:
                                    pool.wait_ge(sums_held, c * NG + (i // GR + 1))
                                pool.wait_ge(table_done[i % NT], c * (16 * TC // NT) + 16 * (i // NT + 1))
                                pool.sem_inc(pool_stepped, 1)
                                pool.indirect_dma_start(
                                    tables[i % NT], bass.IndirectOffsetOnAxis(ap=to_row[:, k, i:i + 1], axis=0),
                                    sums[:, k, i, :], None, compute_op=ALU.add).then_inc(table_done[i % NT], 16)
                                if i == NT - 1:
                                    pool.sem_inc(sent[1 - k], 1)
                    for i in range(NT):
                        pool.wait_ge(table_done[i], 16 * (1 + NCH * TC // NT))

        res = sb_top("res", [NB, NA, D])
        hl = sb_top("hl", [NB, NA, D])
        with ExitStack() as ctx:
            sb, ps = tiles(ctx, "nodes01")
            acc = sb("acc", [NB, NA, 2 * D])
            part = sb("part", [NB, 2, NA * 2 * D])
            y = sb("y", [NB, NA, D])
            y2 = sb("y2", [NB, NA, D])
            scratch = sb("scratch", [NB, NA, D])
            heldA = sb("heldA", [P, NA * NB])
            heldB = sb("heldB", [P, NA * NB])
            w = {n: sb("w_" + n, [D, D]) for n in ("lin0", "l1x", "l1v", "l1u", "l1o", "adapt")}
            b = {n: sb("b_" + n, [NB, D]) for n in ("lin0", "l1h", "l1o", "adapt")}
            u0 = sb("u0", [D, 1])
            ps_turn = ps("ps_turn", [P, 2, 512])
            ps_out = ps("ps_out", [P, 2, 512])
            ps_u = ps("ps_u", [P, 512])
            wl, tab_added, nchain = (sem(n) for n in ("w01_loaded", "tab_added", "n01_chain"))
            tab_got = [sem(f"tab_got{k}") for k in range(2)]
            ready0, ready1, ready2, ready3, u_made, gelu_in, gelu_out, h_ready, h_put = (
                sem("n01_" + n) for n in ("mean", "x1", "hid", "x2", "u_made", "gelu_in", "gelu_out", "h_ready", "h_put"))
            lin0 = Linear(products, [acc[:, :, 0:D]], [w["lin0"][:]], D)
            lin1 = Linear(products, [h[:], acc[:, :, D:2 * D]], [w["l1x"][:], w["l1v"][:]], D)
            lin2 = Linear(products, [y[:]], [w["l1o"][:]], D)
            adapt = Linear(products, [h[:]], [w["adapt"][:]], D)
            norm0, norm1 = Norm(norms, stat), Norm(norms, stat)
            held = [heldA, heldB]

            with nc.Block() as block:

                @block.sync
                def _(sp):
                    for i in range(NT):
                        if i >= 2:
                            sp.wait_ge(tab_added, i - 1)
                        sp.dma_start(part[:, i % 2, :], nodes(tables[i][0:N, :])).then_inc(tab_got[i % 2], 16)
                        if i == 1:
                            for n in w:
                                sp.dma_start(w[n][:], t["w_" + n]).then_inc(wl, 16)
                            for n in b:
                                sp.dma_start(b[n][:], bc(t["b_" + n], [NB, D])).then_inc(wl, 16)
                            sp.dma_start(u0[:], t["u0"]).then_inc(wl, 16)
                    sp.wait_ge(h_ready, 1)
                    sp.dma_start(nodes(h_rows[0:N, :]), h[:].rearrange("b a d -> b (a d)")).then_inc(h_put, 16)
                    sp.wait_ge(h_put, 16)

                @block.vector
                def _(dve):
                    v = nc.vector
                    link = Chain(dve, nchain)
                    flat = acc[:].rearrange("b a d -> b (a d)")
                    for i in range(NT):
                        dve.wait_ge(tab_got[i % 2], 16 * (i // 2 + 1))
                        if i == 0:
                            v.tensor_copy(flat, part[:, 0, :]).then_inc(tab_added, 1)
                        else:
                            v.tensor_tensor(flat, flat, part[:, i % 2, :], ALU.add).then_inc(tab_added, 1)
                        dve.wait_ge(tab_added, i + 1)
                    v.tensor_tensor(acc[:], acc[:], bc(out_share[:].unsqueeze(2), [NB, NA, 2 * D]),
                                    ALU.mult).then_inc(ready0, 1)
                    dve.wait_ge(wl, 16 * (len(w) + len(b) + 1))
                    lin0.dve(dve, nc, ps_out, b["lin0"], y)
                    dve.sem_inc(gelu_in, 1)
                    dve.wait_ge(gelu_out, 1)
                    link(v.tensor_tensor(h[:], h[:], y2[:], ALU.add))
                    norm0.dve(dve, nc, link, h[:], scratch[:])
                    dve.sem_inc(ready1, 1)
                    dve.wait_ge(u_made, 1)
                    link(v.tensor_tensor(b["l1h"][:], b["l1h"][:], ps_u[0:NB, 0:D], ALU.add))
                    lin1.dve(dve, nc, ps_out, b["l1h"], y)
                    v.tensor_scalar(y[:], y[:], 0.0, None, ALU.max).then_inc(ready2, 1)
                    lin2.dve(dve, nc, ps_out, b["l1o"], y2)
                    link(v.tensor_scalar(y2[:], y2[:], 0.0, None, ALU.max))
                    link(v.tensor_tensor(h[:], h[:], y2[:], ALU.add))
                    norm1.dve(dve, nc, link, h[:], scratch[:])
                    dve.sem_inc(h_ready, 1)
                    dve.sem_inc(ready3, 1)
                    link(v.tensor_copy(hl[:], h[:]))
                    adapt.dve(dve, nc, ps_out, b["adapt"], res)

                @block.scalar
                def _(act):
                    lin0.act(act, nc, ps_turn, held)
                    act.wait_ge(gelu_in, 1)
                    nc.scalar.activation(y2[:], y[:], ACT.Gelu).then_inc(gelu_out, 1)
                    norm0.act(act, nc)
                    lin1.act(act, nc, ps_turn, held)
                    lin2.act(act, nc, ps_turn, held)
                    norm1.act(act, nc)
                    adapt.act(act, nc, ps_turn, held)

                @block.tensor
                def _(pe):
                    pe.wait_ge(wl, 16 * (len(w) + len(b) + 1))
                    nc.tensor.matmul(ps_u[0:NB, 0:D], bc(u0[:], [D, NB]), w["l1u"][:], start=True,
                                     stop=True).then_inc(u_made, 1)
                    pe.wait_ge(ready0, 1)
                    lin0.pe(pe, nc, ps_turn, ps_out, held, ident)
                    pe.wait_ge(ready1, 1)
                    lin1.pe(pe, nc, ps_turn, ps_out, held, ident)
                    pe.wait_ge(ready2, 1)
                    lin2.pe(pe, nc, ps_turn, ps_out, held, ident)
                    pe.wait_ge(ready3, 1)
                    adapt.pe(pe, nc, ps_turn, ps_out, held, ident)

        with ExitStack() as ctx:
            sb, ps = tiles(ctx, "sage")
            agg = sb("agg", [NB, NA, 2 * D])
            run_max = sb("run_max", [P, D * W1])
            run_sum = sb("run_sum", [P, D * W1])
            w_agg = sb("w_agg", [2 * D, D])
            w_self = sb("w_self", [D, D])
            vecs = sb("vecs", [NB, 3, D])
            tails = sb("tails", [P, P])
            tails_t = sb("tails_t", [P, P])
            carry_t = sb("carry_t", [P, P])
            carry = sb("carry", [P, P])
            max3, sum3 = (a[:].rearrange("p (f t) -> p f t", t=W1) for a in (run_max, run_sum))
            pass2 = Gathers(sem, "sage")
            names = ("layer_loaded", "sage_masks", "sage_scanned", "sage_rows", "sage_stored", "sage_chain", "ends_got",
                     "node_chain", "agg_ready", "silu_in", "silu_out", "h_put2", "sage_zeroed")
            (layer_loaded, masks, scanned, rows_ready, rows_stored, schain, ends_got, nodechain, agg_ready, silu_in,
             silu_out, h_put2, sage_zeroed) = (sem(n) for n in names)
            fix = Carry(sem, "sage", 2)
            conv = Linear(products, [agg[:], hl[:]], [w_agg[:], w_self[:]], D, LAYERS)
            norm = Norm(norms, stat, LAYERS)

            with nc.Block() as block:

                @block.vector
                def _(dve):
                    nc.vector.memset(run_max[:], 0.0).then_inc(sage_zeroed, 1)
                    nc.vector.memset(run_sum[:], 0.0).then_inc(sage_zeroed, 1)
                    dve.wait_ge(sage_zeroed, 2)

                @block.sync
                def _(sp):
                    for k in range(2):
                        sp.sem_inc(pass2.used[k], 1)

            with nc.Fori(0, LAYERS) as L:
                with ExitStack() as ctx2:
                    sb, ps = tiles(ctx2, "sage_edges")
                    index = sb("index", [P, 2, TC], I32)
                    got = sb("got", [P, 2, TC, D])
                    turned = sb("turned", [P, D * W1])
                    mask_max = sb("mask_max", [P, D * W1], BF16)
                    mask_sum = sb("mask_sum", [P, D * W1], BF16)
                    both = sb("both", [P, TC, 2 * D])
                    in3, mm3, ms3 = (a[:].rearrange("p (f t) -> p f t", t=W1) for a in (turned, mask_max, mask_sum))
                    rows_by_part = scan_rows.rearrange("(p t) d -> p t d", t=T)

                    with nc.Block() as block:

                        @block.sync
                        def _(sp):
                            sp.dma_start(w_agg[:], t["w_agg"][bass.ds(L * (2 * D), 2 * D), :]).then_inc(layer_loaded, 16)
                            sp.dma_start(w_self[:], t["w_self"][bass.ds(L * D, D), :]).then_inc(layer_loaded, 16)
                            sp.dma_start(vecs[:], bc(t["conv_vecs"][bass.ds(L, 1), :, :], [NB, 3, D])).then_inc(layer_loaded, 16)
                            pass2.load_indices(sp, t["src_pad"], index, L)
                            sp.wait_ge(layer_loaded, L * 48 + 48)
                            sp.sem_inc(pass2.sp_done, 1)

                        @block.gpsimd
                        def _(pool):
                            pass2.gather(pool, h_rows, index, got, L)
                            pool.wait_ge(rows_stored, L * (16 * NCH) + 16 * NCH)
                            pool.sem_inc(pool_stepped, 1)
                            for a in range(NA):
                                pool.indirect_dma_start(agg[:, a, :], None, scan_rows,
                                                        bass.IndirectOffsetOnAxis(ap=end_row[:, a:a + 1], axis=0)
                                                        ).then_inc(ends_got, 16)
                            pool.wait_ge(ends_got, L * (16 * NA) + 16 * NA)
                            pool.sem_inc(pass2.sp_done, 1)

                        @block.scalar
                        def _(act):
                            with act.Fori(0, NCH // 2) as g:
                                for k in range(2):
                                    c = L * NCH + g * 2 + k
                                    nc.scalar.activation(mm3, bc(keep_big[:, bass.ds(g * 2 + k, 1), :], [P, D, W1]),
                                                         ACT.Copy).then_inc(masks, 1)
                                    nc.scalar.activation(ms3, bc(keep[:, bass.ds(g * 2 + k, 1), :], [P, D, W1]),
                                                         ACT.Copy).then_inc(masks, 1)
                                    act.wait_ge(pass2.gathered[k], L * (16 * TC * NCH // 2) + g * (16 * TC) + 16 * TC)
                                    nc.scalar.activation(in3[:, :, 1:W1], got[:, k, :, :].rearrange("p t f -> p f t"),
                                                         ACT.Copy).then_inc(pass2.used[k], 1)
                                    act.wait_ge(scanned, c * 2 + 2)
                                    nc.scalar.activation(both[:, :, 0:D].rearrange("p t f -> p f t"), max3[:, :, 1:W1],
                                                         ACT.Copy).then_inc(rows_ready, 1)
                                    nc.scalar.activation(both[:, :, D:2 * D].rearrange("p t f -> p f t"), sum3[:, :, 1:W1],
                                                         ACT.Copy).then_inc(rows_ready, 1)
                                    act.wait_ge(rows_ready, c * 2 + 2)
                                    act.dma_start(rows_by_part[:, bass.ds((g * 2 + k) * TC, TC), :], both[:]
                                                  ).then_inc(rows_stored, 16)
                                    act.wait_ge(rows_stored, c * 16 + 16)

                        @block.vector
                        def _(dve):
                            v = nc.vector
                            with dve.Fori(0, NCH // 2) as g:
                                for k in range(2):
                                    c = L * NCH + g * 2 + k
                                    link = Chain(dve, schain, c * 2)
                                    dve.wait_ge(masks, c * 2 + 2)
                                    dve.wait_ge(pass2.used[k], L * (NCH // 2) + g + 2)
                                    link(v.tensor_copy(in3[:, :, 0:1], max3[:, :, TC:W1]))
                                    v.tensor_tensor_scan(run_max[:], mask_max[:], turned[:], 0.0, ALU.min,
                                                         ALU.max).then_inc(scanned, 1)
                                    dve.wait_ge(scanned, c * 2 + 1)
                                    link(v.tensor_copy(in3[:, :, 0:1], sum3[:, :, TC:W1]))
                                    v.tensor_tensor_scan(run_sum[:], mask_sum[:], turned[:], 0.0, ALU.mult,
                                                         ALU.add).then_inc(scanned, 1)

                with ExitStack() as ctx2:
                    sb, ps = tiles(ctx2, "sage_nodes")
                    y = sb("y", [NB, NA, D])
                    fix.big = y
                    scratch = sb("scratch", [NB, NA, D])
                    heldA = sb("heldA", [P, NA * NB])
                    heldB = sb("heldB", [P, NA * NB])
                    held = [heldA, heldB]
                    ps_turn = ps("ps_turn", [P, 2, 512])
                    ps_out = ps("ps_out", [P, 2, 512])
                    ps_carry = ps("ps_carry", [P, 2, 512])
                    with nc.Block() as block:

                        @block.sync
                        def _(sp):
                            sp.wait_ge(silu_out, L * 2 + 2)
                            sp.dma_start(nodes(h_rows[0:N, :]), hl[:].rearrange("b a d -> b (a d)")).then_inc(h_put2, 16)
                            sp.wait_ge(h_put2, L * 16 + 16)
                            sp.sem_inc(pass2.sp_done, 1)

                        @block.vector
                        def _(dve):
                            v = nc.vector
                            per = 2 + Carry.LINKS + Norm.LINKS + 3
                            link = Chain(dve, nodechain, L * per)
                            dve.wait_ge(ends_got, L * (16 * NA) + 16 * NA)
                            link(v.tensor_copy(tails[:, 0:D].unsqueeze(2), max3[:, :, TC:W1]))
                            link(v.tensor_copy(tails[:, D:2 * D].unsqueeze(2), sum3[:, :, TC:W1]))
                            fix.dve(dve, nc, link, ps_carry, tails_t, carry_t, carry, carry_mask, agg, no_carry, L)
                            v.tensor_tensor(agg[:, :, 0:D], agg[:, :, 0:D], bc(has_in[:].unsqueeze(2), [NB, NA, D]),
                                            ALU.mult).then_inc(agg_ready, 1)
                            v.tensor_tensor(agg[:, :, D:2 * D], agg[:, :, D:2 * D],
                                            bc(in_share[:].unsqueeze(2), [NB, NA, D]), ALU.mult).then_inc(agg_ready, 1)
                            conv.dve(dve, nc, ps_out, vecs[:, 0, :], y, L)
                            norm.dve(dve, nc, link, y[:], scratch[:], L)
                            link(v.tensor_tensor(y[:], y[:], bc(vecs[:, 1, :].unsqueeze(1), [NB, NA, D]), ALU.mult))
                            link(v.tensor_tensor(y[:], y[:], bc(vecs[:, 2, :].unsqueeze(1), [NB, NA, D]), ALU.add))
                            link(v.tensor_tensor(y[:], y[:], res[:], ALU.add))
                            dve.sem_inc(silu_in, 1)
                            assert link.n == per, (link.n, per)

                        @block.scalar
                        def _(act):
                            conv.act(act, nc, ps_turn, held, L)
                            norm.act(act, nc, L)
                            act.wait_ge(silu_in, L + 1)
                            nc.scalar.activation(hl[:], y[:], ACT.Silu).then_inc(silu_out, 1)
                            nc.scalar.activation(res[:], y[:], ACT.Silu).then_inc(silu_out, 1)

                        @block.tensor
                        def _(pe):
                            fix.pe(pe, nc, ps_carry, tails, carry_t, carry, carry_from, ident, nodechain,
                                   L * (2 + Carry.LINKS + Norm.LINKS + 3) + 2, L)
                            pe.wait_ge(agg_ready, L * 2 + 2)
                            conv.pe(pe, nc, ps_turn, ps_out, held, ident, L)

        HID = 4 * D
        with ExitStack() as ctx:
            sb, ps = tiles(ctx, "mlp")
            z = sb("z", [NB, NA, HID])
            scratch = sb("scratch", [NB, NA, HID])
            y = sb("y", [NB, NA, D])
            heldA = sb("heldA", [P, NA * NB])
            heldB = sb("heldB", [P, NA * NB])
            w_in = sb("w_in", [D, HID])
            w_out = sb("w_out", [P, 2, D])
            b_in = sb("b_in", [NB, 3, HID])
            b_out = sb("b_out", [NB, D])
            ps_turn = ps("ps_turn", [P, 2, 512])
            ps_out = ps("ps_out", [P, 2, 512])
            held = [heldA, heldB]
            mlp_loaded, mchain, msilu_in, msilu_out, z_ready, x3_ready, x3_put = (
                sem("mlp_" + n) for n in ("loaded", "chain", "silu_in", "silu_out", "z_ready", "x3_ready", "x3_put"))
            mlp1 = Linear(products, [hl[:]], [w_in[:]], HID)
            mlp2 = Linear(products, [z[:, :, 0:P], z[:, :, P:HID]], [w_out[:, 0, :], w_out[:, 1, :]], D)
            norm_h, norm2 = Norm(norms, stat), Norm(norms, stat)
            with nc.Block() as block:

                @block.sync
                def _(sp):
                    sp.dma_start(w_in[:], t["w_mlp1"]).then_inc(mlp_loaded, 16)
                    sp.dma_start(w_out[:], t["w_mlp2"].rearrange("(s k) f -> k s f", s=2)).then_inc(mlp_loaded, 16)
                    sp.dma_start(b_in[:], bc(t["mlp_vecs"].unsqueeze(0), [NB, 3, HID])).then_inc(mlp_loaded, 16)
                    sp.dma_start(b_out[:], bc(t["b_mlp2"], [NB, D])).then_inc(mlp_loaded, 16)
                    sp.wait_ge(x3_ready, 1)
                    sp.dma_start(nodes(h_rows[0:N, :]), h[:].rearrange("b a d -> b (a d)")).then_inc(x3_put, 16)
                    sp.wait_ge(x3_put, 16)

                @block.vector
                def _(dve):
                    v = nc.vector
                    link = Chain(dve, mchain)
                    dve.wait_ge(mlp_loaded, 64)
                    mlp1.dve(dve, nc, ps_out, b_in[:, 0, :], z)
                    dve.sem_inc(msilu_in, 1)
                    dve.wait_ge(msilu_out, 1)
                    norm_h.dve(dve, nc, link, z[:], scratch[:])
                    link(v.tensor_tensor(z[:], z[:], bc(b_in[:, 1, :].unsqueeze(1), [NB, NA, HID]), ALU.mult))
                    v.tensor_tensor(z[:], z[:], bc(b_in[:, 2, :].unsqueeze(1), [NB, NA, HID]), ALU.add).then_inc(z_ready, 1)
                    mlp2.dve(dve, nc, ps_out, b_out, y)
                    link(v.tensor_tensor(h[:], h[:], y[:], ALU.add))
                    norm2.dve(dve, nc, link, h[:], scratch[:, :, 0:D])
                    dve.sem_inc(x3_ready, 1)

                @block.scalar
                def _(act):
                    mlp1.act(act, nc, ps_turn, held)
                    act.wait_ge(msilu_in, 1)
                    nc.scalar.activation(z[:], z[:], ACT.Silu).then_inc(msilu_out, 1)
                    norm_h.act(act, nc)
                    mlp2.act(act, nc, ps_turn, held)
                    norm2.act(act, nc)

                @block.tensor
                def _(pe):
                    pe.wait_ge(mlp_loaded, 64)
                    mlp1.pe(pe, nc, ps_turn, ps_out, held, ident)
                    pe.wait_ge(z_ready, 1)
                    mlp2.pe(pe, nc, ps_turn, ps_out, held, ident)

        with ExitStack() as ctx:
            sb, ps = tiles(ctx, "last")
            agg = sb("agg", [NB, NA, 2 * D])
            run_sum = sb("run_sum", [P, D * W1])
            sum3 = run_sum[:].rearrange("p (f t) -> p f t", t=W1)
            pass3 = Gathers(sem, "edge")
            (e_zeroed, e_masks, e_scanned, e_rows, e_stored, e_chain, e_ends, e_w, e_made, e_turned) = (
                sem("edge_" + n) for n in ("zeroed", "masks", "scanned", "rows", "stored", "chain", "ends", "w",
                                           "made", "turned"))
            e_loaded = [sem(f"edge_loaded_k{k}") for k in range(2)]
            sum_rows = nc.dram_tensor("sum_rows", [EP, D], F32).ap()
            with ExitStack() as ctx2:
                sb, ps = tiles(ctx2, "last_edges")
                index = sb("index", [P, 2, TC], I32)
                got = sb("got", [P, 2, TC, D])
                msg = sb("msg", [P, TC, D])
                turned = sb("turned", [P, D * W1])
                mask_sum = sb("mask_sum", [P, D * W1], BF16)
                both = sb("both", [P, TC, D])
                attr = sb("attr", [K10 + 1, 2, TC, P])
                w_edge = sb("w_edge", [K10 + 1, D])
                ps_edge = ps("ps_edge", [P, 4, 512])
                in3, ms3 = (a[:].rearrange("p (f t) -> p f t", t=W1) for a in (turned, mask_sum))
                ps_flat = ps_edge[:].rearrange("p b x -> p (b x)")[:, 0:TC * D].rearrange("p (t f) -> p t f", f=D)
                rows_by_part = sum_rows.rearrange("(p t) d -> p t d", t=T)

                with nc.Block() as block:

                    @block.sync
                    def _(sp):
                        for k in range(2):
                            sp.sem_inc(pass3.used[k], 1)
                        sp.sem_inc(e_made, 2)
                        sp.wait_ge(e_zeroed, 2)
                        sp.dma_start(w_edge[:], t["w_edge"]).then_inc(e_w, 16)
                        with sp.Fori(0, NCH // 2) as g:
                            for k in range(2):
                                sp.wait_ge(pass3.used[k], g + 1)
                                sp.dma_start(index[:, k, :], t["src_pad"][:, bass.ds((g * 2 + k) * TC, TC)]
                                             ).then_inc(pass3.index_loaded[k], 16)
                                sp.wait_ge(e_made, g * 2 + (k + 1))
                                sp.dma_start(attr[0:K10, k, :, :], t["edge10"][:, bass.ds((g * 2 + k) * TC, TC), :]
                                             ).then_inc(e_loaded[k], 16)

                    @block.gpsimd
                    def _(pool):
                        pass3.gather(pool, h_rows, index, got, 0)
                        pool.wait_ge(e_stored, 16 * NCH)
                        for a in range(NA):
                            pool.indirect_dma_start(agg[:, a, D:2 * D], None, sum_rows,
                                                    bass.IndirectOffsetOnAxis(ap=end_row[:, a:a + 1], axis=0)
                                                    ).then_inc(e_ends, 16)
                        pool.wait_ge(e_ends, 16 * NA)

                    @block.scalar
                    def _(act):
                        with act.Fori(0, NCH // 2) as g:
                            for k in range(2):
                                c = g * 2 + k
                                nc.scalar.activation(ms3, bc(keep[:, bass.ds(c, 1), :], [P, D, W1]),
                                                     ACT.Copy).then_inc(e_masks, 1)
                                act.wait_ge(pass3.used[k], g + 2)
                                nc.scalar.activation(in3[:, :, 1:W1], msg[:].rearrange("p t f -> p f t"),
                                                     ACT.Relu).then_inc(e_turned, 1)
                                act.wait_ge(e_scanned, c + 1)
                                nc.scalar.activation(both[:].rearrange("p t f -> p f t"), sum3[:, :, 1:W1],
                                                     ACT.Copy).then_inc(e_rows, 1)
                                act.wait_ge(e_rows, c + 1)
                                act.dma_start(rows_by_part[:, bass.ds(c * TC, TC), :], both[:]).then_inc(e_stored, 16)
                                act.wait_ge(e_stored, c * 16 + 16)

                    @block.vector
                    def _(dve):
                        v = nc.vector
                        v.memset(attr[:], 1.0).then_inc(e_zeroed, 1)
                        v.memset(run_sum[:], 0.0).then_inc(e_zeroed, 1)
                        dve.wait_ge(e_zeroed, 2)
                        with dve.Fori(0, NCH // 2) as g:
                            for k in range(2):
                                c = g * 2 + k
                                link = Chain(dve, e_chain, c)
                                dve.wait_ge(pass3.gathered[k], g * (16 * TC) + 16 * TC)
                                dve.wait_ge(e_made, c + 3)
                                v.tensor_tensor(msg[:], got[:, k, :, :], ps_flat, ALU.add).then_inc(pass3.used[k], 1)
                                dve.wait_ge(e_masks, c + 1)
                                dve.wait_ge(e_turned, c + 1)
                                link(v.tensor_copy(in3[:, :, 0:1], sum3[:, :, TC:W1]))
                                v.tensor_tensor_scan(run_sum[:], mask_sum[:], turned[:], 0.0, ALU.mult,
                                                     ALU.add).then_inc(e_scanned, 1)
                                dve.wait_ge(e_scanned, c + 1)

                    @block.tensor
                    def _(pe):
                        pe.wait_ge(e_w, 16)
                        with pe.Fori(0, NCH // 2) as g:
                            for k in range(2):
                                c = g * 2 + k
                                pe.wait_ge(e_loaded[k], g * 16 + 16)
                                pe.wait_ge(pass3.used[1 - k], g + (1 + k))
                                for j in range(TC):
                                    ins = nc.tensor.matmul(ps_edge[:, j // 8, (j % 8) * D:(j % 8 + 1) * D],
                                                           attr[:, k, j, :], w_edge[:], start=True, stop=True)
                                ins.then_inc(e_made, 1)

            with ExitStack() as ctx2:
                sb, ps = tiles(ctx2, "last_nodes")
                y = sb("y", [NB, NA, D])
                y2 = sb("y2", [NB, NA, D])
                scratch = sb("scratch", [NB, NA, D])
                heldA = sb("heldA", [P, NA * NB])
                tails = sb("tails", [P, P])
                tails_t = sb("tails_t", [P, P])
                carry_t = sb("carry_t", [P, P])
                carry = sb("carry", [P, P])
                w1 = sb("w1", [D, D])
                w2 = sb("w2", [D, D])
                vec = sb("vec", [NB, 4, D])
                ones = sb("ones", [NB, NB])
                bn = sb("bn", [NB, 4, D])
                ps_turn = ps("ps_turn", [P, 2, 512])
                ps_out = ps("ps_out", [P, 2, 512])
                ps_carry = ps("ps_carry", [P, 2, 512])
                ps_bn = ps("ps_bn", [P, 2, 512])
                held = [heldA]
                (f_loaded, fchain, f_in, f_hid, f_out, f_sum, f_sq, f_root, f_root_out, f_done, f_put) = (
                    sem("last_" + n) for n in ("loaded", "chain", "in", "hid", "out", "sum", "sq", "root", "root_out",
                                               "done", "put"))
                fix = Carry(sem, "edge", 1)
                l1 = Linear(products, [y2[:]], [w1[:]], D)
                l2 = Linear(products, [y[:]], [w2[:]], D)
                norm3 = Norm(norms, stat)
                with nc.Block() as block:

                    @block.sync
                    def _(sp):
                        sp.dma_start(w1[:], t["w_last1"]).then_inc(f_loaded, 16)
                        sp.dma_start(w2[:], t["w_last2"]).then_inc(f_loaded, 16)
                        sp.dma_start(vec[:], bc(t["last_vecs"].unsqueeze(0), [NB, 4, D])).then_inc(f_loaded, 16)
                        sp.wait_ge(f_done, 1)
                        sp.dma_start(nodes(out), h[:].rearrange("b a d -> b (a d)")).then_inc(f_put, 16)
                        sp.wait_ge(f_put, 16)

                    @block.vector
                    def _(dve):
                        v = nc.vector
                        link = Chain(dve, fchain)
                        link(v.memset(tails[:, 0:D], 0.0))
                        link(v.tensor_copy(tails[:, D:2 * D].unsqueeze(2), sum3[:, :, TC:W1]))
                        fix.dve(dve, nc, link, ps_carry, tails_t, carry_t, carry, carry_mask, agg, None, 0)
                        link(v.tensor_tensor(y2[:], agg[:, :, D:2 * D], bc(has_in[:].unsqueeze(2), [NB, NA, D]), ALU.mult))
                        v.tensor_tensor(y2[:], y2[:], h[:], ALU.add).then_inc(f_in, 1)
                        dve.wait_ge(f_loaded, 48)
                        l1.dve(dve, nc, ps_out, vec[:, 0, :], y)
                        v.tensor_scalar(y[:], y[:], 0.0, None, ALU.max).then_inc(f_hid, 1)
                        l2.dve(dve, nc, ps_out, vec[:, 1, :], y2)
                        link(v.memset(ones[:], 1.0))
                        v.tensor_scalar(y2[:], y2[:], 0.0, None, ALU.max).then_inc(f_out, 1)
                        dve.wait_ge(f_sum, 1)
                        link(v.tensor_scalar(bn[:, 0, :], ps_bn[0:NB, 0, 0:D], 1.0 / N, None, ALU.mult))
                        link(v.tensor_tensor(y2[:], y2[:], bc(bn[:, 0, :].unsqueeze(1), [NB, NA, D]), ALU.subtract))
                        v.tensor_tensor(scratch[:], y2[:], y2[:], ALU.mult).then_inc(f_out, 1)
                        dve.wait_ge(f_sum, 2)
                        v.tensor_scalar(bn[:, 1, :], ps_bn[0:NB, 1, 0:D], 1.0 / N, EPS, ALU.mult, ALU.add).then_inc(f_root, 1)
                        dve.wait_ge(f_root_out, 1)
                        link(v.reciprocal(bn[:, 3, :], bn[:, 2, :]))
                        link(v.tensor_tensor(bn[:, 3, :], bn[:, 3, :], vec[:, 2, :], ALU.mult))
                        link(v.tensor_tensor(y2[:], y2[:], bc(bn[:, 3, :].unsqueeze(1), [NB, NA, D]), ALU.mult))
                        link(v.tensor_tensor(y2[:], y2[:], bc(vec[:, 3, :].unsqueeze(1), [NB, NA, D]), ALU.add))
                        link(v.tensor_tensor(h[:], h[:], y2[:], ALU.add))
                        norm3.dve(dve, nc, link, h[:], scratch[:])
                        dve.sem_inc(f_done, 1)

                    @block.scalar
                    def _(act):
                        l1.act(act, nc, ps_turn, held)
                        l2.act(act, nc, ps_turn, held)
                        act.wait_ge(f_root, 1)
                        nc.scalar.activation(bn[:, 2, :], bn[:, 1, :], ACT.Sqrt).then_inc(f_root_out, 1)
                        norm3.act(act, nc)

                    @block.tensor
                    def _(pe):
                        fix.pe(pe, nc, ps_carry, tails, carry_t, carry, carry_from, ident, fchain, 2, 0)
                        pe.wait_ge(f_loaded, 48)
                        pe.wait_ge(f_in, 1)
                        l1.pe(pe, nc, ps_turn, ps_out, held, ident)
                        pe.wait_ge(f_hid, 1)
                        l2.pe(pe, nc, ps_turn, ps_out, held, ident)
                        for i, tile in enumerate((y2, scratch)):
                            pe.wait_ge(f_out, i + 1)
                            for a in range(NA):
                                ins = nc.tensor.matmul(ps_bn[0:NB, i, 0:D], ones[:], tile[:, a, :], start=(a == 0),
                                                       stop=(a == NA - 1))
                            ins.then_inc(f_sum, 1)


def kernel(**inputs):
    import numpy as np
    import concourse.bacc as bacc
    from concourse.bass_utils import run_bass_kernel_spmd

    a = {k: np.asarray(v) for k, v in inputs.items()}

    def lay(ap):
        return np.ascontiguousarray(ap)

    def edges(v, fill):
        padded = np.full((EP,) + v.shape[1:], fill, v.dtype)
        padded[:E] = v
        return padded

    attr = edges(a["edge_attr_10"], 0)
    w1 = a["L1_gnn_W1"]
    arrays = {
        "x": a["x"], "node_vec": a["node_vec"],
        "src_pad": edges(a["src"], N).reshape(P, T), "dst_pad": edges(a["dst"], N).reshape(P, T),
        "edge64": edges(a["edge_attr_64"], 0), "edge10": attr.reshape(P, T, K10).transpose(2, 1, 0),
        "w_curv": a["L0_gnn_W_curv"].reshape(1, D), "b_curv": a["L0_gnn_b_curv"].reshape(1, D),
        "w_lin0": a["L0_gnn_W_lin"].T, "b_lin0": a["L0_gnn_b_lin"].reshape(1, D),
        "w_l1x": w1[0:D], "w_l1v": w1[D:2 * D], "w_l1u": w1[2 * D:3 * D], "b_l1h": a["L1_gnn_b1"].reshape(1, D),
        "w_l1o": a["L1_gnn_W2"], "b_l1o": a["L1_gnn_b2"].reshape(1, D), "u0": a["L1_gnn_u"][0].reshape(D, 1),
        "w_adapt": a["L2_gnn_adapter_w"].T, "b_adapt": a["L2_gnn_adapter_b"].reshape(1, D),
        "w_agg": a["L2_gnn_conv_wl"].transpose(0, 2, 1).reshape(-1, D), "w_self": a["L2_gnn_conv_wr"].transpose(0, 2, 1).reshape(-1, D),
        "conv_vecs": np.stack([a["L2_gnn_conv_bl"], a["L2_gnn_ln_g"], a["L2_gnn_ln_b"]], 1),
        "w_mlp1": a["L2_gnn_mlp_w1"].T, "w_mlp2": a["L2_gnn_mlp_w2"].T, "b_mlp2": a["L2_gnn_mlp_b2"].reshape(1, D),
        "mlp_vecs": np.stack([a["L2_gnn_mlp_b1"], a["L2_gnn_mlp_ln_g"], a["L2_gnn_mlp_ln_b"]]),
        "w_edge": np.concatenate([a["L3_gnn_W_edge"], a["L3_gnn_b_edge"][None]]),
        "w_last1": a["L3_gnn_W1"], "w_last2": a["L3_gnn_W2"],
        "last_vecs": np.stack([a["L3_gnn_b1"], a["L3_gnn_b2"], a["L3_gnn_bn_gamma"], a["L3_gnn_bn_beta"]]),
    }
    arrays = {"in_" + k: lay(v) for k, v in arrays.items()}
    nc = bacc.Bacc("TRN2", target_bir_lowering=False, num_devices=1)
    t = {k[3:]: nc.dram_tensor(k, v.shape, mybir.dt.from_np(v.dtype), kind="ExternalInput").ap() for k, v in arrays.items()}
    out = nc.dram_tensor("out_0", (N, D), F32, kind="ExternalOutput").ap()
    program(nc, t, out)
    return run_bass_kernel_spmd(nc, [arrays], core_ids=[0]).results[0]["out_0"]
```

```python
from contextlib import ExitStack

import concourse.bass as bass
from concourse import mybir

F32 = mybir.dt.float32
BF16 = mybir.dt.bfloat16
F16 = mybir.dt.float16
I32 = mybir.dt.int32
ALU = mybir.AluOpType
ACT = mybir.ActivationFunctionType
AX = mybir.AxisListType.X

P = 128
D = 64
N = 3125
NB = 125
NA = N // NB
E = 103125
TC = 27
NCH = 30
T = TC * NCH
EP = P * T
W1 = TC + 1
K10 = 10
NT = 9
TROWS = N + 1 + P
GR = 3
NG = TC // GR
XT = 7
TP = TC - XT
PAIR = 2
XB = (XT + PAIR - 1) // PAIR
RING = 10
CENTRE = N // 2
LAYERS = 5
EPS = 1e-5
BIG = 3.0e38
ROUND = 12582912.0
TG = 4
NGT = (NA + TG - 1) // TG
assert CENTRE <= 2048 and 2 * NA % RING == 0 and EP >= E and TC % GR == 0 and TC % NT == 0


def bc(ap, shape):
    return ap.to_broadcast(list(shape))


class Chain:

    def __init__(self, eng, sem, base=0):
        self.eng, self.sem, self.base, self.n = eng, sem, base, 0

    def __call__(self, ins):
        self.n += 1
        ins.then_inc(self.sem, 1)
        self.eng.wait_ge(self.sem, self.base + self.n)


def pieces(total, step):
    return [(i, min(step, total - i)) for i in range(0, total, step)]


class Linear:

    def __init__(self, shared, sources, weights, width, repeats=1):
        self.turned, self.held, self.made, self.added, self.stepped = shared["sems"]
        self.sources, self.weights, self.width = sources, weights, width
        self.nturn = NGT * len(sources)
        self.step = 512 // width if width > P else TG
        self.groups = pieces(NA, self.step)
        self.turn0, self.made0 = shared["count"]
        shared["count"] = (self.turn0 + repeats * self.nturn, self.made0 + repeats * len(self.groups))

    def pe(self, pe, nc, ps_turn, ps_out, held_tiles, ident, L=0):
        i = 0
        for src in self.sources:
            k = src.shape[2]
            for a0, n in pieces(NA, TG):
                if i >= 2:
                    pe.wait_ge(self.held, L * self.nturn + self.turn0 + i - 1)
                    pe.sem_inc(self.stepped, 1)
                for j in range(n):
                    ins = nc.tensor.transpose(ps_turn[0:k, i % 2, j * NB:(j + 1) * NB], src[:, a0 + j, :],
                                              ident[0:NB, 0:NB])
                ins.then_inc(self.turned, 1)
                i += 1
        pe.wait_ge(self.held, L * self.nturn + self.turn0 + self.nturn)
        for i, (a0, n) in enumerate(self.groups):
            if i >= 2:
                pe.wait_ge(self.added, L * len(self.groups) + self.made0 + i - 1)
            for j in range(n):
                for s, (src, w) in enumerate(zip(self.sources, self.weights)):
                    k = src.shape[2]
                    ins = nc.tensor.matmul(ps_out[0:NB, i % 2, j * self.width:(j + 1) * self.width],
                                           held_tiles[s][0:k, (a0 + j) * NB:(a0 + j + 1) * NB], w,
                                           start=(s == 0), stop=(s == len(self.sources) - 1))
            ins.then_inc(self.made, 1)

    def act(self, act, nc, ps_turn, held_tiles, L=0):
        i = 0
        for s, src in enumerate(self.sources):
            k = src.shape[2]
            for a0, n in pieces(NA, TG):
                act.wait_ge(self.turned, L * self.nturn + self.turn0 + i + 1)
                nc.scalar.activation(held_tiles[s][0:k, a0 * NB:(a0 + n) * NB], ps_turn[0:k, i % 2, 0:n * NB],
                                     ACT.Copy).then_inc(self.held, 1)
                i += 1

    def dve(self, dve, nc, ps_out, bias, out, L=0):
        for i, (a0, n) in enumerate(self.groups):
            dve.wait_ge(self.made, L * len(self.groups) + self.made0 + i + 1)
            nc.vector.tensor_tensor(out[:, a0:a0 + n, :],
                                    ps_out[0:NB, i % 2, 0:n * self.width].rearrange("p (a f) -> p a f", f=self.width),
                                    bc(bias[:, 0:self.width].unsqueeze(1), [NB, n, self.width]),
                                    ALU.add).then_inc(self.added, 1)
        dve.wait_ge(self.added, L * len(self.groups) + self.made0 + len(self.groups))


class Norm:

    def __init__(self, shared, stat, repeats=1):
        self.var_ready, self.root_ready = shared["sems"]
        self.start, self.stat = shared["count"], stat
        shared["count"] += repeats

    def dve(self, dve, nc, link, y, scratch, L=0):
        f = y.shape[2]
        mean, var, root, inv = (self.stat[:, i, :] for i in range(4))
        shape = [NB, NA, f]
        link(nc.vector.tensor_reduce(mean, y, AX, ALU.add))
        link(nc.vector.tensor_scalar(mean, mean, 1.0 / f, None, ALU.mult))
        link(nc.vector.tensor_tensor(y, y, bc(mean.unsqueeze(2), shape), ALU.subtract))
        link(nc.vector.tensor_tensor(scratch, y, y, ALU.mult))
        link(nc.vector.tensor_reduce(var, scratch, AX, ALU.add))
        nc.vector.tensor_scalar(var, var, 1.0 / f, EPS, ALU.mult, ALU.add).then_inc(self.var_ready, 1)
        dve.wait_ge(self.root_ready, L + self.start + 1)
        link(nc.vector.reciprocal(inv, root))
        link(nc.vector.tensor_tensor(y, y, bc(inv.unsqueeze(2), shape), ALU.mult))

    def act(self, act, nc, L=0):
        act.wait_ge(self.var_ready, L + self.start + 1)
        nc.scalar.activation(self.stat[:, 2, :], self.stat[:, 1, :], ACT.Sqrt).then_inc(self.root_ready, 1)

    LINKS = 7


class Gathers:

    def __init__(self, sem, name):
        self.gathered = [sem(f"{name}_gathered{k}") for k in range(2)]
        self.index_loaded = [sem(f"{name}_index_loaded{k}") for k in range(2)]
        self.used = [sem(f"{name}_used{k}") for k in range(2)]
        self.hot_made = sem(name + "_hot_made")
        self.hot_used = sem(name + "_hot_used")
        self.picked = sem(name + "_picked")
        self.split = sem(name + "_split")
        self.sp_done = sem(name + "_sp_done")
        self.stepped = sem(name + "_pool_stepped")

    def give_tokens(self, sp):
        for k in range(2):
            sp.sem_inc(self.used[k], 1)
        sp.sem_inc(self.hot_used, RING)
        sp.sem_inc(self.picked, 2)

    def load_index(self, sp, src, by_tile, index, tile_src, k, g, L):
        sp.wait_ge(self.used[k], L * (NCH // 2) + g + 1)
        at = (g * 2 + k) * TC
        sp.dma_start(index[:, k, :], src[:, bass.ds(at, TP)]).then_inc(self.index_loaded[k], 16)
        sp.dma_start(tile_src[:, k, :, :], bc(by_tile[bass.ds(at + TP, XT), :].unsqueeze(0), [P, XT, P])
                     ).then_inc(self.index_loaded[k], 16)

    def gather(self, pool, rows, index, got, L):
        with pool.Fori(0, NCH // 2) as g:
            for k in range(2):
                pool.wait_ge(self.index_loaded[k], L * (16 * NCH) + g * 32 + 32)
                pool.wait_ge(self.used[k], L * (NCH // 2) + g + 1)
                pool.sem_inc(self.stepped, 1)
                for i in range(TP):
                    pool.indirect_dma_start(got[:, k, i, :], None, rows,
                                            bass.IndirectOffsetOnAxis(ap=index[:, k, i:i + 1], axis=0)
                                            ).then_inc(self.gathered[k], 16)

    def wait_gathered(self, eng, k, g, L):
        eng.wait_ge(self.gathered[k], L * (16 * TP * NCH // 2) + g * (16 * TP) + 16 * TP)

    def split_rows(self, dve, nc, x, parts, rest, L):
        v = nc.vector
        link = Chain(dve, self.split, L * 4)
        link(v.tensor_copy(parts[:, :, 0, :], x))
        link(v.tensor_tensor(rest, x, parts[:, :, 0, :], ALU.subtract))
        link(v.tensor_copy(parts[:, :, 1, :], rest))
        link(v.tensor_tensor(parts[:, :, 2, :], rest, parts[:, :, 1, :], ALU.subtract))

    def make_hots(self, dve, nc, hots, tile_src, node_id, c, k, g, L, a0, a1):
        if a0 == 0:
            dve.wait_ge(self.index_loaded[k], L * (16 * NCH) + g * 32 + 32)
        for a in range(a0, a1):
            dve.wait_ge(self.hot_used, c * NA + (a + 1))
            nc.vector.tensor_scalar(hots[:, (k * NA + a) % RING, :],
                                    tile_src[0:NB, k, :, :].rearrange("b t e -> b (t e)"),
                                    node_id[:, a:a + 1], None, ALU.is_equal).then_inc(self.hot_made, 1)

    def pick(self, pe, nc, ps_pick, hots, parts, c, k, buffers):
        pe.wait_ge(self.picked, c + (3 - buffers))
        for a in range(NA):
            pe.wait_ge(self.hot_made, c * NA + (a + 1))
            for j in range(XT):
                ins = nc.tensor.matmul(ps_pick[:, k % buffers, j // PAIR, j % PAIR * 3 * D:(j % PAIR + 1) * 3 * D],
                                       hots[:, (k * NA + a) % RING, j * P:(j + 1) * P],
                                       parts[:, a, :, :].rearrange("b s f -> b (s f)"),
                                       start=(a == 0 and j % PAIR == 0), stop=(a == NA - 1), skip_group_check=True)
            ins.then_inc(self.hot_used, 1)

    def add_parts(self, dve, nc, ps_pick, got, c, k, g, L, buffers):
        dve.wait_ge(self.hot_used, c * NA + (NA + RING))
        dve.wait_ge(self.used[k], L * (NCH // 2) + g + 1)
        full = XT // PAIR
        for b0, b1, n in ((0, full, PAIR), (full, XB, XT % PAIR)):
            if n:
                ins = nc.vector.tensor_reduce(
                    got[:, k, TP + b0 * PAIR:TP + (b1 - 1) * PAIR + n, :].rearrange("p (b t) f -> p b t f", t=n),
                    ps_pick[:, k % buffers, b0:b1, 0:n * 3 * D].rearrange("p b (t s f) -> p b t f s", s=3, f=D),
                    AX, ALU.add)
        ins.then_inc(self.picked, 1)


class Carry:

    LINKS = 2

    def __init__(self, sem, name, reads):
        self.reads = reads
        self.turned, self.scanned = sem(name + "_tails_turned"), sem(name + "_carry_scanned")
        self.back, self.held = sem(name + "_carry_back"), sem(name + "_carry_held")
        self.brought, self.taken = sem(name + "_carry_brought"), sem(name + "_carry_taken")

    def pe(self, pe, nc, ps_carry, tails, carry_t, carry, carry_from, ident, tails_sem, tails_value, L):
        pe.wait_ge(tails_sem, tails_value)
        nc.tensor.transpose(ps_carry[:, 0, 0:P], tails[:], ident[:]).then_inc(self.turned, 1)
        pe.wait_ge(self.scanned, L * 2 + 2)
        nc.tensor.transpose(ps_carry[:, 1, 0:P], carry_t[:], ident[:]).then_inc(self.back, 1)
        pe.wait_ge(self.held, L + 1)
        for i, (a0, n) in enumerate(pieces(NA, TG)):
            if i >= 2:
                pe.wait_ge(self.taken, L * (self.reads * NGT) + self.reads * (i - 1))
            for j in range(n):
                ins = nc.tensor.matmul(ps_carry[0:NB, i % 2, j * P:(j + 1) * P], carry_from[:, a0 + j, :], carry[:],
                                       start=True, stop=True)
            ins.then_inc(self.brought, 1)

    def dve(self, dve, nc, link, ps_carry, tails_t, carry_t, carry, carry_mask, agg, no_carry, L):
        v = nc.vector
        dve.wait_ge(self.turned, L + 1)
        link(v.tensor_copy(tails_t[:], ps_carry[:, 0, 0:P]))
        v.tensor_tensor_scan(carry_t[0:D, :], carry_mask[0:D, :], tails_t[0:D, :], 0.0, ALU.min,
                             ALU.max).then_inc(self.scanned, 1)
        v.tensor_tensor_scan(carry_t[D:P, :], carry_mask[D:P, :], tails_t[D:P, :], 0.0, ALU.mult,
                             ALU.add).then_inc(self.scanned, 1)
        dve.wait_ge(self.back, L + 1)
        v.tensor_copy(carry[:], ps_carry[:, 1, 0:P]).then_inc(self.held, 1)
        for i, (a0, n) in enumerate(pieces(NA, TG)):
            dve.wait_ge(self.brought, L * NGT + i + 1)
            got = ps_carry[0:NB, i % 2, 0:n * P].rearrange("p (a f) -> p a f", f=P)
            at = slice(a0, a0 + n)
            v.tensor_tensor(agg[:, at, D:P], agg[:, at, D:P], got[:, :, D:P], ALU.add).then_inc(self.taken, 1)
            if no_carry is None:
                continue
            v.tensor_tensor(self.big[:, at, :], got[:, :, 0:D], bc(no_carry[:, at].unsqueeze(2), [NB, n, D]),
                            ALU.add).then_inc(self.taken, 1)
        dve.wait_ge(self.taken, L * (self.reads * NGT) + self.reads * NGT)
        if no_carry is not None:
            link(v.tensor_tensor(agg[:, :, 0:D], agg[:, :, 0:D], self.big[:], ALU.max))


def program(nc, t, out):
    top = ExitStack()

    def sem(name):
        return top.enter_context(nc.semaphore(name))

    def tiles(ctx, stage):
        def sb(name, shape, dt=F32):
            return ctx.enter_context(nc.sbuf_tensor(f"{stage}_{name}", list(shape), dt))

        def ps(name, shape, dt=F32):
            return ctx.enter_context(nc.psum_tensor(f"{stage}_{name}", list(shape), dt))
        return sb, ps

    def nodes(ap):
        return ap.rearrange("(b a) d -> b (a d)", a=NA)

    xc_rows = nc.dram_tensor("xc_rows", [N + 1, D + 1], F32).ap()
    first_rows = nc.dram_tensor("first_rows", [EP + NB, D + 1], F32).ap()
    tables = [nc.dram_tensor(f"table{i}", [TROWS, 2 * D], F32).ap() for i in range(NT)]
    scan_rows = nc.dram_tensor("scan_rows", [EP, 2 * D], F32).ap()
    h_rows = nc.dram_tensor("h_rows", [N + 1, D], F32).ap()
    by_tile = nc.dram_tensor("by_tile", [T, P], F16).ap()

    with top:
        sb, _ = tiles(top, "all")
        sb_top = sb
        ident = sb("ident", [P, P])
        later = sb("later", [P, P])
        earlier = sb("earlier", [P, P])
        lane = sb("lane", [P, 1])
        node_id = sb("node_id", [NB, NA])
        src_f = sb("src_f", [P, T])
        src_digits = sb("src_digits", [P, 2, T], BF16)
        ident_na = sb("ident_na", [P, P], BF16)
        count_h = sb("count_h", [P, NB], BF16)
        ident_h = sb("ident_h", [P, P], BF16)
        zero_h = sb("zero_h", [P, P], BF16)
        curv_part = sb("curv_part", [NB, 3, NA], BF16)
        keep = sb("keep", [P, NCH, W1])
        keep_big = sb("keep_big", [P, NCH, W1])
        carry_mask = sb("carry_mask", [P, P])
        carry_from = sb("carry_from", [P, NA, NB])
        no_carry = sb("no_carry", [NB, NA])
        end_row = sb("end_row", [NB, NA], I32)
        has_in = sb("has_in", [NB, NA])
        in_share = sb("in_share", [NB, NA])
        out_share = sb("out_share", [NB, NA])
        h = sb("h", [NB, NA, D])
        stat = sb("stat", [NB, 4, NA])
        products = {"sems": [sem("node_" + n) for n in ("turned", "held", "made", "added", "pe_stepped")], "count": (0, 0)}
        norms = {"sems": [sem("node_" + n) for n in ("var_ready", "root_ready")], "count": 0}

        pool_stepped = sem("pool_stepped")
        table_done = [sem(f"table_done{i}") for i in range(NT)]

        with ExitStack() as ctx:
            sb, ps = tiles(ctx, "prep")
            grid = sb("grid", [P, P], I32)
            count_i = sb("count_i", [P, P], I32)
            lane_i = sb("lane_i", [P, 1], I32)
            node_i = sb("node_i", [NB, NA], I32)
            ends_i = sb("ends_i", [P, 2, T], I32)
            dst_f = sb("dst_f", [P, T])
            dst_hi = sb("dst_hi", [P, T], BF16)
            dst_lo = sb("dst_lo", [P, T], BF16)
            work = sb("work", [P, T])
            work2 = sb("work2", [P, T])
            prev_last = sb("prev_last", [P, 1], I32)
            prev_f = sb("prev_f", [P, 1])
            cont = sb("cont", [P, 1])
            spans = sb("spans", [P, 1])
            curv = sb("curv", [NB, NA])
            curv_rest = sb("curv_rest", [NB, NA])
            hot_hi = sb("hot_hi", [P, 2, TC, NB], BF16)
            hot_lo = sb("hot_lo", [P, 2, TC, NA], BF16)
            deg = sb("deg", [NB, NA])
            run = sb("run", [NB, NA])
            start_f = sb("start_f", [NB, NA])
            end_f = sb("end_f", [NB, NA])
            nwork = sb("nwork", [NB, 4, NA])
            first_row = sb("first_row", [NB, NA], I32)
            xc = sb("xc", [NB, NA, D + 1])
            x0 = sb("x0", [NB, NA, D])
            zero = sb("zero", [P, TROWS])
            head = sb("head", [P, D + 1])
            ps_deg = ps("ps_deg", [P, 512])
            ps_misc = ps("ps_misc", [P, 2, 512])

            loaded, x_loaded, prev_loaded = sem("loaded"), sem("x_loaded"), sem("prev_loaded")
            iota_done, const_done, zeroed = sem("iota_done"), sem("const_done"), sem("zeroed")
            chain, digits = sem("prep_chain"), sem("digits")
            hot_ready = sem("dst_hot_ready")
            hot_used = sem("dst_hot_used")
            deg_made, totals, offsets, keys, keyed, key_used = (
                sem(n) for n in ("deg_made", "totals", "offsets", "keys", "keyed", "key_used"))
            first_ready, xc_ready, xc_stored, placed = (sem(n) for n in ("first_ready", "xc_ready", "xc_stored", "placed"))
            zeros_stored, head_got, head_put, cont_made, cont_rows = (
                sem(n) for n in ("zeros_stored", "head_got", "head_put", "cont_made", "cont_rows"))
            FZ = T * (D + 1) // 15
            first_flat = first_rows[0:EP, :].rearrange("(p t) d -> p (t d)", t=T)
            assert FZ <= 2 * TROWS and T * (D + 1) % 30 == 0

            with nc.Block() as block:

                @block.sync
                def _(sp):
                    sp.sem_inc(hot_used, 2)
                    sp.dma_start(ends_i[:, 0, :], t["src_pad"]).then_inc(loaded, 16)
                    sp.dma_start(ends_i[:, 1, :], t["dst_pad"]).then_inc(loaded, 16)
                    sp.dma_start(x0[:].rearrange("b a d -> b (a d)"), nodes(t["x"])).then_inc(x_loaded, 16)
                    sp.dma_start(curv[:], t["node_vec"].rearrange("(b a) -> b a", a=NA)).then_inc(x_loaded, 16)
                    sp.dma_start(h[:].rearrange("b a d -> b (a d)"), nodes(t["x"])).then_inc(x_loaded, 16)
                    sp.wait_ge(const_done, 2)
                    sp.dma_start(prev_last[1:P, :], t["dst_pad"][0:P - 1, T - 1:T],
                                 allow_slow_non_contiguous=True).then_inc(prev_loaded, 16)
                    for i in range(30):
                        sp.dma_start(first_flat[:, i * (FZ // 2):(i + 1) * (FZ // 2)],
                                     zero[:, 0:FZ // 2]).then_inc(zeros_stored, 16)
                    sp.dma_start(h_rows[N:N + 1, :], zero[0:1, 0:D]).then_inc(zeros_stored, 16)
                    sp.dma_start(xc_rows[N:N + 1, :], zero[0:1, 0:D + 1]).then_inc(xc_stored, 16)
                    sp.wait_ge(xc_ready, 2)
                    sp.dma_start(nodes(xc_rows[0:N, :]), xc[:].rearrange("b a d -> b (a d)")).then_inc(xc_stored, 16)
                    sp.wait_ge(head_got, 16)
                    sp.wait_ge(placed, 16 * NA)
                    sp.dma_start(first_rows[0:EP, :].rearrange("(p t) d -> p (t d)", t=T)[:, 0:D + 1],
                                 head[:]).then_inc(head_put, 16)
                    sp.wait_ge(head_put, 16)
                    for i in range(NT):
                        sp.wait_ge(table_done[i], 16)

                @block.gpsimd
                def _(pool):
                    nc.gpsimd.iota(grid[:], [[1, P]], base=0, channel_multiplier=-1).then_inc(iota_done, 1)
                    nc.gpsimd.iota(count_i[:], [[1, P]], base=0, channel_multiplier=0).then_inc(iota_done, 1)
                    nc.gpsimd.iota(lane_i[:], [[1, 1]], base=0, channel_multiplier=1).then_inc(iota_done, 1)
                    nc.gpsimd.iota(node_i[:], [[1, NA]], base=-CENTRE, channel_multiplier=NA).then_inc(iota_done, 1)
                    nc.gpsimd.memset(prev_last[:], -1).then_inc(const_done, 1)
                    nc.gpsimd.memset(zero[:], 0.0).then_inc(const_done, 1)
                    pool.wait_ge(const_done, 2)
                    for i in range(NT):
                        pool.dma_start(tables[i].rearrange("r d -> (r d)").rearrange("(p k) -> p k", p=P),
                                       zero[:, 0:TROWS]).then_inc(table_done[i], 16)
                    pool.wait_ge(loaded, 32)
                    pool.wait_ge(xc_stored, 32)
                    pool.indirect_dma_start(head[:], None, xc_rows,
                                            bass.IndirectOffsetOnAxis(ap=ends_i[:, 1, 0:1], axis=0)).then_inc(head_got, 16)
                    pool.wait_ge(first_ready, 1)
                    pool.wait_ge(zeros_stored, 16 * 31)
                    for a in range(NA):
                        pool.indirect_dma_start(first_rows, bass.IndirectOffsetOnAxis(ap=first_row[:, a:a + 1], axis=0),
                                                xc[:, a, :], None).then_inc(placed, 16)

                @block.vector
                def _(dve):
                    link = Chain(dve, chain)
                    v = nc.vector
                    dve.wait_ge(iota_done, 4)
                    v.tensor_scalar(ident[:], grid[:], 0.0, None, ALU.is_equal)
                    v.tensor_scalar(ident_h[:], grid[:], 0.0, None, ALU.is_equal)
                    v.tensor_scalar(ident_na[:], grid[:], 0.0, float(NA), ALU.is_equal, ALU.mult)
                    v.tensor_scalar(later[:], grid[:], 0.0, None, ALU.is_gt)
                    v.tensor_scalar(earlier[:], grid[:], 0.0, None, ALU.is_lt)
                    v.tensor_copy(count_h[:], count_i[:, 0:NB])
                    v.tensor_copy(lane[:], lane_i[:])
                    v.tensor_copy(node_id[:], node_i[:])
                    link(v.memset(zero_h[:], 0.0))
                    dve.wait_ge(x_loaded, 48)
                    v.tensor_copy(xc[:, :, 0:D], x0[:]).then_inc(xc_ready, 1)
                    v.tensor_copy(xc[:, :, D], curv[:]).then_inc(xc_ready, 1)
                    link(v.tensor_copy(curv_part[:, 0, :], curv[:]))
                    link(v.tensor_tensor(curv_rest[:], curv[:], curv_part[:, 0, :], ALU.subtract))
                    link(v.tensor_copy(curv_part[:, 1, :], curv_rest[:]))
                    link(v.tensor_tensor(curv_part[:, 2, :], curv_rest[:], curv_part[:, 1, :], ALU.subtract))
                    dve.wait_ge(loaded, 32)
                    for i, full, hi, lo in ((0, src_f, src_digits[:, 0, :], src_digits[:, 1, :]), (1, dst_f, dst_hi[:], dst_lo[:])):
                        link(v.tensor_copy(full[:], ends_i[:, i, :]))
                        link(v.tensor_scalar(work[:], full[:], 1.0 / NA, 0.5 / NA - 0.5, ALU.mult, ALU.add))
                        link(v.tensor_scalar(work[:], work[:], ROUND, ROUND, ALU.add, ALU.subtract))
                        link(v.tensor_copy(hi, work[:]))
                        link(v.tensor_scalar(work[:], work[:], -float(NA), None, ALU.mult))
                        link(v.tensor_tensor(lo, work[:], full[:], ALU.add))
                    link(v.memset(work2[:, 0:1], 0.0))
                    link(v.tensor_tensor(work2[:, 1:T], dst_f[:, 1:T], dst_f[:, 0:T - 1], ALU.is_equal))
                    link(v.memset(keep[:, :, 0:1], 0.0))
                    link(v.tensor_copy(keep[:, :, 1:W1], work2[:].rearrange("p (c t) -> p c t", t=TC)))
                    link(v.tensor_scalar(keep_big[:], keep[:], 2.0, -1.0, ALU.mult, ALU.add))
                    link(v.tensor_scalar(keep_big[:], keep_big[:], BIG, None, ALU.mult))
                    dve.wait_ge(prev_loaded, 16)
                    link(v.tensor_copy(prev_f[:], prev_last[:]))
                    link(v.tensor_tensor(cont[:], prev_f[:], dst_f[:, 0:1], ALU.is_equal))
                    link(v.tensor_tensor(spans[:], dst_f[:, 0:1], dst_f[:, T - 1:T], ALU.is_equal))
                    v.tensor_tensor(cont[:], cont[:], spans[:], ALU.mult).then_inc(cont_made, 1)
                    dve.wait_ge(cont_rows, 1)
                    link(v.tensor_copy(carry_mask[:], ps_misc[:, 0, 0:P]))
                    link(v.tensor_scalar(carry_mask[0:D, :], carry_mask[0:D, :], 2.0, -1.0, ALU.mult, ALU.add))
                    link(v.tensor_scalar(carry_mask[0:D, :], carry_mask[0:D, :], BIG, None, ALU.mult))

                    with dve.Fori(0, NCH // 2) as g:
                        for k in range(2):
                            dve.wait_ge(hot_used, g * 2 + (k + 1))
                            v.tensor_tensor(hot_hi[:, k, :, :], bc(count_h[:].unsqueeze(1), [P, TC, NB]),
                                            bc(dst_hi[:, bass.ds((g * 2 + k) * TC, TC)].unsqueeze(2), [P, TC, NB]),
                                            ALU.is_equal).then_inc(hot_ready, 1)
                            v.tensor_tensor(hot_lo[:, k, :, :], bc(count_h[:, 0:NA].unsqueeze(1), [P, TC, NA]),
                                            bc(dst_lo[:, bass.ds((g * 2 + k) * TC, TC)].unsqueeze(2), [P, TC, NA]),
                                            ALU.is_equal).then_inc(hot_ready, 1)

                    dve.wait_ge(deg_made, 1)
                    link(v.tensor_copy(deg[:], ps_deg[0:NB, 0:NA]))
                    link(v.memset(nwork[:, 3, :], 1.0))
                    link(v.tensor_tensor_scan(run[:], nwork[:, 3, :], deg[:], 0.0, ALU.mult, ALU.add))
                    v.tensor_copy(nwork[:, 0, 0:1], run[:, NA - 1:NA]).then_inc(totals, 1)
                    dve.wait_ge(offsets, 1)
                    link(v.tensor_tensor(end_f[:], run[:], bc(ps_misc[0:NB, 1, 0:1], [NB, NA]), ALU.add))
                    link(v.tensor_tensor(start_f[:], end_f[:], deg[:], ALU.subtract))
                    link(v.tensor_scalar(has_in[:], deg[:], 1.0, None, ALU.min))
                    link(v.tensor_scalar(nwork[:, 1, :], start_f[:], float(EP), None, ALU.subtract))
                    link(v.tensor_scalar(nwork[:, 1, :], nwork[:, 1, :], lane[0:NB, :], None, ALU.subtract))
                    link(v.tensor_tensor(nwork[:, 1, :], nwork[:, 1, :], has_in[:], ALU.mult))
                    link(v.tensor_scalar(nwork[:, 1, :], nwork[:, 1, :], lane[0:NB, :], float(EP), ALU.add, ALU.add))
                    v.tensor_copy(first_row[:], nwork[:, 1, :]).then_inc(first_ready, 1)
                    link(v.tensor_scalar(nwork[:, 2, :], deg[:], 1.0, None, ALU.max))
                    link(v.reciprocal(in_share[:], nwork[:, 2, :]))
                    link(v.tensor_tensor(in_share[:], in_share[:], has_in[:], ALU.mult))
                    link(v.tensor_scalar(end_f[:], end_f[:], 1.0, 0.0, ALU.subtract, ALU.max))
                    link(v.tensor_copy(end_row[:], end_f[:]))
                    link(v.tensor_scalar(nwork[:, 0, :], end_f[:], 1.0 / T, 0.5 / T - 0.5, ALU.mult, ALU.add))
                    link(v.tensor_scalar(nwork[:, 0, :], nwork[:, 0, :], ROUND, ROUND, ALU.add, ALU.subtract))
                    link(v.tensor_scalar(nwork[:, 1, :], nwork[:, 0, :], float(T), None, ALU.mult))
                    link(v.tensor_tensor(nwork[:, 1, :], start_f[:], nwork[:, 1, :], ALU.is_lt))
                    link(v.tensor_tensor(nwork[:, 1, :], nwork[:, 1, :], has_in[:], ALU.mult))
                    link(v.tensor_scalar(no_carry[:], nwork[:, 1, :], 1.0, BIG, ALU.subtract, ALU.mult))
                    link(v.tensor_tensor(nwork[:, 2, :], nwork[:, 0, :], nwork[:, 1, :], ALU.mult))
                    v.tensor_scalar(nwork[:, 2, :], nwork[:, 2, :], 1.0, None, ALU.subtract).then_inc(keys, 1)
                    for i, (a0, n) in enumerate(pieces(NA, TG)):
                        dve.wait_ge(keyed, i + 1)
                        v.tensor_scalar(carry_from[:, a0:a0 + n, :],
                                        ps_misc[:, i % 2, 0:n * NB].rearrange("p (a b) -> p a b", b=NB),
                                        lane[:], None, ALU.is_equal).then_inc(key_used, 1)

                @block.tensor
                def _(pe):
                    pe.wait_ge(chain, 1)
                    nc.tensor.matmul(ps_deg[0:NB, 0:NA], zero_h[:, 0:NB], zero_h[:, 0:NA], start=True, stop=False,
                                     skip_group_check=True)
                    pe.wait_ge(cont_made, 1)
                    nc.tensor.matmul(ps_misc[:, 0, 0:P], bc(cont[:], [P, P]), ident[:],
                                     start=True, stop=True).then_inc(cont_rows, 1)
                    with pe.Fori(0, NCH // 2) as g:
                        for k in range(2):
                            pe.wait_ge(hot_ready, g * 4 + (2 * k + 2))
                            for j in range(TC):
                                ins = nc.tensor.matmul(ps_deg[0:NB, 0:NA], hot_hi[:, k, j, :], hot_lo[:, k, j, :],
                                                       start=False, stop=False, skip_group_check=True)
                            ins.then_inc(hot_used, 1)
                    nc.tensor.matmul(ps_deg[0:NB, 0:NA], zero_h[:, 0:NB], zero_h[:, 0:NA],
                                     start=False, stop=True, skip_group_check=True).then_inc(deg_made, 1)
                    pe.wait_ge(totals, 1)
                    nc.tensor.matmul(ps_misc[0:NB, 1, 0:1], later[0:NB, 0:NB], nwork[:, 0, 0:1],
                                     start=True, stop=True).then_inc(offsets, 1)
                    pe.wait_ge(keys, 1)
                    for i, (a0, n) in enumerate(pieces(NA, TG)):
                        if i >= 2:
                            pe.wait_ge(key_used, i - 1)
                        for j in range(n):
                            ins = nc.tensor.matmul(ps_misc[:, i % 2, j * NB:(j + 1) * NB],
                                                   bc(nwork[:, 2, a0 + j:a0 + j + 1], [NB, P]), ident[0:NB, 0:NB],
                                                   start=True, stop=True)
                        ins.then_inc(keyed, 1)

        with ExitStack() as ctx:
            sb, ps = tiles(ctx, "scatter")
            CF = D + 1
            filled = sb("filled", [P, 2, TC, CF])
            fill_in = sb("fill_in", [P, CF * W1])
            fill_keep = sb("fill_keep", [P, CF * W1], BF16)
            fill_out = sb("fill_out", [P, CF * W1])
            w_curv = sb("w_curv", [P, D])
            b_curv = sb("b_curv", [P, D])
            diff = sb("diff", [P, TC])
            gate = sb("gate", [P, D, TC])
            rows = sb("rows", [P, 2, TC, 2 * D])
            same = sb("same", [P, 2, TC, P])
            before = sb("before", [P, TC, P], BF16)
            hot_hi = sb("hot_hi", [P, TC, NB], BF16)
            hot_lo = sb("hot_lo", [P, TC, NA], BF16)
            turned_hot = sb("turned_hot", [NB, 2, GR, P], BF16)
            picked = sb("picked", [P, TC, NA])
            curv_src = sb("curv_src", [P, 2, TC])
            dup = sb("dup", [P, 2, TC])
            spare = sb("spare", [P, 1])
            to_row = sb("to_row", [P, 2, TC], I32)
            src_now = sb("src_now", [P, 2, 2, TC], BF16)
            ps_deg = ps("ps_deg", [P, 512])
            ps_hot = ps("ps_hot", [P, 1024], BF16)
            ps_pick = ps("ps_pick", [P, 2, 512])
            sums = sb("sums", [P, 2, TC, 2 * D])
            ps_src = ps("ps_src", [P, 2, 512])
            ps_sum = ps("ps_sum", [P, 2, 512])
            in3, keep3, out3 = (a[:].rearrange("p (f t) -> p f t", t=W1) for a in (fill_in, fill_keep, fill_out))

            fill_loaded = [sem(f"fill_loaded{k}") for k in range(2)]
            edge_loaded = [sem(f"edge_loaded{k}") for k in range(2)]
            curv_loaded, fill_turned, fill_masked, fill_scanned = (
                sem(n) for n in ("curv_loaded", "fill_turned", "fill_masked", "fill_scanned"))
            wchain, arg_ready, gate_ready, rows_made = (sem(n) for n in ("wchain", "arg_ready", "gate_ready", "rows_made"))
            src_rows, same_made, summed, sums_held, same_free = (
                sem(n) for n in ("src_rows", "same_made", "summed", "sums_held", "same_free"))
            index_ready, src_copied = sem("index_ready"), sem("src_copied")
            hot_ready, hot_turned, hot_held, looked, pick_used, deg_made = (
                sem("src_" + n) for n in ("hot_ready", "hot_turned", "hot_held", "looked", "pick_used", "deg_made"))
            sent = [sem(f"sent{k}") for k in range(2)]

            with nc.Block() as block:

                @block.sync
                def _(sp):
                    sp.dma_start(w_curv[:], bc(t["w_curv"], [P, D])).then_inc(curv_loaded, 16)
                    sp.dma_start(b_curv[:], bc(t["b_curv"], [P, D])).then_inc(curv_loaded, 16)
                    sp.wait_ge(curv_loaded, 32)
                    sp.sem_inc(fill_turned, 2)
                    sp.sem_inc(same_free, 2)
                    first_by_part = first_rows[0:EP, :].rearrange("(p t) d -> p t d", t=T)
                    edge_by_part = t["edge64"].rearrange("(p t) d -> p t d", t=T)
                    with sp.Fori(0, NCH // 2) as g:
                        for k in range(2):
                            sp.wait_ge(fill_turned, g * 2 + (k + 1))
                            sp.dma_start(filled[:, k, :, :], first_by_part[:, bass.ds((g * 2 + k) * TC, TC), :]
                                         ).then_inc(fill_loaded[k], 16)
                            sp.wait_ge(same_free, g * 2 + (k + 1))
                            sp.dma_start(rows[:, k, :, D:2 * D], edge_by_part[:, bass.ds((g * 2 + k) * TC, TC), :]
                                         ).then_inc(edge_loaded[k], 16)


                @block.scalar
                def _(act):
                    def copy_sources(c, k):
                        nc.scalar.activation(src_now[:, k, :, :], src_digits[:, :, bass.ds(c * TC, TC)],
                                             ACT.Copy).then_inc(src_copied, 1)

                    def hold_hot(c, j):
                        act.wait_ge(hot_turned, c * NG + (j + 1))
                        if j >= 2:
                            act.wait_ge(looked, c * NG + (j - 1))
                        nc.scalar.activation(turned_hot[:, j % 2, :, :].rearrange("p t e -> p (t e)"),
                                             ps_hot[0:NB, 0:GR * P], ACT.Copy).then_inc(hot_held, 1)

                    def hold_sums(c, k, q, j):
                        act.wait_ge(summed, c * NG + (j + 1))
                        if j == 0:
                            act.wait_ge(sent[k], q + 1)
                        nc.scalar.activation(sums[:, k, j * GR:(j + 1) * GR, :].rearrange("p t f -> p (t f)"),
                                             ps_sum[:, j % 2, 0:GR * P], ACT.Copy).then_inc(sums_held, 1)

                    def step(i, k, q, q_before, first=False, last=False):
                        if not last:
                            copy_sources(i + 1, 1 - k)
                        act.wait_ge(fill_scanned, i + 1)
                        nc.scalar.activation(keep3, bc(keep[:, bass.ds(i, 1), :], [P, CF, W1]),
                                             ACT.Copy).then_inc(fill_masked, 1)
                        act.wait_ge(fill_loaded[k], q * 16 + 16)
                        nc.scalar.activation(in3[:, :, 1:W1], filled[:, k, :, :].rearrange("p t f -> p f t"),
                                             ACT.Copy).then_inc(fill_turned, 1)
                        for j in range(NG):
                            if not last:
                                hold_hot(i + 1, j)
                            if not first:
                                hold_sums(i - 1, 1 - k, q_before, j)
                        act.wait_ge(arg_ready, i + 1)
                        nc.scalar.activation(gate[:], gate[:], ACT.Sigmoid).then_inc(gate_ready, 1)

                    copy_sources(0, 0)
                    for j in range(NG):
                        hold_hot(0, j)
                    step(0, 0, 0, 0, first=True)
                    with act.Fori(0, NCH // 2 - 1) as g:
                        step(g * 2 + 1, 1, g, g)
                        step(g * 2 + 2, 0, g + 1, g)
                    step(NCH - 1, 1, NCH // 2 - 1, NCH // 2 - 1, last=True)
                    for j in range(NG):
                        hold_sums(NCH - 1, 1, NCH // 2 - 1, j)

                @block.vector
                def _(dve):
                    v = nc.vector
                    link = Chain(dve, wchain)
                    dve.wait_ge(curv_loaded, 32)
                    dve.sem_inc(fill_scanned, 1)
                    dve.sem_inc(sent[0], 1)
                    link(v.tensor_scalar(spare[:], lane[:], float(N + 1), None, ALU.add))
                    link(v.memset(fill_out[:], 0.0))

                    def make_hot(c):
                        v.tensor_tensor(hot_hi[:], bc(count_h[:].unsqueeze(1), [P, TC, NB]),
                                        bc(src_digits[:, 0, bass.ds(c * TC, TC)].unsqueeze(2), [P, TC, NB]),
                                        ALU.is_equal).then_inc(hot_ready, 1)
                        v.tensor_tensor(hot_lo[:], bc(count_h[:, 0:NA].unsqueeze(1), [P, TC, NA]),
                                        bc(src_digits[:, 1, bass.ds(c * TC, TC)].unsqueeze(2), [P, TC, NA]),
                                        ALU.is_equal).then_inc(hot_ready, 1)

                    def prepare(c, k, link, lag=True):
                        def pick(j):
                            at = slice(j * GR, (j + 1) * GR)
                            dve.wait_ge(looked, c * NG + (j + 1))
                            v.tensor_tensor(picked[:, at, :],
                                            ps_pick[:, j % 2, 0:GR * NA].rearrange("p (t a) -> p t a", a=NA),
                                            hot_lo[:, at, :], ALU.mult).then_inc(pick_used, 1)

                        for j in range(NG):
                            at = slice(j * GR, (j + 1) * GR)
                            dve.wait_ge(src_rows, c * NG + (j + 1))
                            if lag:
                                dve.wait_ge(summed, c * NG - (2 * NG - j - 1))
                            v.tensor_tensor(same[:, k, at, :],
                                            ps_src[:, j % 2, 0:GR * P].rearrange("p (t e) -> p t e", e=P),
                                            bc(src_f[:, bass.ds(c * TC + j * GR, GR)].unsqueeze(2), [P, GR, P]),
                                            ALU.is_equal).then_inc(same_made, 1)
                            if j:
                                pick(j - 1)
                            dve.wait_ge(same_made, c * NG + (j + 1))
                            for i in range(j * GR, (j + 1) * GR):
                                ins = v.tensor_tensor_reduce(out=before[:, i, :], in0=same[:, k, i, :], in1=earlier[:],
                                                             scale=1.0, scalar=0.0, op0=ALU.mult, op1=ALU.add,
                                                             accum_out=dup[:, k, i:i + 1])
                        link(ins)
                        pick(NG - 1)
                        dve.wait_ge(pick_used, c * NG + NG)
                        link(v.tensor_reduce(curv_src[:, k, :], picked[:], AX, ALU.add))

                    def make_rows(c, k, q, link):
                        link(v.tensor_scalar(dup[:, k, :], dup[:, k, :], 1.0, None, ALU.min))
                        link(v.scalar_tensor_tensor(out=diff[:], in0=src_f[:, bass.ds(c * TC, TC)], scalar=spare[:, 0:1],
                                                    in1=dup[:, k, :], op0=ALU.subtract, op1=ALU.mult))
                        dve.wait_ge(sent[k], q + 1)
                        v.tensor_tensor(to_row[:, k, :], src_f[:, bass.ds(c * TC, TC)], diff[:],
                                        ALU.subtract).then_inc(index_ready, 1)
                        dve.wait_ge(fill_masked, c + 1)
                        dve.wait_ge(fill_turned, c + 3)
                        link(v.tensor_copy(in3[:, :, 0:1], out3[:, :, TC:W1]))
                        v.tensor_tensor_scan(fill_out[:], fill_keep[:], fill_in[:], 0.0, ALU.mult,
                                             ALU.add).then_inc(fill_scanned, 1)
                        dve.wait_ge(fill_scanned, c + 2)
                        dve.wait_ge(index_ready, c + 1)
                        link(v.tensor_tensor(diff[:], curv_src[:, k, :], out3[:, D, 1:W1], ALU.subtract))
                        link(v.scalar_tensor_tensor(out=diff[:], in0=diff[:], scalar=-1.0, in1=diff[:], op0=ALU.mult,
                                                    op1=ALU.max))
                        v.tensor_tensor(gate[:], bc(diff[:].unsqueeze(1), [P, D, TC]),
                                        bc(w_curv[:].unsqueeze(2), [P, D, TC]), ALU.mult).then_inc(rows_made, 1)
                        dve.wait_ge(rows_made, c * 2 + 1)
                        v.tensor_tensor(gate[:], gate[:], bc(b_curv[:].unsqueeze(2), [P, D, TC]),
                                        ALU.add).then_inc(arg_ready, 1)
                        dve.wait_ge(gate_ready, c + 1)
                        dve.wait_ge(same_free, c + 1)
                        v.tensor_tensor(rows[:, k, :, 0:D].rearrange("p t f -> p f t"), gate[:], out3[:, 0:D, 1:W1],
                                        ALU.mult).then_inc(rows_made, 1)
                        dve.wait_ge(rows_made, c * 2 + 2)

                    def step(i, k, q, link, lag=True, hot=True, last=False):
                        if not last:
                            prepare(i + 1, 1 - k, link, lag)
                        if hot:
                            make_hot(i + 2)
                        make_rows(i, k, q, link)

                    make_hot(0)
                    prepare(0, 0, link, lag=False)
                    make_hot(1)
                    base, per = link.n, 7
                    step(0, 0, 0, link, lag=False)
                    assert link.n == base + per
                    with dve.Fori(0, NCH // 2 - 2) as g:
                        step(g * 2 + 1, 1, g, Chain(dve, wchain, g * (2 * per) + (base + per)))
                        step(g * 2 + 2, 0, g + 1, Chain(dve, wchain, g * (2 * per) + (base + 2 * per)))
                    link = Chain(dve, wchain, base + (NCH - 3) * per)
                    step(NCH - 3, 1, NCH // 2 - 2, link)
                    step(NCH - 2, 0, NCH // 2 - 1, link, hot=False)
                    step(NCH - 1, 1, NCH // 2 - 1, link, hot=False, last=True)
                    dve.wait_ge(deg_made, 1)
                    link(v.tensor_scalar(stat[:, 0, :], ps_deg[0:NB, 0:NA], 1.0, None, ALU.max))
                    link(v.reciprocal(out_share[:], stat[:, 0, :]))

                @block.tensor
                def _(pe):
                    def spread(c, k, j):
                        if j >= 2:
                            pe.wait_ge(same_made, c * NG + (j - 1))
                        for i in range(j * GR, (j + 1) * GR):
                            for d, scaled in ((0, ident_na), (1, ident_h)):
                                ins = nc.tensor.matmul(ps_src[:, j % 2, (i % GR) * P:(i % GR + 1) * P],
                                                       bc(src_now[:, k, d, i:i + 1], [P, P]), scaled[:],
                                                       start=(d == 0), stop=(d == 1))
                        ins.then_inc(src_rows, 1)

                    def turn_hot(c, j):
                        if j:
                            pe.wait_ge(hot_held, c * NG + j)
                        for i in range(GR):
                            ins = nc.tensor.transpose(ps_hot[0:NB, i * P:(i + 1) * P], hot_hi[:, j * GR + i, :],
                                                      ident_h[:])
                        ins.then_inc(hot_turned, 1)
                        for i in range(j * GR, (j + 1) * GR):
                            nc.tensor.matmul(ps_deg[0:NB, 0:NA], hot_hi[:, i, :], hot_lo[:, i, :], start=False,
                                             stop=False, skip_group_check=True)

                    def look_up(c, j):
                        if j >= 2:
                            pe.wait_ge(pick_used, c * NG + (j - 1))
                        pe.wait_ge(hot_held, c * NG + (j + 1))
                        for i in range(GR):
                            for s in range(3):
                                ins = nc.tensor.matmul(ps_pick[:, j % 2, i * NA:(i + 1) * NA],
                                                       turned_hot[:, j % 2, i, :], curv_part[:, s, :],
                                                       start=(s == 0), stop=(s == 2))
                        ins.then_inc(looked, 1)

                    def add_up(c, k, j):
                        if j >= 2:
                            pe.wait_ge(sums_held, c * NG + (j - 1))
                        for i in range(j * GR, (j + 1) * GR):
                            ins = nc.tensor.matmul(ps_sum[:, j % 2, (i % GR) * P:(i % GR + 1) * P], same[:, k, i, :],
                                                   rows[:, k, i, :], start=True, stop=True)
                        ins.then_inc(summed, 1)

                    def step(i, k, q_before, first=False, last=False):
                        if not last:
                            pe.wait_ge(hot_ready, i * 2 + 4)
                            pe.wait_ge(src_copied, i + 2)
                        for j in range(NG):
                            if not last:
                                turn_hot(i + 1, j)
                                if j:
                                    look_up(i + 1, j - 1)
                                spread(i + 1, 1 - k, j)
                            if not first:
                                if j == 0:
                                    pe.wait_ge(rows_made, i * 2)
                                    pe.wait_ge(edge_loaded[1 - k], q_before * 16 + 16)
                                add_up(i - 1, 1 - k, j)
                        if not last:
                            look_up(i + 1, NG - 1)
                        if not first:
                            pe.wait_ge(sums_held, i * NG)
                            pe.sem_inc(same_free, 1)

                    nc.tensor.matmul(ps_deg[0:NB, 0:NA], zero_h[:, 0:NB], zero_h[:, 0:NA], start=True, stop=False,
                                     skip_group_check=True)
                    pe.wait_ge(hot_ready, 2)
                    pe.wait_ge(src_copied, 1)
                    for j in range(NG):
                        turn_hot(0, j)
                        look_up(0, j)
                        spread(0, 0, j)
                    step(0, 0, 0, first=True)
                    with pe.Fori(0, NCH // 2 - 1) as g:
                        step(g * 2 + 1, 1, g)
                        step(g * 2 + 2, 0, g)
                    step(NCH - 1, 1, NCH // 2 - 1, last=True)
                    pe.wait_ge(rows_made, NCH * 2)
                    pe.wait_ge(edge_loaded[1], NCH // 2 * 16)
                    for j in range(NG):
                        add_up(NCH - 1, 1, j)
                    nc.tensor.matmul(ps_deg[0:NB, 0:NA], zero_h[:, 0:NB], zero_h[:, 0:NA], start=False, stop=True,
                                     skip_group_check=True).then_inc(deg_made, 1)

                @block.gpsimd
                def _(pool):
                    with pool.Fori(0, NCH // 2) as g:
                        for k in range(2):
                            c = g * 2 + k
                            pool.wait_ge(index_ready, c + 1)
                            for i in range(TC):
                                if i % GR == 0:
                                    pool.wait_ge(sums_held, c * NG + (i // GR + 1))
                                pool.wait_ge(table_done[i % NT], c * (16 * TC // NT) + 16 * (i // NT + 1))
                                pool.sem_inc(pool_stepped, 1)
                                pool.indirect_dma_start(
                                    tables[i % NT], bass.IndirectOffsetOnAxis(ap=to_row[:, k, i:i + 1], axis=0),
                                    sums[:, k, i, :], None, compute_op=ALU.add).then_inc(table_done[i % NT], 16)
                                if i == NT - 1:
                                    pool.sem_inc(sent[1 - k], 1)
                    for i in range(NT):
                        pool.wait_ge(table_done[i], 16 * (1 + NCH * TC // NT))

        res = sb_top("res", [NB, NA, D])
        hl = sb_top("hl", [NB, NA, D])
        with ExitStack() as ctx:
            sb, ps = tiles(ctx, "nodes01")
            acc = sb("acc", [NB, NA, 2 * D])
            part = sb("part", [NB, 2, NA * 2 * D])
            y = sb("y", [NB, NA, D])
            y2 = sb("y2", [NB, NA, D])
            scratch = sb("scratch", [NB, NA, D])
            heldA = sb("heldA", [P, NA * NB])
            heldB = sb("heldB", [P, NA * NB])
            w = {n: sb("w_" + n, [D, D]) for n in ("lin0", "l1x", "l1v", "l1u", "l1o", "adapt")}
            b = {n: sb("b_" + n, [NB, D]) for n in ("lin0", "l1h", "l1o", "adapt")}
            u0 = sb("u0", [D, 1])
            src_turned = sb("src_turned", [P, T], I32)
            src_half = sb("src_half", [P, T], F16)
            ps_turn = ps("ps_turn", [P, 2, 512])
            ps_out = ps("ps_out", [P, 2, 512])
            ps_u = ps("ps_u", [P, 512])
            wl, tab_added, nchain = (sem(n) for n in ("w01_loaded", "tab_added", "n01_chain"))
            turned_loaded, half_ready, half_put = (sem(n) for n in ("turned_loaded", "half_ready", "half_put"))
            tab_got = [sem(f"tab_got{k}") for k in range(2)]
            ready0, ready1, ready2, ready3, u_made, gelu_in, gelu_out, h_ready, h_put = (
                sem("n01_" + n) for n in ("mean", "x1", "hid", "x2", "u_made", "gelu_in", "gelu_out", "h_ready", "h_put"))
            lin0 = Linear(products, [acc[:, :, 0:D]], [w["lin0"][:]], D)
            lin1 = Linear(products, [h[:], acc[:, :, D:2 * D]], [w["l1x"][:], w["l1v"][:]], D)
            lin2 = Linear(products, [y[:]], [w["l1o"][:]], D)
            adapt = Linear(products, [h[:]], [w["adapt"][:]], D)
            norm0, norm1 = Norm(norms, stat), Norm(norms, stat)
            held = [heldA, heldB]

            with nc.Block() as block:

                @block.sync
                def _(sp):
                    sp.dma_start(src_turned[:], t["src_turned"]).then_inc(turned_loaded, 16)
                    for i in range(NT):
                        if i >= 2:
                            sp.wait_ge(tab_added, i - 1)
                        sp.dma_start(part[:, i % 2, :], nodes(tables[i][0:N, :])).then_inc(tab_got[i % 2], 16)
                        if i == 1:
                            for n in w:
                                sp.dma_start(w[n][:], t["w_" + n]).then_inc(wl, 16)
                            for n in b:
                                sp.dma_start(b[n][:], bc(t["b_" + n], [NB, D])).then_inc(wl, 16)
                            sp.dma_start(u0[:], t["u0"]).then_inc(wl, 16)
                    sp.wait_ge(half_ready, 1)
                    sp.dma_start(by_tile.rearrange("t p -> (t p)").rearrange("(q k) -> q k", k=T),
                                 src_half[:]).then_inc(half_put, 16)
                    sp.wait_ge(half_put, 16)
                    sp.wait_ge(h_ready, 1)
                    sp.dma_start(nodes(h_rows[0:N, :]), h[:].rearrange("b a d -> b (a d)")).then_inc(h_put, 16)
                    sp.wait_ge(h_put, 16)

                @block.vector
                def _(dve):
                    v = nc.vector
                    link = Chain(dve, nchain)
                    flat = acc[:].rearrange("b a d -> b (a d)")
                    dve.wait_ge(turned_loaded, 16)
                    v.tensor_scalar(src_half[:], src_turned[:], float(CENTRE), None, ALU.subtract).then_inc(half_ready, 1)
                    for i in range(NT):
                        dve.wait_ge(tab_got[i % 2], 16 * (i // 2 + 1))
                        if i == 0:
                            v.tensor_copy(flat, part[:, 0, :]).then_inc(tab_added, 1)
                        else:
                            v.tensor_tensor(flat, flat, part[:, i % 2, :], ALU.add).then_inc(tab_added, 1)
                        dve.wait_ge(tab_added, i + 1)
                    v.tensor_tensor(acc[:], acc[:], bc(out_share[:].unsqueeze(2), [NB, NA, 2 * D]),
                                    ALU.mult).then_inc(ready0, 1)
                    dve.wait_ge(wl, 16 * (len(w) + len(b) + 1))
                    lin0.dve(dve, nc, ps_out, b["lin0"], y)
                    dve.sem_inc(gelu_in, 1)
                    dve.wait_ge(gelu_out, 1)
                    link(v.tensor_tensor(h[:], h[:], y2[:], ALU.add))
                    norm0.dve(dve, nc, link, h[:], scratch[:])
                    dve.sem_inc(ready1, 1)
                    dve.wait_ge(u_made, 1)
                    link(v.tensor_tensor(b["l1h"][:], b["l1h"][:], ps_u[0:NB, 0:D], ALU.add))
                    lin1.dve(dve, nc, ps_out, b["l1h"], y)
                    v.tensor_scalar(y[:], y[:], 0.0, None, ALU.max).then_inc(ready2, 1)
                    lin2.dve(dve, nc, ps_out, b["l1o"], y2)
                    link(v.tensor_scalar(y2[:], y2[:], 0.0, None, ALU.max))
                    link(v.tensor_tensor(h[:], h[:], y2[:], ALU.add))
                    norm1.dve(dve, nc, link, h[:], scratch[:])
                    dve.sem_inc(h_ready, 1)
                    dve.sem_inc(ready3, 1)
                    link(v.tensor_copy(hl[:], h[:]))
                    adapt.dve(dve, nc, ps_out, b["adapt"], res)

                @block.scalar
                def _(act):
                    lin0.act(act, nc, ps_turn, held)
                    act.wait_ge(gelu_in, 1)
                    nc.scalar.activation(y2[:], y[:], ACT.Gelu).then_inc(gelu_out, 1)
                    norm0.act(act, nc)
                    lin1.act(act, nc, ps_turn, held)
                    lin2.act(act, nc, ps_turn, held)
                    norm1.act(act, nc)
                    adapt.act(act, nc, ps_turn, held)

                @block.tensor
                def _(pe):
                    pe.wait_ge(wl, 16 * (len(w) + len(b) + 1))
                    nc.tensor.matmul(ps_u[0:NB, 0:D], bc(u0[:], [D, NB]), w["l1u"][:], start=True,
                                     stop=True).then_inc(u_made, 1)
                    pe.wait_ge(ready0, 1)
                    lin0.pe(pe, nc, ps_turn, ps_out, held, ident)
                    pe.wait_ge(ready1, 1)
                    lin1.pe(pe, nc, ps_turn, ps_out, held, ident)
                    pe.wait_ge(ready2, 1)
                    lin2.pe(pe, nc, ps_turn, ps_out, held, ident)
                    pe.wait_ge(ready3, 1)
                    adapt.pe(pe, nc, ps_turn, ps_out, held, ident)

        with ExitStack() as ctx:
            sb, ps = tiles(ctx, "sage")
            agg = sb("agg", [NB, NA, 2 * D])
            run_max = sb("run_max", [P, D * W1])
            run_sum = sb("run_sum", [P, D * W1])
            w_agg = sb("w_agg", [2 * D, D])
            w_self = sb("w_self", [D, D])
            vecs = sb("vecs", [NB, 3, D])
            tails = sb("tails", [P, P])
            tails_t = sb("tails_t", [P, P])
            carry_t = sb("carry_t", [P, P])
            carry = sb("carry", [P, P])
            max3, sum3 = (a[:].rearrange("p (f t) -> p f t", t=W1) for a in (run_max, run_sum))
            source_rows = Gathers(sem, "source")
            names = ("layer_loaded", "sage_masks", "sage_scanned", "sage_rows", "sage_stored", "sage_chain", "ends_got",
                     "node_chain", "agg_ready", "silu_in", "silu_out", "h_put2", "sage_zeroed")
            (layer_loaded, masks, scanned, rows_ready, rows_stored, schain, ends_got, nodechain, agg_ready, silu_in,
             silu_out, h_put2, sage_zeroed) = (sem(n) for n in names)
            fix = Carry(sem, "sage", 2)
            conv = Linear(products, [agg[:], hl[:]], [w_agg[:], w_self[:]], D, LAYERS)
            norm = Norm(norms, stat, LAYERS)

            with nc.Block() as block:

                @block.vector
                def _(dve):
                    nc.vector.memset(run_max[:], 0.0).then_inc(sage_zeroed, 1)
                    nc.vector.memset(run_sum[:], 0.0).then_inc(sage_zeroed, 1)
                    dve.wait_ge(sage_zeroed, 2)

                @block.sync
                def _(sp):
                    source_rows.give_tokens(sp)

            with nc.Fori(0, LAYERS) as L:
                with ExitStack() as ctx2:
                    sb, ps = tiles(ctx2, "sage_edges")
                    index = sb("index", [P, 2, TP], I32)
                    tile_src = sb("tile_src", [P, 2, XT, P], F16)
                    hots = sb("hots", [NB, RING, XT * P], BF16)
                    parts = sb("parts", [NB, NA, 3, D], BF16)
                    rest = sb("rest", [NB, NA, D])
                    ps_pick = ps("ps_pick", [P, 2, XB, 512])
                    got = sb("got", [P, 2, TC, D])
                    turned = sb("turned", [P, D * W1])
                    mask_max = sb("mask_max", [P, D * W1], BF16)
                    mask_sum = sb("mask_sum", [P, D * W1], BF16)
                    both = sb("both", [P, TC, 2 * D])
                    in3, mm3, ms3 = (a[:].rearrange("p (f t) -> p f t", t=W1) for a in (turned, mask_max, mask_sum))
                    rows_by_part = scan_rows.rearrange("(p t) d -> p t d", t=T)

                    with nc.Block() as block:

                        @block.sync
                        def _(sp):
                            sp.dma_start(w_agg[:], t["w_agg"][bass.ds(L * (2 * D), 2 * D), :]).then_inc(layer_loaded, 16)
                            sp.dma_start(w_self[:], t["w_self"][bass.ds(L * D, D), :]).then_inc(layer_loaded, 16)
                            sp.dma_start(vecs[:], bc(t["conv_vecs"][bass.ds(L, 1), :, :], [NB, 3, D])).then_inc(layer_loaded, 16)
                            with sp.Fori(0, NCH // 2) as g:
                                for k in range(2):
                                    source_rows.load_index(sp, t["src_pad"], by_tile, index, tile_src, k, g, L)
                            sp.wait_ge(layer_loaded, L * 48 + 48)
                            sp.sem_inc(source_rows.sp_done, 1)

                        @block.gpsimd
                        def _(pool):
                            source_rows.gather(pool, h_rows, index, got, L)
                            pool.wait_ge(rows_stored, L * (16 * NCH) + 16 * NCH)
                            pool.sem_inc(pool_stepped, 1)
                            for a in range(NA):
                                pool.indirect_dma_start(agg[:, a, :], None, scan_rows,
                                                        bass.IndirectOffsetOnAxis(ap=end_row[:, a:a + 1], axis=0)
                                                        ).then_inc(ends_got, 16)
                            pool.wait_ge(ends_got, L * (16 * NA) + 16 * NA)
                            pool.sem_inc(source_rows.sp_done, 1)

                        @block.scalar
                        def _(act):
                            with act.Fori(0, NCH // 2) as g:
                                for k in range(2):
                                    c = L * NCH + g * 2 + k
                                    nc.scalar.activation(mm3, bc(keep_big[:, bass.ds(g * 2 + k, 1), :], [P, D, W1]),
                                                         ACT.Copy).then_inc(masks, 1)
                                    nc.scalar.activation(ms3, bc(keep[:, bass.ds(g * 2 + k, 1), :], [P, D, W1]),
                                                         ACT.Copy).then_inc(masks, 1)
                                    source_rows.wait_gathered(act, k, g, L)
                                    act.wait_ge(source_rows.picked, c + 3)
                                    nc.scalar.activation(in3[:, :, 1:W1], got[:, k, :, :].rearrange("p t f -> p f t"),
                                                         ACT.Copy).then_inc(source_rows.used[k], 1)
                                    act.wait_ge(scanned, c * 2 + 2)
                                    nc.scalar.activation(both[:, :, 0:D].rearrange("p t f -> p f t"), max3[:, :, 1:W1],
                                                         ACT.Copy).then_inc(rows_ready, 1)
                                    nc.scalar.activation(both[:, :, D:2 * D].rearrange("p t f -> p f t"), sum3[:, :, 1:W1],
                                                         ACT.Copy).then_inc(rows_ready, 1)
                                    act.wait_ge(rows_ready, c * 2 + 2)
                                    act.dma_start(rows_by_part[:, bass.ds((g * 2 + k) * TC, TC), :], both[:]
                                                  ).then_inc(rows_stored, 16)
                                    act.wait_ge(rows_stored, c * 16 + 16)

                        @block.vector
                        def _(dve):
                            v = nc.vector

                            def hots_of(i, k, g, a0, a1):
                                source_rows.make_hots(dve, nc, hots, tile_src, node_id, L * NCH + i, k, g, L, a0, a1)

                            def scan(i, k, g, which):
                                c = L * NCH + i
                                if which == 0:
                                    dve.wait_ge(masks, c * 2 + 2)
                                    dve.wait_ge(source_rows.used[k], L * (NCH // 2) + g + 2)
                                out3, out, mask, keeps, joins = ((max3, run_max, mask_max, ALU.min, ALU.max),
                                                                 (sum3, run_sum, mask_sum, ALU.mult, ALU.add))[which]
                                Chain(dve, schain, c * 2 + which)(v.tensor_copy(in3[:, :, 0:1], out3[:, :, TC:W1]))
                                v.tensor_tensor_scan(out[:], mask[:], turned[:], 0.0, keeps, joins).then_inc(scanned, 1)
                                dve.wait_ge(scanned, c * 2 + (which + 1))

                            def add_parts(i, k, g):
                                source_rows.add_parts(dve, nc, ps_pick, got, L * NCH + i, k, g, L, 2)

                            def step(i, k, g, g_next):
                                hots_of(i + 1, 1 - k, g_next, 0, 8)
                                add_parts(i, k, g)
                                hots_of(i + 1, 1 - k, g_next, 8, 14)
                                scan(i, k, g, 0)
                                hots_of(i + 1, 1 - k, g_next, 14, 19)
                                scan(i, k, g, 1)
                                hots_of(i + 1, 1 - k, g_next, 19, NA)

                            source_rows.split_rows(dve, nc, hl[:], parts, rest[:], L)
                            hots_of(0, 0, 0, 0, NA)
                            with dve.Fori(0, NCH // 2 - 1) as g:
                                step(g * 2, 0, g, g)
                                step(g * 2 + 1, 1, g, g + 1)
                            step(NCH - 2, 0, NCH // 2 - 1, NCH // 2 - 1)
                            add_parts(NCH - 1, 1, NCH // 2 - 1)
                            scan(NCH - 1, 1, NCH // 2 - 1, 0)
                            scan(NCH - 1, 1, NCH // 2 - 1, 1)
                            dve.sem_inc(source_rows.stepped, 1)

                        @block.tensor
                        def _(pe):
                            pe.wait_ge(source_rows.split, L * 4 + 4)
                            pe.sem_inc(source_rows.stepped, 1)
                            with pe.Fori(0, NCH // 2) as g:
                                for k in range(2):
                                    source_rows.pick(pe, nc, ps_pick, hots, parts, L * NCH + g * 2 + k, k, 2)

                with ExitStack() as ctx2:
                    sb, ps = tiles(ctx2, "sage_nodes")
                    y = sb("y", [NB, NA, D])
                    fix.big = y
                    scratch = sb("scratch", [NB, NA, D])
                    heldA = sb("heldA", [P, NA * NB])
                    heldB = sb("heldB", [P, NA * NB])
                    held = [heldA, heldB]
                    ps_turn = ps("ps_turn", [P, 2, 512])
                    ps_out = ps("ps_out", [P, 2, 512])
                    ps_carry = ps("ps_carry", [P, 2, 512])
                    with nc.Block() as block:

                        @block.sync
                        def _(sp):
                            sp.wait_ge(silu_out, L * 2 + 2)
                            sp.dma_start(nodes(h_rows[0:N, :]), hl[:].rearrange("b a d -> b (a d)")).then_inc(h_put2, 16)
                            sp.wait_ge(h_put2, L * 16 + 16)
                            sp.sem_inc(source_rows.sp_done, 1)

                        @block.vector
                        def _(dve):
                            v = nc.vector
                            per = 2 + Carry.LINKS + Norm.LINKS + 3
                            link = Chain(dve, nodechain, L * per)
                            dve.wait_ge(ends_got, L * (16 * NA) + 16 * NA)
                            link(v.tensor_copy(tails[:, 0:D].unsqueeze(2), max3[:, :, TC:W1]))
                            link(v.tensor_copy(tails[:, D:2 * D].unsqueeze(2), sum3[:, :, TC:W1]))
                            fix.dve(dve, nc, link, ps_carry, tails_t, carry_t, carry, carry_mask, agg, no_carry, L)
                            v.tensor_tensor(agg[:, :, 0:D], agg[:, :, 0:D], bc(has_in[:].unsqueeze(2), [NB, NA, D]),
                                            ALU.mult).then_inc(agg_ready, 1)
                            v.tensor_tensor(agg[:, :, D:2 * D], agg[:, :, D:2 * D],
                                            bc(in_share[:].unsqueeze(2), [NB, NA, D]), ALU.mult).then_inc(agg_ready, 1)
                            conv.dve(dve, nc, ps_out, vecs[:, 0, :], y, L)
                            norm.dve(dve, nc, link, y[:], scratch[:], L)
                            link(v.tensor_tensor(y[:], y[:], bc(vecs[:, 1, :].unsqueeze(1), [NB, NA, D]), ALU.mult))
                            link(v.tensor_tensor(y[:], y[:], bc(vecs[:, 2, :].unsqueeze(1), [NB, NA, D]), ALU.add))
                            link(v.tensor_tensor(y[:], y[:], res[:], ALU.add))
                            dve.sem_inc(silu_in, 1)
                            assert link.n == per, (link.n, per)

                        @block.scalar
                        def _(act):
                            conv.act(act, nc, ps_turn, held, L)
                            norm.act(act, nc, L)
                            act.wait_ge(silu_in, L + 1)
                            nc.scalar.activation(hl[:], y[:], ACT.Silu).then_inc(silu_out, 1)
                            nc.scalar.activation(res[:], y[:], ACT.Silu).then_inc(silu_out, 1)

                        @block.tensor
                        def _(pe):
                            fix.pe(pe, nc, ps_carry, tails, carry_t, carry, carry_from, ident, nodechain,
                                   L * (2 + Carry.LINKS + Norm.LINKS + 3) + 2, L)
                            pe.wait_ge(agg_ready, L * 2 + 2)
                            conv.pe(pe, nc, ps_turn, ps_out, held, ident, L)

        HID = 4 * D
        with ExitStack() as ctx:
            sb, ps = tiles(ctx, "mlp")
            z = sb("z", [NB, NA, HID])
            scratch = sb("scratch", [NB, NA, HID])
            y = sb("y", [NB, NA, D])
            heldA = sb("heldA", [P, NA * NB])
            heldB = sb("heldB", [P, NA * NB])
            w_in = sb("w_in", [D, HID])
            w_out = sb("w_out", [P, 2, D])
            b_in = sb("b_in", [NB, 3, HID])
            b_out = sb("b_out", [NB, D])
            ps_turn = ps("ps_turn", [P, 2, 512])
            ps_out = ps("ps_out", [P, 2, 512])
            held = [heldA, heldB]
            mlp_loaded, mchain, msilu_in, msilu_out, z_ready, x3_ready, x3_put = (
                sem("mlp_" + n) for n in ("loaded", "chain", "silu_in", "silu_out", "z_ready", "x3_ready", "x3_put"))
            mlp1 = Linear(products, [hl[:]], [w_in[:]], HID)
            mlp2 = Linear(products, [z[:, :, 0:P], z[:, :, P:HID]], [w_out[:, 0, :], w_out[:, 1, :]], D)
            norm_h, norm2 = Norm(norms, stat), Norm(norms, stat)
            with nc.Block() as block:

                @block.sync
                def _(sp):
                    sp.dma_start(w_in[:], t["w_mlp1"]).then_inc(mlp_loaded, 16)
                    sp.dma_start(w_out[:], t["w_mlp2"].rearrange("(s k) f -> k s f", s=2)).then_inc(mlp_loaded, 16)
                    sp.dma_start(b_in[:], bc(t["mlp_vecs"].unsqueeze(0), [NB, 3, HID])).then_inc(mlp_loaded, 16)
                    sp.dma_start(b_out[:], bc(t["b_mlp2"], [NB, D])).then_inc(mlp_loaded, 16)
                    sp.wait_ge(x3_ready, 1)
                    sp.dma_start(nodes(h_rows[0:N, :]), h[:].rearrange("b a d -> b (a d)")).then_inc(x3_put, 16)
                    sp.wait_ge(x3_put, 16)

                @block.vector
                def _(dve):
                    v = nc.vector
                    link = Chain(dve, mchain)
                    dve.wait_ge(mlp_loaded, 64)
                    mlp1.dve(dve, nc, ps_out, b_in[:, 0, :], z)
                    dve.sem_inc(msilu_in, 1)
                    dve.wait_ge(msilu_out, 1)
                    norm_h.dve(dve, nc, link, z[:], scratch[:])
                    link(v.tensor_tensor(z[:], z[:], bc(b_in[:, 1, :].unsqueeze(1), [NB, NA, HID]), ALU.mult))
                    v.tensor_tensor(z[:], z[:], bc(b_in[:, 2, :].unsqueeze(1), [NB, NA, HID]), ALU.add).then_inc(z_ready, 1)
                    mlp2.dve(dve, nc, ps_out, b_out, y)
                    link(v.tensor_tensor(h[:], h[:], y[:], ALU.add))
                    norm2.dve(dve, nc, link, h[:], scratch[:, :, 0:D])
                    dve.sem_inc(x3_ready, 1)

                @block.scalar
                def _(act):
                    mlp1.act(act, nc, ps_turn, held)
                    act.wait_ge(msilu_in, 1)
                    nc.scalar.activation(z[:], z[:], ACT.Silu).then_inc(msilu_out, 1)
                    norm_h.act(act, nc)
                    mlp2.act(act, nc, ps_turn, held)
                    norm2.act(act, nc)

                @block.tensor
                def _(pe):
                    pe.wait_ge(mlp_loaded, 64)
                    mlp1.pe(pe, nc, ps_turn, ps_out, held, ident)
                    pe.wait_ge(z_ready, 1)
                    mlp2.pe(pe, nc, ps_turn, ps_out, held, ident)

        with ExitStack() as ctx:
            sb, ps = tiles(ctx, "last")
            agg = sb("agg", [NB, NA, 2 * D])
            run_sum = sb("run_sum", [P, D * W1])
            sum3 = run_sum[:].rearrange("p (f t) -> p f t", t=W1)
            (e_zeroed, e_masks, e_scanned, e_rows, e_stored, e_chain, e_ends, e_w, e_made, e_turned) = (
                sem("edge_" + n) for n in ("zeroed", "masks", "scanned", "rows", "stored", "chain", "ends", "w",
                                           "made", "turned"))
            e_loaded = [sem(f"edge_loaded_k{k}") for k in range(2)]
            L = LAYERS
            sum_rows = nc.dram_tensor("sum_rows", [EP, D], F32).ap()
            with ExitStack() as ctx2:
                sb, ps = tiles(ctx2, "last_edges")
                index = sb("index", [P, 2, TP], I32)
                tile_src = sb("tile_src", [P, 2, XT, P], F16)
                hots = sb("hots", [NB, RING, XT * P], BF16)
                parts = sb("parts", [NB, NA, 3, D], BF16)
                rest = sb("rest", [NB, NA, D])
                ps_pick = ps("ps_pick", [P, 1, XB, 512])
                got = sb("got", [P, 2, TC, D])
                msg = sb("msg", [P, TC, D])
                turned = sb("turned", [P, D * W1])
                mask_sum = sb("mask_sum", [P, D * W1], BF16)
                both = sb("both", [P, TC, D])
                attr = sb("attr", [K10 + 1, 2, TC, P])
                w_edge = sb("w_edge", [K10 + 1, D])
                ps_edge = ps("ps_edge", [P, 4, 512])
                in3, ms3 = (a[:].rearrange("p (f t) -> p f t", t=W1) for a in (turned, mask_sum))
                ps_flat = ps_edge[:].rearrange("p b x -> p (b x)")[:, 0:TC * D].rearrange("p (t f) -> p t f", f=D)
                rows_by_part = sum_rows.rearrange("(p t) d -> p t d", t=T)

                with nc.Block() as block:

                    @block.sync
                    def _(sp):
                        sp.sem_inc(e_made, 2)
                        sp.wait_ge(e_zeroed, 2)
                        sp.dma_start(w_edge[:], t["w_edge"]).then_inc(e_w, 16)
                        with sp.Fori(0, NCH // 2) as g:
                            for k in range(2):
                                source_rows.load_index(sp, t["src_pad"], by_tile, index, tile_src, k, g, L)
                                sp.wait_ge(e_made, g * 2 + (k + 1))
                                sp.dma_start(attr[0:K10, k, :, :], t["edge10"][:, bass.ds((g * 2 + k) * TC, TC), :]
                                             ).then_inc(e_loaded[k], 16)

                    @block.gpsimd
                    def _(pool):
                        source_rows.gather(pool, h_rows, index, got, L)
                        pool.wait_ge(e_stored, 16 * NCH)
                        for a in range(NA):
                            pool.indirect_dma_start(agg[:, a, D:2 * D], None, sum_rows,
                                                    bass.IndirectOffsetOnAxis(ap=end_row[:, a:a + 1], axis=0)
                                                    ).then_inc(e_ends, 16)
                        pool.wait_ge(e_ends, 16 * NA)

                    @block.scalar
                    def _(act):
                        with act.Fori(0, NCH // 2) as g:
                            for k in range(2):
                                c = g * 2 + k
                                nc.scalar.activation(ms3, bc(keep[:, bass.ds(c, 1), :], [P, D, W1]),
                                                     ACT.Copy).then_inc(e_masks, 1)
                                act.wait_ge(source_rows.used[k], g + (L * (NCH // 2) + 2))
                                nc.scalar.activation(in3[:, :, 1:W1], msg[:].rearrange("p t f -> p f t"),
                                                     ACT.Relu).then_inc(e_turned, 1)
                                act.wait_ge(e_scanned, c + 1)
                                nc.scalar.activation(both[:].rearrange("p t f -> p f t"), sum3[:, :, 1:W1],
                                                     ACT.Copy).then_inc(e_rows, 1)
                                act.wait_ge(e_rows, c + 1)
                                act.dma_start(rows_by_part[:, bass.ds(c * TC, TC), :], both[:]).then_inc(e_stored, 16)
                                act.wait_ge(e_stored, c * 16 + 16)

                    @block.vector
                    def _(dve):
                        v = nc.vector
                        v.memset(attr[:], 1.0).then_inc(e_zeroed, 1)
                        v.memset(run_sum[:], 0.0).then_inc(e_zeroed, 1)
                        dve.wait_ge(e_zeroed, 2)

                        def hots_of(i, k, g, a0, a1):
                            source_rows.make_hots(dve, nc, hots, tile_src, node_id, i + L * NCH, k, g, L, a0, a1)

                        def add_parts(i, k, g):
                            source_rows.add_parts(dve, nc, ps_pick, got, i + L * NCH, k, g, L, 1)

                        def message(i, k, g):
                            source_rows.wait_gathered(dve, k, g, L)
                            dve.wait_ge(source_rows.picked, i + (L * NCH + 3))
                            dve.wait_ge(e_made, i + 3)
                            v.tensor_tensor(msg[:], got[:, k, :, :], ps_flat, ALU.add).then_inc(source_rows.used[k], 1)

                        def scan(i):
                            dve.wait_ge(e_masks, i + 1)
                            dve.wait_ge(e_turned, i + 1)
                            Chain(dve, e_chain, i)(v.tensor_copy(in3[:, :, 0:1], sum3[:, :, TC:W1]))
                            v.tensor_tensor_scan(run_sum[:], mask_sum[:], turned[:], 0.0, ALU.mult,
                                                 ALU.add).then_inc(e_scanned, 1)
                            dve.wait_ge(e_scanned, i + 1)

                        def step(i, k, g, g_next):
                            hots_of(i + 1, 1 - k, g_next, 0, 5)
                            add_parts(i, k, g)
                            hots_of(i + 1, 1 - k, g_next, 5, 10)
                            message(i, k, g)
                            hots_of(i + 1, 1 - k, g_next, 10, 18)
                            scan(i)
                            hots_of(i + 1, 1 - k, g_next, 18, NA)

                        source_rows.split_rows(dve, nc, h[:], parts, rest[:], L)
                        hots_of(0, 0, 0, 0, NA)
                        with dve.Fori(0, NCH // 2 - 1) as g:
                            step(g * 2, 0, g, g)
                            step(g * 2 + 1, 1, g, g + 1)
                        step(NCH - 2, 0, NCH // 2 - 1, NCH // 2 - 1)
                        add_parts(NCH - 1, 1, NCH // 2 - 1)
                        message(NCH - 1, 1, NCH // 2 - 1)
                        scan(NCH - 1)

                    @block.tensor
                    def _(pe):
                        pe.wait_ge(e_w, 16)
                        pe.wait_ge(source_rows.split, L * 4 + 4)
                        with pe.Fori(0, NCH // 2) as g:
                            for k in range(2):
                                c = g * 2 + k
                                source_rows.pick(pe, nc, ps_pick, hots, parts, c + L * NCH, k, 1)
                                pe.wait_ge(e_loaded[k], g * 16 + 16)
                                pe.wait_ge(source_rows.used[1 - k], g + (L * (NCH // 2) + 1 + k))
                                for j in range(TC):
                                    ins = nc.tensor.matmul(ps_edge[:, j // 8, (j % 8) * D:(j % 8 + 1) * D],
                                                           attr[:, k, j, :], w_edge[:], start=True, stop=True)
                                ins.then_inc(e_made, 1)

            with ExitStack() as ctx2:
                sb, ps = tiles(ctx2, "last_nodes")
                y = sb("y", [NB, NA, D])
                y2 = sb("y2", [NB, NA, D])
                scratch = sb("scratch", [NB, NA, D])
                heldA = sb("heldA", [P, NA * NB])
                tails = sb("tails", [P, P])
                tails_t = sb("tails_t", [P, P])
                carry_t = sb("carry_t", [P, P])
                carry = sb("carry", [P, P])
                w1 = sb("w1", [D, D])
                w2 = sb("w2", [D, D])
                vec = sb("vec", [NB, 4, D])
                ones = sb("ones", [NB, NB])
                bn = sb("bn", [NB, 4, D])
                ps_turn = ps("ps_turn", [P, 2, 512])
                ps_out = ps("ps_out", [P, 2, 512])
                ps_carry = ps("ps_carry", [P, 2, 512])
                ps_bn = ps("ps_bn", [P, 2, 512])
                held = [heldA]
                (f_loaded, fchain, f_in, f_hid, f_out, f_sum, f_sq, f_root, f_root_out, f_done, f_put) = (
                    sem("last_" + n) for n in ("loaded", "chain", "in", "hid", "out", "sum", "sq", "root", "root_out",
                                               "done", "put"))
                fix = Carry(sem, "edge", 1)
                l1 = Linear(products, [y2[:]], [w1[:]], D)
                l2 = Linear(products, [y[:]], [w2[:]], D)
                norm3 = Norm(norms, stat)
                with nc.Block() as block:

                    @block.sync
                    def _(sp):
                        sp.dma_start(w1[:], t["w_last1"]).then_inc(f_loaded, 16)
                        sp.dma_start(w2[:], t["w_last2"]).then_inc(f_loaded, 16)
                        sp.dma_start(vec[:], bc(t["last_vecs"].unsqueeze(0), [NB, 4, D])).then_inc(f_loaded, 16)
                        sp.wait_ge(f_done, 1)
                        sp.dma_start(nodes(out), h[:].rearrange("b a d -> b (a d)")).then_inc(f_put, 16)
                        sp.wait_ge(f_put, 16)

                    @block.vector
                    def _(dve):
                        v = nc.vector
                        link = Chain(dve, fchain)
                        link(v.memset(tails[:, 0:D], 0.0))
                        link(v.tensor_copy(tails[:, D:2 * D].unsqueeze(2), sum3[:, :, TC:W1]))
                        fix.dve(dve, nc, link, ps_carry, tails_t, carry_t, carry, carry_mask, agg, None, 0)
                        link(v.tensor_tensor(y2[:], agg[:, :, D:2 * D], bc(has_in[:].unsqueeze(2), [NB, NA, D]), ALU.mult))
                        v.tensor_tensor(y2[:], y2[:], h[:], ALU.add).then_inc(f_in, 1)
                        dve.wait_ge(f_loaded, 48)
                        l1.dve(dve, nc, ps_out, vec[:, 0, :], y)
                        v.tensor_scalar(y[:], y[:], 0.0, None, ALU.max).then_inc(f_hid, 1)
                        l2.dve(dve, nc, ps_out, vec[:, 1, :], y2)
                        link(v.memset(ones[:], 1.0))
                        v.tensor_scalar(y2[:], y2[:], 0.0, None, ALU.max).then_inc(f_out, 1)
                        dve.wait_ge(f_sum, 1)
                        link(v.tensor_scalar(bn[:, 0, :], ps_bn[0:NB, 0, 0:D], 1.0 / N, None, ALU.mult))
                        link(v.tensor_tensor(y2[:], y2[:], bc(bn[:, 0, :].unsqueeze(1), [NB, NA, D]), ALU.subtract))
                        v.tensor_tensor(scratch[:], y2[:], y2[:], ALU.mult).then_inc(f_out, 1)
                        dve.wait_ge(f_sum, 2)
                        v.tensor_scalar(bn[:, 1, :], ps_bn[0:NB, 1, 0:D], 1.0 / N, EPS, ALU.mult, ALU.add).then_inc(f_root, 1)
                        dve.wait_ge(f_root_out, 1)
                        link(v.reciprocal(bn[:, 3, :], bn[:, 2, :]))
                        link(v.tensor_tensor(bn[:, 3, :], bn[:, 3, :], vec[:, 2, :], ALU.mult))
                        link(v.tensor_tensor(y2[:], y2[:], bc(bn[:, 3, :].unsqueeze(1), [NB, NA, D]), ALU.mult))
                        link(v.tensor_tensor(y2[:], y2[:], bc(vec[:, 3, :].unsqueeze(1), [NB, NA, D]), ALU.add))
                        link(v.tensor_tensor(h[:], h[:], y2[:], ALU.add))
                        norm3.dve(dve, nc, link, h[:], scratch[:])
                        dve.sem_inc(f_done, 1)

                    @block.scalar
                    def _(act):
                        l1.act(act, nc, ps_turn, held)
                        l2.act(act, nc, ps_turn, held)
                        act.wait_ge(f_root, 1)
                        nc.scalar.activation(bn[:, 2, :], bn[:, 1, :], ACT.Sqrt).then_inc(f_root_out, 1)
                        norm3.act(act, nc)

                    @block.tensor
                    def _(pe):
                        fix.pe(pe, nc, ps_carry, tails, carry_t, carry, carry_from, ident, fchain, 2, 0)
                        pe.wait_ge(f_loaded, 48)
                        pe.wait_ge(f_in, 1)
                        l1.pe(pe, nc, ps_turn, ps_out, held, ident)
                        pe.wait_ge(f_hid, 1)
                        l2.pe(pe, nc, ps_turn, ps_out, held, ident)
                        for i, tile in enumerate((y2, scratch)):
                            pe.wait_ge(f_out, i + 1)
                            for a in range(NA):
                                ins = nc.tensor.matmul(ps_bn[0:NB, i, 0:D], ones[:], tile[:, a, :], start=(a == 0),
                                                       stop=(a == NA - 1))
                            ins.then_inc(f_sum, 1)


def kernel(**inputs):
    import numpy as np
    import concourse.bacc as bacc
    from concourse.bass_utils import run_bass_kernel_spmd

    a = {k: np.asarray(v) for k, v in inputs.items()}

    def lay(ap):
        return np.ascontiguousarray(ap)

    def edges(v, fill):
        padded = np.full((EP,) + v.shape[1:], fill, v.dtype)
        padded[:E] = v
        return padded

    attr = edges(a["edge_attr_10"], 0)
    w1 = a["L1_gnn_W1"]
    arrays = {
        "x": a["x"], "node_vec": a["node_vec"],
        "src_pad": edges(a["src"], N).reshape(P, T), "dst_pad": edges(a["dst"], N).reshape(P, T),
        "src_turned": edges(a["src"], N).reshape(P, T).T.reshape(P, T),
        "edge64": edges(a["edge_attr_64"], 0), "edge10": attr.reshape(P, T, K10).transpose(2, 1, 0),
        "w_curv": a["L0_gnn_W_curv"].reshape(1, D), "b_curv": a["L0_gnn_b_curv"].reshape(1, D),
        "w_lin0": a["L0_gnn_W_lin"].T, "b_lin0": a["L0_gnn_b_lin"].reshape(1, D),
        "w_l1x": w1[0:D], "w_l1v": w1[D:2 * D], "w_l1u": w1[2 * D:3 * D], "b_l1h": a["L1_gnn_b1"].reshape(1, D),
        "w_l1o": a["L1_gnn_W2"], "b_l1o": a["L1_gnn_b2"].reshape(1, D), "u0": a["L1_gnn_u"][0].reshape(D, 1),
        "w_adapt": a["L2_gnn_adapter_w"].T, "b_adapt": a["L2_gnn_adapter_b"].reshape(1, D),
        "w_agg": a["L2_gnn_conv_wl"].transpose(0, 2, 1).reshape(-1, D), "w_self": a["L2_gnn_conv_wr"].transpose(0, 2, 1).reshape(-1, D),
        "conv_vecs": np.stack([a["L2_gnn_conv_bl"], a["L2_gnn_ln_g"], a["L2_gnn_ln_b"]], 1),
        "w_mlp1": a["L2_gnn_mlp_w1"].T, "w_mlp2": a["L2_gnn_mlp_w2"].T, "b_mlp2": a["L2_gnn_mlp_b2"].reshape(1, D),
        "mlp_vecs": np.stack([a["L2_gnn_mlp_b1"], a["L2_gnn_mlp_ln_g"], a["L2_gnn_mlp_ln_b"]]),
        "w_edge": np.concatenate([a["L3_gnn_W_edge"], a["L3_gnn_b_edge"][None]]),
        "w_last1": a["L3_gnn_W1"], "w_last2": a["L3_gnn_W2"],
        "last_vecs": np.stack([a["L3_gnn_b1"], a["L3_gnn_b2"], a["L3_gnn_bn_gamma"], a["L3_gnn_bn_beta"]]),
    }
    arrays = {"in_" + k: lay(v) for k, v in arrays.items()}
    nc = bacc.Bacc("TRN2", target_bir_lowering=False, num_devices=1)
    t = {k[3:]: nc.dram_tensor(k, v.shape, mybir.dt.from_np(v.dtype), kind="ExternalInput").ap() for k, v in arrays.items()}
    out = nc.dram_tensor("out_0", (N, D), F32, kind="ExternalOutput").ap()
    program(nc, t, out)
    return run_bass_kernel_spmd(nc, [arrays], core_ids=[0]).results[0]["out_0"]
```

```python
from contextlib import ExitStack

import concourse.bass as bass
from concourse import mybir

F32 = mybir.dt.float32
BF16 = mybir.dt.bfloat16
F16 = mybir.dt.float16
I32 = mybir.dt.int32
ALU = mybir.AluOpType
ACT = mybir.ActivationFunctionType
AX = mybir.AxisListType.X

P = 128
D = 64
N = 3125
NB = 125
NA = N // NB
E = 103125
TC = 27
NCH = 30
T = TC * NCH
EP = P * T
W1 = TC + 1
K10 = 10
NT = 9
TROWS = -(-(N + 1 + P) // P) * P
RW = 2 * D + 1
GR = 3
NG = TC // GR
PICKED = 8
PICKED_LAST = 6
PAIR = 2
assert PICKED % PAIR == PICKED_LAST % PAIR == 0
RING = 10
CENTRE = N // 2
LAYERS = 5
EPS = 1e-5
BIG = 3.0e38
ROUND = 12582912.0
TG = 4
NGT = (NA + TG - 1) // TG
assert CENTRE <= 2048 and 2 * NA % RING == 0 and EP >= E and TC % GR == 0 and TC % NT == 0


def bc(ap, shape):
    return ap.to_broadcast(list(shape))


class Chain:

    def __init__(self, eng, sem, base=0):
        self.eng, self.sem, self.base, self.n = eng, sem, base, 0

    def __call__(self, ins):
        self.n += 1
        ins.then_inc(self.sem, 1)
        self.eng.wait_ge(self.sem, self.base + self.n)


def pieces(total, step):
    return [(i, min(step, total - i)) for i in range(0, total, step)]


class Linear:

    def __init__(self, shared, sources, weights, width, repeats=1):
        self.turned, self.held, self.made, self.added, self.stepped = shared["sems"]
        self.sources, self.weights, self.width = sources, weights, width
        self.nturn = NGT * len(sources)
        self.step = 512 // width if width > P else TG
        self.groups = pieces(NA, self.step)
        self.turn0, self.made0 = shared["count"]
        shared["count"] = (self.turn0 + repeats * self.nturn, self.made0 + repeats * len(self.groups))

    def pe(self, pe, nc, ps_turn, ps_out, held_tiles, ident, L=0):
        i = 0
        for src in self.sources:
            k = src.shape[2]
            for a0, n in pieces(NA, TG):
                if i >= 2:
                    pe.wait_ge(self.held, L * self.nturn + self.turn0 + i - 1)
                    pe.sem_inc(self.stepped, 1)
                for j in range(n):
                    ins = nc.tensor.transpose(ps_turn[0:k, i % 2, j * NB:(j + 1) * NB], src[:, a0 + j, :],
                                              ident[0:NB, 0:NB])
                ins.then_inc(self.turned, 1)
                i += 1
        pe.wait_ge(self.held, L * self.nturn + self.turn0 + self.nturn)
        for i, (a0, n) in enumerate(self.groups):
            if i >= 2:
                pe.wait_ge(self.added, L * len(self.groups) + self.made0 + i - 1)
            for j in range(n):
                for s, (src, w) in enumerate(zip(self.sources, self.weights)):
                    k = src.shape[2]
                    ins = nc.tensor.matmul(ps_out[0:NB, i % 2, j * self.width:(j + 1) * self.width],
                                           held_tiles[s][0:k, (a0 + j) * NB:(a0 + j + 1) * NB], w,
                                           start=(s == 0), stop=(s == len(self.sources) - 1))
            ins.then_inc(self.made, 1)

    def act(self, act, nc, ps_turn, held_tiles, L=0):
        i = 0
        for s, src in enumerate(self.sources):
            k = src.shape[2]
            for a0, n in pieces(NA, TG):
                act.wait_ge(self.turned, L * self.nturn + self.turn0 + i + 1)
                nc.scalar.activation(held_tiles[s][0:k, a0 * NB:(a0 + n) * NB], ps_turn[0:k, i % 2, 0:n * NB],
                                     ACT.Copy).then_inc(self.held, 1)
                i += 1

    def dve(self, dve, nc, ps_out, bias, out, L=0):
        for i, (a0, n) in enumerate(self.groups):
            dve.wait_ge(self.made, L * len(self.groups) + self.made0 + i + 1)
            nc.vector.tensor_tensor(out[:, a0:a0 + n, :],
                                    ps_out[0:NB, i % 2, 0:n * self.width].rearrange("p (a f) -> p a f", f=self.width),
                                    bc(bias[:, 0:self.width].unsqueeze(1), [NB, n, self.width]),
                                    ALU.add).then_inc(self.added, 1)
        dve.wait_ge(self.added, L * len(self.groups) + self.made0 + len(self.groups))


class Norm:

    LINKS = 7

    def __init__(self, shared, stat, repeats=1):
        self.var_ready, self.root_ready = shared["sems"]
        self.start, self.stat = shared["count"], stat
        shared["count"] += repeats

    def centre(self, nc, link, y, at=slice(0, NA)):
        mean, y = self.stat[:, 0, at], y[:, at, :]
        link(nc.vector.tensor_reduce(mean, y, AX, ALU.add))
        link(nc.vector.tensor_scalar(mean, mean, 1.0 / y.shape[2], None, ALU.mult))
        link(nc.vector.tensor_tensor(y, y, bc(mean.unsqueeze(2), list(y.shape)), ALU.subtract))

    def variance(self, nc, link, y, scratch, at=slice(0, NA)):
        var, y, scratch = self.stat[:, 1, at], y[:, at, :], scratch[:, at, :]
        link(nc.vector.tensor_tensor(scratch, y, y, ALU.mult))
        link(nc.vector.tensor_reduce(var, scratch, AX, ALU.add))
        nc.vector.tensor_scalar(var, var, 1.0 / y.shape[2], EPS, ALU.mult, ALU.add).then_inc(self.var_ready, 1)

    def scale(self, dve, nc, link, y, i=0, at=slice(0, NA)):
        root, inv, y = self.stat[:, 2, at], self.stat[:, 3, at], y[:, at, :]
        dve.wait_ge(self.root_ready, i + (self.start + 1))
        link(nc.vector.reciprocal(inv, root))
        link(nc.vector.tensor_tensor(y, y, bc(inv.unsqueeze(2), list(y.shape)), ALU.mult))

    def dve(self, dve, nc, link, y, scratch):
        self.centre(nc, link, y)
        self.variance(nc, link, y, scratch)
        self.scale(dve, nc, link, y)

    def act(self, act, nc, i=0, at=slice(0, NA)):
        act.wait_ge(self.var_ready, i + (self.start + 1))
        nc.scalar.activation(self.stat[:, 2, at], self.stat[:, 1, at], ACT.Sqrt).then_inc(self.root_ready, 1)


class Gathers:

    def __init__(self, sem, name, stepped):
        self.xt, self.tp = PICKED, TC - PICKED
        self.gathered = [sem(f"{name}_gathered{k}") for k in range(2)]
        self.index_loaded = [sem(f"{name}_index_loaded{k}") for k in range(2)]
        self.used = [sem(f"{name}_used{k}") for k in range(2)]
        self.hot_made = sem(name + "_hot_made")
        self.hot_used = sem(name + "_hot_used")
        self.picked = sem(name + "_picked")
        self.split = sem(name + "_split")
        self.stepped = stepped

    def give_tokens(self, sp):
        for k in range(2):
            sp.sem_inc(self.used[k], 1)
        sp.sem_inc(self.hot_used, RING)
        sp.sem_inc(self.picked, 2)

    def load_index(self, sp, src, by_tile, index, tile_src, k, g, L):
        at = (g * 2 + k) * TC
        sp.dma_start(index[:, k, :], src[:, bass.ds(at, TC - PICKED_LAST)]).then_inc(self.index_loaded[k], 16)
        sp.dma_start(tile_src[:, k, :, :], bc(by_tile[bass.ds(at + (TC - PICKED), PICKED), :].unsqueeze(0), [P, PICKED, P])
                     ).then_inc(self.index_loaded[k], 16)

    def load_first(self, sp, src, by_tile, index, tile_src, L):
        for k in range(2):
            self.load_index(sp, src, by_tile, index, tile_src, k, 0, L)

    def gather(self, pool, rows, index, got, L):
        with pool.Fori(0, NCH // 2) as g:
            for k in range(2):
                pool.wait_ge(self.index_loaded[k], L * (16 * NCH) + g * 32 + 32)
                pool.wait_ge(self.used[k], L * (NCH // 2) + g + 1)
                pool.sem_inc(self.stepped, 1)
                for i in range(self.tp):
                    pool.indirect_dma_start(got[:, k, i, :], None, rows,
                                            bass.IndirectOffsetOnAxis(ap=index[:, k, i:i + 1], axis=0)
                                            ).then_inc(self.gathered[k], 16)

    def wait_gathered(self, eng, k, g, L):
        eng.wait_ge(self.gathered[k], L * (16 * (TC - PICKED) * NCH // 2) + g * (16 * self.tp) + 16 * self.tp)

    def split_rows(self, dve, nc, x, parts, rest, L):
        v = nc.vector
        link = Chain(dve, self.split, L * 4)
        link(v.tensor_copy(parts[:, :, 0, :], x))
        link(v.tensor_tensor(rest, x, parts[:, :, 0, :], ALU.subtract))
        link(v.tensor_copy(parts[:, :, 1, :], rest))
        link(v.tensor_tensor(parts[:, :, 2, :], rest, parts[:, :, 1, :], ALU.subtract))

    def make_hots(self, dve, nc, hots, tile_src, node_id, c, k, g, L, a0, a1):
        if a0 == 0:
            dve.wait_ge(self.index_loaded[k], L * (16 * NCH) + g * 32 + 32)
        for a in range(a0, a1):
            dve.wait_ge(self.hot_used, c * NA + (a + 1))
            nc.vector.tensor_scalar(hots[:, (k * NA + a) % RING, :],
                                    tile_src[0:NB, k, PICKED - self.xt:PICKED, :].rearrange("b t e -> b (t e)"),
                                    node_id[:, a:a + 1], None, ALU.is_equal).then_inc(self.hot_made, 1)

    def pick(self, pe, nc, ps_pick, hots, parts, c, k, buffers):
        pe.wait_ge(self.picked, c + (3 - buffers))
        for a in range(NA):
            pe.wait_ge(self.hot_made, c * NA + (a + 1))
            for j in range(self.xt):
                ins = nc.tensor.matmul(ps_pick[:, k % buffers, j // PAIR, j % PAIR * 3 * D:(j % PAIR + 1) * 3 * D],
                                       hots[:, (k * NA + a) % RING, j * P:(j + 1) * P],
                                       parts[:, a, :, :].rearrange("b s f -> b (s f)"),
                                       start=(a == 0 and j % PAIR == 0), stop=(a == NA - 1), skip_group_check=True)
            ins.then_inc(self.hot_used, 1)

    def add_parts(self, dve, nc, ps_pick, got, c, k, g, L, buffers):
        dve.wait_ge(self.hot_used, c * NA + (NA + RING))
        dve.wait_ge(self.used[k], L * (NCH // 2) + g + 1)
        nc.vector.tensor_reduce(got[:, k, self.tp:TC, :].rearrange("p (b t) f -> p b t f", t=PAIR),
                                ps_pick[:, k % buffers, :, 0:PAIR * 3 * D].rearrange("p b (t s f) -> p b t f s", s=3, f=D),
                                AX, ALU.add).then_inc(self.picked, 1)


class Carry:

    READS = 2

    def __init__(self, sem, name, stepped):
        self.tails_ready = sem(name + "_tails_ready")
        self.turned, self.scanned = sem(name + "_tails_turned"), sem(name + "_carry_scanned")
        self.stepped = stepped
        self.back, self.held = sem(name + "_carry_back"), sem(name + "_carry_held")
        self.brought, self.taken = sem(name + "_carry_brought"), sem(name + "_carry_taken")

    def turn(self, pe, nc, ps_carry, tails, carry_t, ident, L):
        pe.wait_ge(self.tails_ready, L * 2 + 2)
        pe.sem_inc(self.stepped, 1)
        nc.tensor.transpose(ps_carry[:, 0, 0:P], tails[:], ident[:]).then_inc(self.turned, 1)

    def turn_back(self, pe, nc, ps_carry, carry_t, ident, L):
        pe.wait_ge(self.scanned, L * 2 + 2)
        pe.sem_inc(self.stepped, 1)
        nc.tensor.transpose(ps_carry[:, 1, 0:P], carry_t[:], ident[:]).then_inc(self.back, 1)
        pe.wait_ge(self.held, L * 2 + 2)

    def bring(self, pe, nc, ps_carry, carry, carry_from, i, L):
        a0, n = pieces(NA, TG)[i]
        if i >= 2:
            pe.wait_ge(self.taken, L * (self.READS * NGT) + self.READS * (i - 1))
        for j in range(n):
            ins = nc.tensor.matmul(ps_carry[0:NB, i % 2, j * P:(j + 1) * P], carry_from[:, a0 + j, :], carry[:],
                                   start=True, stop=True)
        ins.then_inc(self.brought, 1)

    def scan(self, dve, nc, ps_carry, tails_t, carry_t, carry, carry_mask, L):
        v = nc.vector
        dve.wait_ge(self.turned, L + 1)
        v.tensor_copy(tails_t[:], ps_carry[:, 0, 0:P]).then_inc(self.held, 1)
        dve.wait_ge(self.held, L * 2 + 1)
        v.tensor_tensor_scan(carry_t[0:D, :], carry_mask[0:D, :], tails_t[0:D, :], 0.0, ALU.min,
                             ALU.max).then_inc(self.scanned, 1)
        v.tensor_tensor_scan(carry_t[D:P, :], carry_mask[D:P, :], tails_t[D:P, :], 0.0, ALU.mult,
                             ALU.add).then_inc(self.scanned, 1)
        dve.wait_ge(self.back, L + 1)
        v.tensor_copy(carry[:], ps_carry[:, 1, 0:P]).then_inc(self.held, 1)

    def add(self, dve, nc, ps_carry, agg, big, no_carry, i, L):
        v = nc.vector
        a0, n = pieces(NA, TG)[i]
        dve.wait_ge(self.brought, L * NGT + i + 1)
        got = ps_carry[0:NB, i % 2, 0:n * P].rearrange("p (a f) -> p a f", f=P)
        at = slice(a0, a0 + n)
        v.tensor_tensor(agg[:, at, D:P], agg[:, at, D:P], got[:, :, D:P], ALU.add
                        ).then_inc(self.taken, 1 if big is not None else 2)
        if big is not None:
            v.tensor_tensor(big[:, at, :], got[:, :, 0:D], bc(no_carry[:, at].unsqueeze(2), [NB, n, D]),
                            ALU.add).then_inc(self.taken, 1)
        dve.wait_ge(self.taken, L * (self.READS * NGT) + self.READS * (i + 1))


def program(nc, t, out):
    top = ExitStack()

    def sem(name):
        return top.enter_context(nc.semaphore(name))

    def tiles(ctx, stage):
        def sb(name, shape, dt=F32):
            return ctx.enter_context(nc.sbuf_tensor(f"{stage}_{name}", list(shape), dt))

        def ps(name, shape, dt=F32):
            return ctx.enter_context(nc.psum_tensor(f"{stage}_{name}", list(shape), dt))
        return sb, ps

    def nodes(ap):
        return ap.rearrange("(b a) d -> b (a d)", a=NA)

    xc_rows = nc.dram_tensor("xc_rows", [N + 1, D + 1], F32).ap()
    first_rows = nc.dram_tensor("first_rows", [EP + NB, D + 1], F32).ap()
    tables = [nc.dram_tensor(f"table{i}", [TROWS, RW], F32).ap() for i in range(NT)]
    scan_rows = nc.dram_tensor("scan_rows", [EP, 2 * D], F32).ap()
    h_rows = nc.dram_tensor("h_rows", [N + 1, D], F32).ap()
    by_tile = nc.dram_tensor("by_tile", [T, P], F16).ap()

    with top:
        sb, _ = tiles(top, "all")
        sb_top = sb
        ident = sb("ident", [P, P])
        later = sb("later", [P, P])
        earlier = sb("earlier", [P, P])
        lane = sb("lane", [P, 1])
        node_id = sb("node_id", [NB, NA])
        src_f = sb("src_f", [P, T])
        src_c = sb("src_c", [P, T])
        src_lo = sb("src_lo", [P, T], BF16)
        count_h = sb("count_h", [P, NB], BF16)
        zero_h = sb("zero_h", [P, P], BF16)
        curv_part = sb("curv_part", [NB, 3, NA], BF16)
        keep = sb("keep", [P, NCH, W1])
        keep_big = sb("keep_big", [P, NCH, W1])
        carry_mask = sb("carry_mask", [P, P])
        carry_from = sb("carry_from", [P, NA, NB])
        no_carry = sb("no_carry", [NB, NA])
        end_row = sb("end_row", [NB, NA], I32)
        has_in = sb("has_in", [NB, NA])
        in_share = sb("in_share", [NB, NA])
        out_share = sb("out_share", [NB, NA])
        h = sb("h", [NB, NA, D])
        stat = sb("stat", [NB, 4, NA])
        stepped = sem("stepped")
        products = {"sems": [sem("node_" + n) for n in ("turned", "held", "made", "added")] + [stepped], "count": (0, 0)}

        norms = {"sems": [sem("node_" + n) for n in ("var_ready", "root_ready")], "count": 0}
        table_done = [sem(f"table_done{i}") for i in range(NT)]

        with ExitStack() as ctx:
            sb, ps = tiles(ctx, "prep")
            grid = sb("grid", [P, P], I32)
            count_i = sb("count_i", [P, P], I32)
            lane_i = sb("lane_i", [P, 1], I32)
            node_i = sb("node_i", [NB, NA], I32)
            ends_i = sb("ends_i", [P, 2, T], I32)
            dst_f = sb("dst_f", [P, T])
            dst_hi = sb("dst_hi", [P, T], BF16)
            dst_lo = sb("dst_lo", [P, T], BF16)
            work = sb("work", [P, T])
            work2 = sb("work2", [P, T])
            prev_last = sb("prev_last", [P, 1], I32)
            prev_f = sb("prev_f", [P, 1])
            cont = sb("cont", [P, 1])
            spans = sb("spans", [P, 1])
            curv = sb("curv", [NB, NA])
            curv_rest = sb("curv_rest", [NB, NA])
            hot_hi = sb("hot_hi", [P, 2, TC, NB], BF16)
            hot_lo = sb("hot_lo", [P, 2, TC, NA], BF16)
            deg = sb("deg", [NB, NA])
            run = sb("run", [NB, NA])
            start_f = sb("start_f", [NB, NA])
            end_f = sb("end_f", [NB, NA])
            nwork = sb("nwork", [NB, 4, NA])
            first_row = sb("first_row", [NB, NA], I32)
            xc = sb("xc", [NB, NA, D + 1])
            x0 = sb("x0", [NB, NA, D])
            zero = sb("zero", [P, TROWS * RW // P])
            src_turned = sb("src_turned", [P, T], I32)
            src_half = sb("src_half", [P, T], F16)
            head = sb("head", [P, D + 1])
            ps_deg = ps("ps_deg", [P, 512])
            ps_misc = ps("ps_misc", [P, 2, 512])

            loaded, x_loaded, prev_loaded = sem("loaded"), sem("x_loaded"), sem("prev_loaded")
            iota_done, const_done = sem("iota_done"), sem("const_done")
            chain = sem("prep_chain")
            turned_loaded, half_ready, half_put = (sem(n) for n in ("turned_loaded", "half_ready", "half_put"))
            hot_ready = sem("dst_hot_ready")
            hot_used = sem("dst_hot_used")
            deg_made, totals, offsets, keys, keyed, key_used = (
                sem(n) for n in ("deg_made", "totals", "offsets", "keys", "keyed", "key_used"))
            first_ready, xc_ready, xc_stored, placed = (sem(n) for n in ("first_ready", "xc_ready", "xc_stored", "placed"))
            zeros_stored, head_got, head_put, cont_made, cont_rows = (
                sem(n) for n in ("zeros_stored", "head_got", "head_put", "cont_made", "cont_rows"))
            FZ = T * (D + 1) // 15
            first_flat = first_rows[0:EP, :].rearrange("(p t) d -> p (t d)", t=T)
            assert FZ // 2 <= TROWS * RW // P and T * (D + 1) % 30 == 0

            with nc.Block() as block:

                @block.sync
                def _(sp):
                    sp.sem_inc(hot_used, 2)
                    sp.dma_start(ends_i[:, 0, :], t["src_pad"]).then_inc(loaded, 16)
                    sp.dma_start(ends_i[:, 1, :], t["dst_pad"]).then_inc(loaded, 16)
                    sp.dma_start(x0[:].rearrange("b a d -> b (a d)"), nodes(t["x"])).then_inc(x_loaded, 16)
                    sp.dma_start(curv[:], t["node_vec"].rearrange("(b a) -> b a", a=NA)).then_inc(x_loaded, 16)
                    sp.dma_start(h[:].rearrange("b a d -> b (a d)"), nodes(t["x"])).then_inc(x_loaded, 16)
                    sp.dma_start(src_turned[:], t["src_turned"]).then_inc(turned_loaded, 16)
                    sp.wait_ge(const_done, 2)
                    sp.dma_start(prev_last[1:P, :], t["dst_pad"][0:P - 1, T - 1:T],
                                 allow_slow_non_contiguous=True).then_inc(prev_loaded, 16)
                    for i in range(30):
                        sp.dma_start(first_flat[:, i * (FZ // 2):(i + 1) * (FZ // 2)],
                                     zero[:, 0:FZ // 2]).then_inc(zeros_stored, 16)
                    sp.dma_start(h_rows[N:N + 1, :], zero[0:1, 0:D]).then_inc(zeros_stored, 16)
                    sp.dma_start(xc_rows[N:N + 1, :], zero[0:1, 0:D + 1]).then_inc(xc_stored, 16)
                    sp.wait_ge(xc_ready, 2)
                    sp.dma_start(nodes(xc_rows[0:N, :]), xc[:].rearrange("b a d -> b (a d)")).then_inc(xc_stored, 16)
                    sp.wait_ge(half_ready, 1)
                    sp.dma_start(by_tile.rearrange("t p -> (t p)").rearrange("(q k) -> q k", k=T),
                                 src_half[:]).then_inc(half_put, 16)
                    sp.wait_ge(half_put, 16)
                    sp.wait_ge(head_got, 16)
                    sp.wait_ge(placed, 16 * NA)
                    sp.dma_start(first_rows[0:EP, :].rearrange("(p t) d -> p (t d)", t=T)[:, 0:D + 1],
                                 head[:]).then_inc(head_put, 16)
                    sp.wait_ge(head_put, 16)
                    for i in range(NT):
                        sp.wait_ge(table_done[i], 16)

                @block.gpsimd
                def _(pool):
                    nc.gpsimd.iota(grid[:], [[1, P]], base=0, channel_multiplier=-1).then_inc(iota_done, 1)
                    nc.gpsimd.iota(count_i[:], [[1, P]], base=0, channel_multiplier=0).then_inc(iota_done, 1)
                    nc.gpsimd.iota(lane_i[:], [[1, 1]], base=0, channel_multiplier=1).then_inc(iota_done, 1)
                    nc.gpsimd.iota(node_i[:], [[1, NA]], base=-CENTRE, channel_multiplier=NA).then_inc(iota_done, 1)
                    nc.gpsimd.memset(prev_last[:], -1).then_inc(const_done, 1)
                    nc.gpsimd.memset(zero[:], 0.0).then_inc(const_done, 1)
                    pool.wait_ge(const_done, 2)
                    for i in range(NT):
                        pool.dma_start(tables[i].rearrange("r d -> (r d)").rearrange("(p k) -> p k", p=P),
                                       zero[:]).then_inc(table_done[i], 16)
                    pool.wait_ge(loaded, 32)
                    pool.wait_ge(xc_stored, 32)
                    pool.indirect_dma_start(head[:], None, xc_rows,
                                            bass.IndirectOffsetOnAxis(ap=ends_i[:, 1, 0:1], axis=0)).then_inc(head_got, 16)
                    pool.wait_ge(first_ready, 1)
                    pool.wait_ge(zeros_stored, 16 * 31)
                    for a in range(NA):
                        pool.indirect_dma_start(first_rows, bass.IndirectOffsetOnAxis(ap=first_row[:, a:a + 1], axis=0),
                                                xc[:, a, :], None).then_inc(placed, 16)

                @block.vector
                def _(dve):
                    link = Chain(dve, chain)
                    v = nc.vector
                    dve.wait_ge(iota_done, 4)
                    v.tensor_scalar(ident[:], grid[:], 0.0, None, ALU.is_equal)
                    v.tensor_scalar(later[:], grid[:], 0.0, None, ALU.is_gt)
                    v.tensor_scalar(earlier[:], grid[:], 0.0, None, ALU.is_lt)
                    v.tensor_copy(count_h[:], count_i[:, 0:NB])
                    v.tensor_copy(lane[:], lane_i[:])
                    v.tensor_copy(node_id[:], node_i[:])
                    link(v.memset(zero_h[:], 0.0))
                    dve.wait_ge(x_loaded, 48)
                    v.tensor_copy(xc[:, :, 0:D], x0[:]).then_inc(xc_ready, 1)
                    v.tensor_copy(xc[:, :, D], curv[:]).then_inc(xc_ready, 1)
                    link(v.tensor_copy(curv_part[:, 0, :], curv[:]))
                    link(v.tensor_tensor(curv_rest[:], curv[:], curv_part[:, 0, :], ALU.subtract))
                    link(v.tensor_copy(curv_part[:, 1, :], curv_rest[:]))
                    link(v.tensor_tensor(curv_part[:, 2, :], curv_rest[:], curv_part[:, 1, :], ALU.subtract))
                    dve.wait_ge(turned_loaded, 16)
                    v.tensor_scalar(src_half[:], src_turned[:], float(CENTRE), None, ALU.subtract).then_inc(half_ready, 1)
                    dve.wait_ge(loaded, 32)
                    for i, full, hi, lo in ((0, src_f, None, src_lo[:]), (1, dst_f, dst_hi[:], dst_lo[:])):
                        link(v.tensor_copy(full[:], ends_i[:, i, :]))
                        link(v.tensor_scalar(work[:], full[:], 1.0 / NA, 0.5 / NA - 0.5, ALU.mult, ALU.add))
                        link(v.tensor_scalar(work[:], work[:], ROUND, ROUND, ALU.add, ALU.subtract))
                        if hi is not None:
                            link(v.tensor_copy(hi, work[:]))
                        link(v.tensor_scalar(work[:], work[:], -float(NA), None, ALU.mult))
                        link(v.tensor_tensor(lo, work[:], full[:], ALU.add))
                    link(v.tensor_scalar(src_c[:], src_f[:], float(CENTRE), None, ALU.subtract))
                    link(v.memset(work2[:, 0:1], 0.0))
                    link(v.tensor_tensor(work2[:, 1:T], dst_f[:, 1:T], dst_f[:, 0:T - 1], ALU.is_equal))
                    link(v.memset(keep[:, :, 0:1], 0.0))
                    link(v.tensor_copy(keep[:, :, 1:W1], work2[:].rearrange("p (c t) -> p c t", t=TC)))
                    link(v.tensor_scalar(keep_big[:], keep[:], 2.0, -1.0, ALU.mult, ALU.add))
                    link(v.tensor_scalar(keep_big[:], keep_big[:], BIG, None, ALU.mult))
                    dve.wait_ge(prev_loaded, 16)
                    link(v.tensor_copy(prev_f[:], prev_last[:]))
                    link(v.tensor_tensor(cont[:], prev_f[:], dst_f[:, 0:1], ALU.is_equal))
                    link(v.tensor_tensor(spans[:], dst_f[:, 0:1], dst_f[:, T - 1:T], ALU.is_equal))
                    v.tensor_tensor(cont[:], cont[:], spans[:], ALU.mult).then_inc(cont_made, 1)
                    dve.wait_ge(cont_rows, 1)
                    link(v.tensor_copy(carry_mask[:], ps_misc[:, 0, 0:P]))
                    link(v.tensor_scalar(carry_mask[0:D, :], carry_mask[0:D, :], 2.0, -1.0, ALU.mult, ALU.add))
                    link(v.tensor_scalar(carry_mask[0:D, :], carry_mask[0:D, :], BIG, None, ALU.mult))

                    with dve.Fori(0, NCH // 2) as g:
                        for k in range(2):
                            dve.wait_ge(hot_used, g * 2 + (k + 1))
                            v.tensor_tensor(hot_hi[:, k, :, :], bc(count_h[:].unsqueeze(1), [P, TC, NB]),
                                            bc(dst_hi[:, bass.ds((g * 2 + k) * TC, TC)].unsqueeze(2), [P, TC, NB]),
                                            ALU.is_equal).then_inc(hot_ready, 1)
                            v.tensor_tensor(hot_lo[:, k, :, :], bc(count_h[:, 0:NA].unsqueeze(1), [P, TC, NA]),
                                            bc(dst_lo[:, bass.ds((g * 2 + k) * TC, TC)].unsqueeze(2), [P, TC, NA]),
                                            ALU.is_equal).then_inc(hot_ready, 1)

                    dve.wait_ge(deg_made, 1)
                    link(v.tensor_copy(deg[:], ps_deg[0:NB, 0:NA]))
                    link(v.memset(nwork[:, 3, :], 1.0))
                    link(v.tensor_tensor_scan(run[:], nwork[:, 3, :], deg[:], 0.0, ALU.mult, ALU.add))
                    v.tensor_copy(nwork[:, 0, 0:1], run[:, NA - 1:NA]).then_inc(totals, 1)
                    dve.wait_ge(offsets, 1)
                    link(v.tensor_tensor(end_f[:], run[:], bc(ps_misc[0:NB, 1, 0:1], [NB, NA]), ALU.add))
                    link(v.tensor_tensor(start_f[:], end_f[:], deg[:], ALU.subtract))
                    link(v.tensor_scalar(has_in[:], deg[:], 1.0, None, ALU.min))
                    link(v.tensor_scalar(nwork[:, 1, :], start_f[:], float(EP), None, ALU.subtract))
                    link(v.tensor_scalar(nwork[:, 1, :], nwork[:, 1, :], lane[0:NB, :], None, ALU.subtract))
                    link(v.tensor_tensor(nwork[:, 1, :], nwork[:, 1, :], has_in[:], ALU.mult))
                    link(v.tensor_scalar(nwork[:, 1, :], nwork[:, 1, :], lane[0:NB, :], float(EP), ALU.add, ALU.add))
                    v.tensor_copy(first_row[:], nwork[:, 1, :]).then_inc(first_ready, 1)
                    link(v.tensor_scalar(nwork[:, 2, :], deg[:], 1.0, None, ALU.max))
                    link(v.reciprocal(in_share[:], nwork[:, 2, :]))
                    link(v.tensor_tensor(in_share[:], in_share[:], has_in[:], ALU.mult))
                    link(v.tensor_scalar(end_f[:], end_f[:], 1.0, 0.0, ALU.subtract, ALU.max))
                    link(v.tensor_copy(end_row[:], end_f[:]))
                    link(v.tensor_scalar(nwork[:, 0, :], end_f[:], 1.0 / T, 0.5 / T - 0.5, ALU.mult, ALU.add))
                    link(v.tensor_scalar(nwork[:, 0, :], nwork[:, 0, :], ROUND, ROUND, ALU.add, ALU.subtract))
                    link(v.tensor_scalar(nwork[:, 1, :], nwork[:, 0, :], float(T), None, ALU.mult))
                    link(v.tensor_tensor(nwork[:, 1, :], start_f[:], nwork[:, 1, :], ALU.is_lt))
                    link(v.tensor_tensor(nwork[:, 1, :], nwork[:, 1, :], has_in[:], ALU.mult))
                    link(v.tensor_scalar(no_carry[:], nwork[:, 1, :], 1.0, BIG, ALU.subtract, ALU.mult))
                    link(v.tensor_tensor(nwork[:, 2, :], nwork[:, 0, :], nwork[:, 1, :], ALU.mult))
                    v.tensor_scalar(nwork[:, 2, :], nwork[:, 2, :], 1.0, None, ALU.subtract).then_inc(keys, 1)
                    for i, (a0, n) in enumerate(pieces(NA, TG)):
                        dve.wait_ge(keyed, i + 1)
                        v.tensor_scalar(carry_from[:, a0:a0 + n, :],
                                        ps_misc[:, i % 2, 0:n * NB].rearrange("p (a b) -> p a b", b=NB),
                                        lane[:], None, ALU.is_equal).then_inc(key_used, 1)

                @block.tensor
                def _(pe):
                    pe.wait_ge(chain, 1)
                    nc.tensor.matmul(ps_deg[0:NB, 0:NA], zero_h[:, 0:NB], zero_h[:, 0:NA], start=True, stop=False,
                                     skip_group_check=True)
                    pe.wait_ge(cont_made, 1)
                    nc.tensor.matmul(ps_misc[:, 0, 0:P], bc(cont[:], [P, P]), ident[:],
                                     start=True, stop=True).then_inc(cont_rows, 1)
                    with pe.Fori(0, NCH // 2) as g:
                        for k in range(2):
                            pe.wait_ge(hot_ready, g * 4 + (2 * k + 2))
                            for j in range(TC):
                                ins = nc.tensor.matmul(ps_deg[0:NB, 0:NA], hot_hi[:, k, j, :], hot_lo[:, k, j, :],
                                                       start=False, stop=False, skip_group_check=True)
                            ins.then_inc(hot_used, 1)
                    nc.tensor.matmul(ps_deg[0:NB, 0:NA], zero_h[:, 0:NB], zero_h[:, 0:NA],
                                     start=False, stop=True, skip_group_check=True).then_inc(deg_made, 1)
                    pe.wait_ge(totals, 1)
                    nc.tensor.matmul(ps_misc[0:NB, 1, 0:1], later[0:NB, 0:NB], nwork[:, 0, 0:1],
                                     start=True, stop=True).then_inc(offsets, 1)
                    pe.wait_ge(keys, 1)
                    for i, (a0, n) in enumerate(pieces(NA, TG)):
                        if i >= 2:
                            pe.wait_ge(key_used, i - 1)
                        for j in range(n):
                            ins = nc.tensor.matmul(ps_misc[:, i % 2, j * NB:(j + 1) * NB],
                                                   bc(nwork[:, 2, a0 + j:a0 + j + 1], [NB, P]), ident[0:NB, 0:NB],
                                                   start=True, stop=True)
                        ins.then_inc(keyed, 1)

        with ExitStack() as ctx:
            sb, ps = tiles(ctx, "scatter")
            CF = D + 1
            filled = sb("filled", [P, 2, TC, CF])
            fill_in = sb("fill_in", [P, CF * W1])
            fill_keep = sb("fill_keep", [P, CF * W1], BF16)
            fill_out = sb("fill_out", [P, CF * W1])
            w_curv = sb("w_curv", [P, D])
            b_curv = sb("b_curv", [P, D])
            diff = sb("diff", [P, TC])
            gate = sb("gate", [P, D, TC])
            rows = sb("rows", [P, 2, TC, RW])
            sums = sb("sums", [P, 2, TC, RW])
            tile_src = sb("tile_src", [P, TC, P], F16)
            same = sb("same", [P, 2, TC, P])
            before = sb("before", [P, TC, P], BF16)
            turned_hot = sb("turned_hot", [NB, TC, P], BF16)
            hot_lo = sb("hot_lo", [P, TC, NA], BF16)
            next_id = sb("next_id", [NB, 1])
            picked = sb("picked", [P, TC, NA])
            curv_src = sb("curv_src", [P, 2, TC])
            dup = sb("dup", [P, 2, TC])
            spare = sb("spare", [P, 1])
            to_row = sb("to_row", [P, 2, TC], I32)
            HALF = (TC + 1) // 2
            ps_pick = ps("ps_pick", [P, 2, 512])
            ps_sum = ps("ps_sum", [P, 3, 512])
            assert HALF * NA <= 512 and GR * RW <= 512 and NG % 3 == 0
            in3, keep3, out3 = (a[:].rearrange("p (f t) -> p f t", t=W1) for a in (fill_in, fill_keep, fill_out))

            fill_loaded = [sem(f"fill_loaded{k}") for k in range(2)]
            edge_loaded = [sem(f"edge_loaded{k}") for k in range(2)]
            curv_loaded, fill_turned, fill_masked, fill_scanned, tile_loaded = (
                sem(n) for n in ("curv_loaded", "fill_turned", "fill_masked", "fill_scanned", "tile_loaded"))
            wchain, arg_ready, gate_ready, rows_made = (sem(n) for n in ("wchain", "arg_ready", "gate_ready", "rows_made"))
            same_made, summed, sums_held, same_free, index_ready = (
                sem(n) for n in ("same_made", "summed", "sums_held", "same_free", "index_ready"))
            hot_ready, looked, pick_used = (sem("src_" + n) for n in ("hot_ready", "looked", "pick_used"))
            sent = [sem(f"sent{k}") for k in range(2)]

            with nc.Block() as block:

                @block.sync
                def _(sp):
                    sp.dma_start(w_curv[:], bc(t["w_curv"], [P, D])).then_inc(curv_loaded, 16)
                    sp.dma_start(b_curv[:], bc(t["b_curv"], [P, D])).then_inc(curv_loaded, 16)
                    sp.wait_ge(curv_loaded, 32)
                    sp.sem_inc(fill_turned, 2)
                    sp.sem_inc(same_free, 2)
                    sp.sem_inc(same_made, 1)
                    first_by_part = first_rows[0:EP, :].rearrange("(p t) d -> p t d", t=T)
                    edge_by_part = t["edge64"].rearrange("(p t) d -> p t d", t=T)
                    with sp.Fori(0, NCH // 2) as g:
                        for k in range(2):
                            c = g * 2 + k
                            sp.wait_ge(same_made, c + 1)
                            sp.dma_start(tile_src[:], bc(by_tile[bass.ds(c * TC, TC), :].unsqueeze(0), [P, TC, P])
                                         ).then_inc(tile_loaded, 16)
                            sp.wait_ge(fill_turned, c + 1)
                            sp.dma_start(filled[:, k, :, :], first_by_part[:, bass.ds(c * TC, TC), :]
                                         ).then_inc(fill_loaded[k], 16)
                            sp.wait_ge(same_free, c + 1)
                            sp.dma_start(rows[:, k, :, D:2 * D], edge_by_part[:, bass.ds(c * TC, TC), :]
                                         ).then_inc(edge_loaded[k], 16)


                @block.scalar
                def _(act):
                    def fill(c, k, q):
                        act.wait_ge(fill_scanned, c + 1)
                        nc.scalar.activation(keep3, bc(keep[:, bass.ds(c, 1), :], [P, CF, W1]),
                                             ACT.Copy).then_inc(fill_masked, 1)
                        act.wait_ge(fill_loaded[k], q * 16 + 16)
                        nc.scalar.activation(in3[:, :, 1:W1], filled[:, k, :, :].rearrange("p t f -> p f t"),
                                             ACT.Copy).then_inc(fill_turned, 1)

                    def step(i, k, q, q_next, last=False):
                        act.wait_ge(arg_ready, i + 1)
                        nc.scalar.activation(gate[:], gate[:], ACT.Sigmoid).then_inc(gate_ready, 1)
                        if not last:
                            fill(i + 1, 1 - k, q_next)
                        act.wait_ge(sent[k], q + 1)
                        for j in range(NG):
                            act.wait_ge(summed, i * NG + (j + 1))
                            nc.scalar.activation(sums[:, k, j * GR:(j + 1) * GR, :].rearrange("p t f -> p (t f)"),
                                                 ps_sum[:, j % 3, 0:GR * RW], ACT.Copy).then_inc(sums_held, 1)

                    fill(0, 0, 0)
                    with act.Fori(0, NCH // 2 - 1) as g:
                        step(g * 2, 0, g, g)
                        step(g * 2 + 1, 1, g, g + 1)
                    step(NCH - 2, 0, NCH // 2 - 1, NCH // 2 - 1)
                    step(NCH - 1, 1, NCH // 2 - 1, 0, last=True)

                @block.vector
                def _(dve):
                    v = nc.vector
                    link = Chain(dve, wchain)
                    dve.wait_ge(curv_loaded, 32)
                    dve.sem_inc(fill_scanned, 1)
                    dve.sem_inc(sent[0], 1)
                    link(v.tensor_scalar(spare[:], lane[:], float(N + 1), None, ALU.add))
                    link(v.tensor_scalar(next_id[:], node_id[:, 0:1], float(NA), None, ALU.add))
                    link(v.memset(rows[:, :, :, 2 * D:RW], 1.0))
                    link(v.memset(fill_out[:], 0.0))

                    def find(c, link):
                        dve.wait_ge(tile_loaded, c * 16 + 16)
                        link(v.tensor_scalar(before[0:NB, :, :], tile_src[0:NB, :, :], next_id[:, 0:1], None, ALU.is_ge))
                        v.scalar_tensor_tensor(out=turned_hot[:], in0=tile_src[0:NB, :, :], scalar=node_id[:, 0:1],
                                               in1=before[0:NB, :, :], op0=ALU.is_ge, op1=ALU.subtract
                                               ).then_inc(hot_ready, 1)
                        link(v.tensor_tensor(hot_lo[:], bc(count_h[:, 0:NA].unsqueeze(1), [P, TC, NA]),
                                             bc(src_lo[:, bass.ds(c * TC, TC)].unsqueeze(2), [P, TC, NA]), ALU.is_equal))

                    def compare(c, k):
                        dve.wait_ge(same_free, c + 1)
                        v.tensor_tensor(same[:, k, :, :], tile_src[:],
                                        bc(src_c[:, bass.ds(c * TC, TC)].unsqueeze(2), [P, TC, P]),
                                        ALU.is_equal).then_inc(same_made, 1)

                    def count(c, k, link):
                        dve.wait_ge(same_made, c + 2)
                        dve.wait_ge(hot_ready, c + 1)
                        for i in range(TC):
                            ins = v.tensor_tensor_reduce(out=before[:, i, :], in0=same[:, k, i, :], in1=earlier[:],
                                                         scale=1.0, scalar=0.0, op0=ALU.mult, op1=ALU.add,
                                                         accum_out=dup[:, k, i:i + 1])
                        link(ins)
                        dve.wait_ge(looked, c + 1)
                        for j, (t0, n) in enumerate(pieces(TC, HALF)):
                            v.tensor_tensor(picked[:, t0:t0 + n, :],
                                            ps_pick[:, j, 0:n * NA].rearrange("p (t a) -> p t a", a=NA),
                                            hot_lo[:, t0:t0 + n, :], ALU.mult).then_inc(pick_used, 1)
                        dve.wait_ge(pick_used, c * 2 + 2)
                        link(v.tensor_reduce(curv_src[:, k, :], picked[:], AX, ALU.add))

                    def index_rows(c, k, q, link):
                        link(v.tensor_scalar(dup[:, k, :], dup[:, k, :], 1.0, None, ALU.min))
                        link(v.scalar_tensor_tensor(out=diff[:], in0=src_f[:, bass.ds(c * TC, TC)], scalar=spare[:, 0:1],
                                                    in1=dup[:, k, :], op0=ALU.subtract, op1=ALU.mult))
                        dve.wait_ge(sent[k], q + 1)
                        v.tensor_tensor(to_row[:, k, :], src_f[:, bass.ds(c * TC, TC)], diff[:],
                                        ALU.subtract).then_inc(index_ready, 1)

                    def gate_arguments(c, k, link):
                        dve.wait_ge(fill_masked, c + 1)
                        dve.wait_ge(fill_turned, c + 3)
                        link(v.tensor_copy(in3[:, :, 0:1], out3[:, :, TC:W1]))
                        v.tensor_tensor_scan(fill_out[:], fill_keep[:], fill_in[:], 0.0, ALU.mult,
                                             ALU.add).then_inc(fill_scanned, 1)
                        dve.wait_ge(fill_scanned, c + 2)
                        dve.wait_ge(index_ready, c + 1)
                        link(v.tensor_tensor(diff[:], curv_src[:, k, :], out3[:, D, 1:W1], ALU.subtract))
                        link(v.scalar_tensor_tensor(out=diff[:], in0=diff[:], scalar=-1.0, in1=diff[:], op0=ALU.mult,
                                                    op1=ALU.max))
                        v.tensor_tensor(gate[:], bc(diff[:].unsqueeze(1), [P, D, TC]),
                                        bc(w_curv[:].unsqueeze(2), [P, D, TC]), ALU.mult).then_inc(rows_made, 1)
                        dve.wait_ge(rows_made, c * 2 + 1)
                        v.tensor_tensor(gate[:], gate[:], bc(b_curv[:].unsqueeze(2), [P, D, TC]),
                                        ALU.add).then_inc(arg_ready, 1)

                    def gated(c, k):
                        dve.wait_ge(gate_ready, c + 1)
                        dve.wait_ge(same_free, c + 1)
                        v.tensor_tensor(rows[:, k, :, 0:D].rearrange("p t f -> p f t"), gate[:], out3[:, 0:D, 1:W1],
                                        ALU.mult).then_inc(rows_made, 1)
                        dve.wait_ge(rows_made, c * 2 + 2)

                    def step(i, k, q, link, last=False):
                        index_rows(i, k, q, link)
                        gate_arguments(i, k, link)
                        if not last:
                            find(i + 1, link)
                            compare(i + 1, 1 - k)
                        gated(i, k)
                        if not last:
                            count(i + 1, 1 - k, link)

                    find(0, link)
                    compare(0, 0)
                    count(0, 0, link)
                    base, per = link.n, 9
                    with dve.Fori(0, NCH // 2 - 1) as g:
                        step(g * 2, 0, g, Chain(dve, wchain, g * (2 * per) + base))
                        step(g * 2 + 1, 1, g, Chain(dve, wchain, g * (2 * per) + (base + per)))
                    link = Chain(dve, wchain, base + (NCH - 2) * per)
                    step(NCH - 2, 0, NCH // 2 - 1, link)
                    assert link.n == per
                    step(NCH - 1, 1, NCH // 2 - 1, link, last=True)

                @block.tensor
                def _(pe):
                    def look_up(c):
                        pe.wait_ge(hot_ready, c + 1)
                        for j, (t0, n) in enumerate(pieces(TC, HALF)):
                            for i in range(n):
                                for s in range(3):
                                    ins = nc.tensor.matmul(ps_pick[:, j, i * NA:(i + 1) * NA], turned_hot[:, t0 + i, :],
                                                           curv_part[:, s, :], start=(s == 0), stop=(s == 2))
                        ins.then_inc(looked, 1)

                    def add_up(c, k, q, first=False):
                        pe.wait_ge(same_made, c + 2)
                        pe.wait_ge(rows_made, c * 2 + 2)
                        pe.wait_ge(edge_loaded[k], q * 16 + 16)
                        for j in range(NG):
                            if not first:
                                pe.wait_ge(sums_held, c * NG + (j - 2))
                            elif j >= 3:
                                pe.wait_ge(sums_held, j - 2)
                            for i in range(GR):
                                ins = nc.tensor.matmul(ps_sum[:, j % 3, i * RW:(i + 1) * RW], same[:, k, j * GR + i, :],
                                                       rows[:, k, j * GR + i, :], start=True, stop=True)
                            ins.then_inc(summed, 1)

                    def step(i, k, q, first=False, last=False):
                        if not last:
                            look_up(i + 1)
                        add_up(i, k, q, first)
                        pe.wait_ge(summed, i * NG + NG)
                        pe.sem_inc(same_free, 1)

                    look_up(0)
                    step(0, 0, 0, first=True)
                    with pe.Fori(0, NCH // 2 - 1) as g:
                        step(g * 2 + 1, 1, g)
                        step(g * 2 + 2, 0, g + 1)
                    step(NCH - 1, 1, NCH // 2 - 1, last=True)

                @block.gpsimd
                def _(pool):
                    with pool.Fori(0, NCH // 2) as g:
                        for k in range(2):
                            c = g * 2 + k
                            pool.wait_ge(index_ready, c + 1)
                            for i in range(TC):
                                if i % GR == 0:
                                    pool.wait_ge(sums_held, c * NG + (i // GR + 1))
                                pool.wait_ge(table_done[i % NT], c * (16 * TC // NT) + 16 * (i // NT + 1))
                                pool.sem_inc(stepped, 1)
                                pool.indirect_dma_start(
                                    tables[i % NT], bass.IndirectOffsetOnAxis(ap=to_row[:, k, i:i + 1], axis=0),
                                    sums[:, k, i, :], None, compute_op=ALU.add).then_inc(table_done[i % NT], 16)
                                if i == NT - 1:
                                    pool.sem_inc(sent[1 - k], 1)
                    for i in range(NT):
                        pool.wait_ge(table_done[i], 16 * (1 + NCH * TC // NT))

        res = sb_top("res", [NB, NA, D])
        hl = sb_top("hl", [NB, NA, D])
        parts = sb_top("parts", [NB, NA, 3, D], BF16)
        index = sb_top("index", [P, 2, TC - PICKED_LAST], I32)
        tile_src = sb_top("picked_src", [P, 2, PICKED, P], F16)
        with ExitStack() as ctx:
            sb, ps = tiles(ctx, "nodes01")
            AHEAD = 4
            acc = sb("acc", [NB, NA, RW])
            part = sb("part", [NB, AHEAD, NA * RW])
            y = sb("y", [NB, NA, D])
            y2 = sb("y2", [NB, NA, D])
            scratch = sb("scratch", [NB, NA, D])
            heldA = sb("heldA", [P, NA * NB])
            heldB = sb("heldB", [P, NA * NB])
            w = {n: sb("w_" + n, [D, D]) for n in ("lin0", "l1x", "l1v", "l1u", "l1o", "adapt")}
            b = {n: sb("b_" + n, [NB, D]) for n in ("lin0", "l1h", "l1o", "adapt")}
            u0 = sb("u0", [D, 1])
            ps_turn = ps("ps_turn", [P, 2, 512])
            ps_out = ps("ps_out", [P, 2, 512])
            ps_u = ps("ps_u", [P, 512])
            wl, tab_added, nchain = (sem(n) for n in ("w01_loaded", "tab_added", "n01_chain"))
            tab_got = [sem(f"tab_got{k}") for k in range(AHEAD)]
            ready0, ready1, ready2, ready3, u_made, gelu_in, gelu_out, h_ready, h_put = (
                sem("n01_" + n) for n in ("mean", "x1", "hid", "x2", "u_made", "gelu_in", "gelu_out", "h_ready", "h_put"))
            lin0 = Linear(products, [acc[:, :, 0:D]], [w["lin0"][:]], D)
            lin1 = Linear(products, [h[:], acc[:, :, D:2 * D]], [w["l1x"][:], w["l1v"][:]], D)
            lin2 = Linear(products, [y[:]], [w["l1o"][:]], D)
            adapt = Linear(products, [h[:]], [w["adapt"][:]], D)
            norm0, norm1 = Norm(norms, stat), Norm(norms, stat)
            held = [heldA, heldB]

            with nc.Block() as block:

                @block.sync
                def _(sp):
                    for i in range(NT):
                        if i >= AHEAD:
                            sp.wait_ge(tab_added, i - AHEAD + 1)
                        sp.dma_start(part[:, i % AHEAD, :], nodes(tables[i][0:N, :])).then_inc(tab_got[i % AHEAD], 16)
                        if i == AHEAD - 1:
                            for n in w:
                                sp.dma_start(w[n][:], t["w_" + n]).then_inc(wl, 16)
                            for n in b:
                                sp.dma_start(b[n][:], bc(t["b_" + n], [NB, D])).then_inc(wl, 16)
                            sp.dma_start(u0[:], t["u0"]).then_inc(wl, 16)
                    sp.wait_ge(h_ready, 1)
                    sp.dma_start(nodes(h_rows[0:N, :]), h[:].rearrange("b a d -> b (a d)")).then_inc(h_put, 16)
                    sp.wait_ge(h_put, 16)

                @block.vector
                def _(dve):
                    v = nc.vector
                    link = Chain(dve, nchain)
                    flat = acc[:].rearrange("b a d -> b (a d)")
                    for i in range(NT):
                        dve.wait_ge(tab_got[i % AHEAD], 16 * (i // AHEAD + 1))
                        if i == 0:
                            v.tensor_copy(flat, part[:, 0, :]).then_inc(tab_added, 1)
                        else:
                            v.tensor_tensor(flat, flat, part[:, i % AHEAD, :], ALU.add).then_inc(tab_added, 1)
                        dve.wait_ge(tab_added, i + 1)
                    link(v.tensor_scalar(out_share[:], acc[:, :, 2 * D], 1.0, None, ALU.max))
                    link(v.reciprocal(out_share[:], out_share[:]))
                    v.tensor_tensor(acc[:], acc[:], bc(out_share[:].unsqueeze(2), [NB, NA, RW]),
                                    ALU.mult).then_inc(ready0, 1)
                    dve.wait_ge(wl, 16 * (len(w) + len(b) + 1))
                    lin0.dve(dve, nc, ps_out, b["lin0"], y)
                    dve.sem_inc(gelu_in, 1)
                    dve.wait_ge(gelu_out, 1)
                    link(v.tensor_tensor(h[:], h[:], y2[:], ALU.add))
                    norm0.dve(dve, nc, link, h[:], scratch[:])
                    dve.sem_inc(ready1, 1)
                    dve.wait_ge(u_made, 1)
                    link(v.tensor_tensor(b["l1h"][:], b["l1h"][:], ps_u[0:NB, 0:D], ALU.add))
                    lin1.dve(dve, nc, ps_out, b["l1h"], y)
                    v.tensor_scalar(y[:], y[:], 0.0, None, ALU.max).then_inc(ready2, 1)
                    lin2.dve(dve, nc, ps_out, b["l1o"], y2)
                    link(v.tensor_scalar(y2[:], y2[:], 0.0, None, ALU.max))
                    link(v.tensor_tensor(h[:], h[:], y2[:], ALU.add))
                    norm1.dve(dve, nc, link, h[:], scratch[:])
                    dve.sem_inc(h_ready, 1)
                    dve.sem_inc(ready3, 1)
                    link(v.tensor_copy(hl[:], h[:]))
                    adapt.dve(dve, nc, ps_out, b["adapt"], res)

                @block.scalar
                def _(act):
                    lin0.act(act, nc, ps_turn, held)
                    act.wait_ge(gelu_in, 1)
                    nc.scalar.activation(y2[:], y[:], ACT.Gelu).then_inc(gelu_out, 1)
                    norm0.act(act, nc)
                    lin1.act(act, nc, ps_turn, held)
                    lin2.act(act, nc, ps_turn, held)
                    norm1.act(act, nc)
                    adapt.act(act, nc, ps_turn, held)

                @block.tensor
                def _(pe):
                    pe.wait_ge(wl, 16 * (len(w) + len(b) + 1))
                    nc.tensor.matmul(ps_u[0:NB, 0:D], bc(u0[:], [D, NB]), w["l1u"][:], start=True,
                                     stop=True).then_inc(u_made, 1)
                    pe.wait_ge(ready0, 1)
                    lin0.pe(pe, nc, ps_turn, ps_out, held, ident)
                    pe.wait_ge(ready1, 1)
                    lin1.pe(pe, nc, ps_turn, ps_out, held, ident)
                    pe.wait_ge(ready2, 1)
                    lin2.pe(pe, nc, ps_turn, ps_out, held, ident)
                    pe.wait_ge(ready3, 1)
                    adapt.pe(pe, nc, ps_turn, ps_out, held, ident)

        with ExitStack() as ctx:
            sb, ps = tiles(ctx, "sage")
            agg = sb("agg", [NB, NA, 2 * D])
            run_max = sb("run_max", [P, D * W1])
            run_sum = sb("run_sum", [P, D * W1])
            w_agg = sb("w_agg", [2 * D, D])
            w_self = sb("w_self", [D, D])
            vecs = sb("vecs", [NB, 3, D])
            tails = sb("tails", [P, P])
            tails_t = sb("tails_t", [P, P])
            carry_t = sb("carry_t", [P, P])
            carry = sb("carry", [P, P])
            max3, sum3 = (a[:].rearrange("p (f t) -> p f t", t=W1) for a in (run_max, run_sum))
            source_rows = Gathers(sem, "source", stepped)
            names = ("layer_loaded", "sage_masks", "sage_scanned", "sage_rows", "sage_stored", "sage_chain",
                     "node_chain", "silu_in", "silu_out", "h_put2", "sage_zeroed")
            (layer_loaded, masks, scanned, rows_ready, rows_stored, schain, nodechain, silu_in,
             silu_out, h_put2, sage_zeroed) = (sem(n) for n in names)
            ends_got = [sem(f"ends_got{i}") for i in range(NGT)]
            norm = Norm(norms, stat, 2 * LAYERS)
            agg_ready, turned_out, held_out, made, added = (
                sem("conv_" + n) for n in ("agg_ready", "turned", "held", "made", "added"))
            fix = Carry(sem, "sage", stepped)

            with nc.Block() as block:

                @block.vector
                def _(dve):
                    nc.vector.memset(run_max[:], 0.0).then_inc(sage_zeroed, 1)
                    nc.vector.memset(run_sum[:], 0.0).then_inc(sage_zeroed, 1)
                    dve.wait_ge(sage_zeroed, 2)
                    source_rows.split_rows(dve, nc, hl[:], parts, agg[:, :, 0:D], 0)

                @block.sync
                def _(sp):
                    source_rows.give_tokens(sp)
                    source_rows.load_first(sp, t["src_pad"], by_tile, index, tile_src, 0)

            with nc.Fori(0, LAYERS) as L:
                with ExitStack() as ctx2:
                    sb, ps = tiles(ctx2, "sage_edges")
                    hots = sb("hots", [NB, RING, source_rows.xt * P], BF16)
                    ps_pick = ps("ps_pick", [P, 2, source_rows.xt // PAIR, 512])
                    got = sb("got", [P, 2, TC, D])
                    turned = sb("turned", [P, D * W1])
                    mask_max = sb("mask_max", [P, D * W1], BF16)
                    mask_sum = sb("mask_sum", [P, D * W1], BF16)
                    both = sb("both", [P, TC, 2 * D])
                    in3, mm3, ms3 = (a[:].rearrange("p (f t) -> p f t", t=W1) for a in (turned, mask_max, mask_sum))
                    rows_by_part = scan_rows.rearrange("(p t) d -> p t d", t=T)

                    with nc.Block() as block:

                        @block.sync
                        def _(sp):
                            sp.dma_start(w_agg[:], t["w_agg"][bass.ds(L * (2 * D), 2 * D), :]).then_inc(layer_loaded, 16)
                            sp.dma_start(w_self[:], t["w_self"][bass.ds(L * D, D), :]).then_inc(layer_loaded, 16)
                            sp.dma_start(vecs[:], bc(t["conv_vecs"][bass.ds(L, 1), :, :], [NB, 3, D])).then_inc(layer_loaded, 16)
                            with sp.Fori(0, NCH // 2 - 1) as g:
                                for k in range(2):
                                    sp.wait_ge(source_rows.used[k], L * (NCH // 2) + g + 2)
                                    source_rows.load_index(sp, t["src_pad"], by_tile, index, tile_src, k, g + 1, L)
                            sp.wait_ge(layer_loaded, L * 48 + 48)
                            sp.sem_inc(stepped, 1)

                        @block.gpsimd
                        def _(pool):
                            source_rows.gather(pool, h_rows, index, got, L)

                        @block.scalar
                        def _(act):
                            def step(i, k, g, first=False):
                                c = L * NCH + i
                                nc.scalar.activation(mm3, bc(keep_big[:, bass.ds(i, 1), :], [P, D, W1]),
                                                     ACT.Copy).then_inc(masks, 1)
                                nc.scalar.activation(ms3, bc(keep[:, bass.ds(i, 1), :], [P, D, W1]),
                                                     ACT.Copy).then_inc(masks, 1)
                                source_rows.wait_gathered(act, k, g, L)
                                act.wait_ge(source_rows.picked, c + 3)
                                nc.scalar.activation(in3[:, :, 1:W1], got[:, k, :, :].rearrange("p t f -> p f t"),
                                                     ACT.Copy).then_inc(source_rows.used[k], 1)
                                act.wait_ge(scanned, c * 2 + 1)
                                if not first:
                                    act.wait_ge(rows_stored, c * 16)
                                nc.scalar.activation(both[:, :, 0:D].rearrange("p t f -> p f t"), max3[:, :, 1:W1],
                                                     ACT.Copy).then_inc(rows_ready, 1)
                                act.wait_ge(scanned, c * 2 + 2)
                                nc.scalar.activation(both[:, :, D:2 * D].rearrange("p t f -> p f t"), sum3[:, :, 1:W1],
                                                     ACT.Copy).then_inc(rows_ready, 1)
                                act.wait_ge(rows_ready, c * 2 + 2)
                                act.dma_start(rows_by_part[:, bass.ds(i * TC, TC), :], both[:]).then_inc(rows_stored, 16)

                            step(0, 0, 0, first=True)
                            with act.Fori(0, NCH // 2 - 1) as g:
                                step(g * 2 + 1, 1, g)
                                step(g * 2 + 2, 0, g + 1)
                            step(NCH - 1, 1, NCH // 2 - 1)
                            act.wait_ge(rows_stored, L * (16 * NCH) + 16 * NCH)
                            act.sem_inc(stepped, 1)

                        @block.vector
                        def _(dve):
                            v = nc.vector

                            def hots_of(i, k, g, a0, a1):
                                source_rows.make_hots(dve, nc, hots, tile_src, node_id, L * NCH + i, k, g, L, a0, a1)

                            def scan(i, k, g, which):
                                c = L * NCH + i
                                if which == 0:
                                    dve.wait_ge(masks, c * 2 + 2)
                                    dve.wait_ge(source_rows.used[k], L * (NCH // 2) + g + 2)
                                out3, out, mask, keeps, joins = ((max3, run_max, mask_max, ALU.min, ALU.max),
                                                                 (sum3, run_sum, mask_sum, ALU.mult, ALU.add))[which]
                                Chain(dve, schain, c * 2 + which)(v.tensor_copy(in3[:, :, 0:1], out3[:, :, TC:W1]))
                                v.tensor_tensor_scan(out[:], mask[:], turned[:], 0.0, keeps, joins).then_inc(scanned, 1)
                                dve.wait_ge(scanned, c * 2 + (which + 1))

                            def add_parts(i, k, g):
                                source_rows.add_parts(dve, nc, ps_pick, got, L * NCH + i, k, g, L, 2)

                            def step(i, k, g, g_next):
                                hots_of(i + 1, 1 - k, g_next, 0, 8)
                                add_parts(i, k, g)
                                hots_of(i + 1, 1 - k, g_next, 8, 14)
                                scan(i, k, g, 0)
                                hots_of(i + 1, 1 - k, g_next, 14, 19)
                                scan(i, k, g, 1)
                                hots_of(i + 1, 1 - k, g_next, 19, NA)

                            hots_of(0, 0, 0, 0, NA)
                            with dve.Fori(0, NCH // 2 - 1) as g:
                                step(g * 2, 0, g, g)
                                step(g * 2 + 1, 1, g, g + 1)
                            step(NCH - 2, 0, NCH // 2 - 1, NCH // 2 - 1)
                            add_parts(NCH - 1, 1, NCH // 2 - 1)
                            scan(NCH - 1, 1, NCH // 2 - 1, 0)
                            scan(NCH - 1, 1, NCH // 2 - 1, 1)
                            dve.sem_inc(stepped, 1)

                        @block.tensor
                        def _(pe):
                            with pe.Fori(0, NCH // 2) as g:
                                for k in range(2):
                                    source_rows.pick(pe, nc, ps_pick, hots, parts, L * NCH + g * 2 + k, k, 2)

                with ExitStack() as ctx2:
                    sb, ps = tiles(ctx2, "sage_nodes")
                    y = sb("y", [NB, NA, D])
                    big = sb("big", [NB, NA, D])
                    scratch = sb("scratch", [NB, NA, D])
                    agg_t = sb("agg_t", [P, NA * NB])
                    self_t = sb("self_t", [D, NA * NB])
                    ps_turn = ps("ps_turn", [P, 2, 512])
                    ps_out = ps("ps_out", [P, 2, 512])
                    ps_carry = ps("ps_carry", [P, 2, 512])
                    groups = pieces(NA, TG)
                    FIRST = 4
                    assert FIRST + 3 == NGT
                    halves = (slice(0, FIRST * TG), slice(FIRST * TG, NA))
                    with nc.Block() as block:

                        @block.sync
                        def _(sp):
                            source_rows.load_first(sp, t["src_pad"], by_tile, index, tile_src, L + 1)
                            sp.wait_ge(silu_out, L * 3 + 2)
                            sp.dma_start(nodes(h_rows[0:N, :]), hl[:].rearrange("b a d -> b (a d)")).then_inc(h_put2, 16)
                            sp.wait_ge(h_put2, L * 16 + 16)
                            sp.sem_inc(stepped, 1)

                        @block.gpsimd
                        def _(pool):
                            for i, (a0, n) in enumerate(groups):
                                for a in range(a0, a0 + n):
                                    pool.indirect_dma_start(agg[:, a, :], None, scan_rows,
                                                            bass.IndirectOffsetOnAxis(ap=end_row[:, a:a + 1], axis=0)
                                                            ).then_inc(ends_got[i], 16)
                            for i, (a0, n) in enumerate(groups):
                                pool.wait_ge(ends_got[i], L * (16 * n) + 16 * n)
                            pool.sem_inc(stepped, 1)

                        @block.vector
                        def _(dve):
                            v = nc.vector
                            per = 1 + NGT + 2 * (Norm.LINKS + 1)
                            link = Chain(dve, nodechain, L * per)
                            v.tensor_copy(tails[:, 0:D].unsqueeze(2), max3[:, :, TC:W1]).then_inc(fix.tails_ready, 1)
                            v.tensor_copy(tails[:, D:2 * D].unsqueeze(2), sum3[:, :, TC:W1]).then_inc(fix.tails_ready, 1)
                            link(v.tensor_tensor(res[:], res[:], bc(vecs[:, 2, :].unsqueeze(1), [NB, NA, D]), ALU.add))
                            fix.scan(dve, nc, ps_carry, tails_t, carry_t, carry, carry_mask, L)

                            def with_bias(i):
                                a0, n = groups[i]
                                dve.wait_ge(made, L * NGT + i + 1)
                                v.tensor_tensor(y[:, a0:a0 + n, :],
                                                ps_out[0:NB, i % 2, 0:n * D].rearrange("p (a f) -> p a f", f=D),
                                                bc(vecs[:, 0, :].unsqueeze(1), [NB, n, D]), ALU.add).then_inc(added, 1)

                            def finish(h):
                                at = halves[h]
                                norm.scale(dve, nc, link, y[:], L * 2 + h, at)
                                link(v.tensor_tensor(y[:, at, :], y[:, at, :],
                                                     bc(vecs[:, 1, :].unsqueeze(1), [NB, at.stop - at.start, D]), ALU.mult))
                                v.tensor_tensor(y[:, at, :], y[:, at, :], res[:, at, :], ALU.add).then_inc(silu_in, 1)

                            for i, (a0, n) in enumerate(groups):
                                at = slice(a0, a0 + n)
                                dve.wait_ge(ends_got[i], L * (16 * n) + 16 * n)
                                fix.add(dve, nc, ps_carry, agg, big, no_carry, i, L)
                                v.tensor_tensor(agg[:, at, D:2 * D], agg[:, at, D:2 * D],
                                                bc(in_share[:, at].unsqueeze(2), [NB, n, D]), ALU.mult).then_inc(agg_ready, 1)
                                link(v.tensor_tensor(agg[:, at, 0:D], agg[:, at, 0:D], big[:, at, :], ALU.max))
                                v.tensor_tensor(agg[:, at, 0:D], agg[:, at, 0:D],
                                                bc(has_in[:, at].unsqueeze(2), [NB, n, D]), ALU.mult).then_inc(agg_ready, 1)
                                if i:
                                    with_bias(i - 1)
                                if i == FIRST:
                                    dve.wait_ge(added, L * NGT + FIRST)
                                    norm.centre(nc, link, y[:], halves[0])
                                elif i == FIRST + 1:
                                    norm.variance(nc, link, y[:], scratch[:], halves[0])
                                elif i == FIRST + 2:
                                    finish(0)
                            with_bias(NGT - 1)
                            dve.wait_ge(added, L * NGT + NGT)
                            norm.centre(nc, link, y[:], halves[1])
                            norm.variance(nc, link, y[:], scratch[:], halves[1])
                            finish(1)
                            dve.wait_ge(silu_out, L * 3 + 2)
                            source_rows.split_rows(dve, nc, hl[:], parts, scratch[:], L + 1)
                            dve.sem_inc(stepped, 1)
                            assert link.n == per, (link.n, per)

                        @block.scalar
                        def _(act):
                            def hold(out, i, at):
                                act.wait_ge(turned_out, L * (2 * NGT) + i + 1)
                                a0, n = at
                                nc.scalar.activation(out[:, a0 * NB:(a0 + n) * NB], ps_turn[0:out.shape[0], i % 2, 0:n * NB],
                                                     ACT.Copy).then_inc(held_out, 1)

                            def silu(h, at):
                                act.wait_ge(silu_in, L * 2 + (h + 1))
                                nc.scalar.activation(hl[:, at, :], y[:, at, :], ACT.Silu).then_inc(silu_out, 1)

                            for i, at in enumerate(groups):
                                hold(self_t, i, at)
                            for i, at in enumerate(groups):
                                hold(agg_t, NGT + i, at)
                                if i == FIRST + 1:
                                    norm.act(act, nc, L * 2, halves[0])
                            norm.act(act, nc, L * 2 + 1, halves[1])
                            for h in range(2):
                                silu(h, halves[h])
                            nc.scalar.activation(res[:], y[:], ACT.Silu).then_inc(silu_out, 1)

                        @block.tensor
                        def _(pe):
                            def turn(src, i, at):
                                if i >= 2:
                                    pe.wait_ge(held_out, L * (2 * NGT) + (i - 1))
                                    pe.sem_inc(stepped, 1)
                                a0, n = at
                                for j in range(n):
                                    ins = nc.tensor.transpose(ps_turn[0:src.shape[2], i % 2, j * NB:(j + 1) * NB],
                                                              src[:, a0 + j, :], ident[0:NB, 0:NB])
                                ins.then_inc(turned_out, 1)

                            fix.turn(pe, nc, ps_carry, tails, carry_t, ident, L)
                            for i, at in enumerate(groups):
                                turn(hl, i, at)
                            fix.turn_back(pe, nc, ps_carry, carry_t, ident, L)
                            for i in range(2):
                                fix.bring(pe, nc, ps_carry, carry, carry_from, i, L)
                            for i, (a0, n) in enumerate(groups):
                                pe.wait_ge(agg_ready, L * (2 * NGT) + (2 * i + 2))
                                pe.sem_inc(stepped, 1)
                                turn(agg, NGT + i, (a0, n))
                                if i + 2 < NGT:
                                    fix.bring(pe, nc, ps_carry, carry, carry_from, i + 2, L)
                                pe.wait_ge(held_out, L * (2 * NGT) + (NGT + i + 1))
                                if i >= 2:
                                    pe.wait_ge(added, L * NGT + (i - 1))
                                for j in range(n):
                                    for first, held, w in ((True, agg_t, w_agg), (False, self_t, w_self)):
                                        ins = nc.tensor.matmul(ps_out[0:NB, i % 2, j * D:(j + 1) * D],
                                                               held[:, (a0 + j) * NB:(a0 + j + 1) * NB], w[:],
                                                               start=first, stop=not first)
                                ins.then_inc(made, 1)

        HID = 4 * D
        attr = sb_top("attr", [K10 + 1, 2, TC, P])
        with ExitStack() as ctx:
            sb, ps = tiles(ctx, "mlp")
            z = sb("z", [NB, NA, HID])
            scratch = sb("scratch", [NB, NA, HID])
            y = sb("y", [NB, NA, D])
            heldA = sb("heldA", [P, NA * NB])
            heldB = sb("heldB", [P, NA * NB])
            w_in = sb("w_in", [D, HID])
            w_out = sb("w_out", [P, 2, D])
            w_gain = sb("w_gain", [P, 2, D])
            b_in = sb("b_in", [NB, HID])
            cols = sb("cols", [P, 2, 2])
            share = sb("share", [NB, 2, NA])
            ps_shift = ps("ps_shift", [P, 512])
            b_out = sb("b_out", [NB, D])
            zero_bias = sb("zero_bias", [NB, D])
            ps_turn = ps("ps_turn", [P, 2, 512])
            ps_out = ps("ps_out", [P, 2, 512])
            held = [heldA, heldB]
            mlp_loaded, mchain, msilu_in, msilu_out, z_ready, x3_ready, x3_put = (
                sem("mlp_" + n) for n in ("loaded", "chain", "silu_in", "silu_out", "z_ready", "x3_ready", "x3_put"))
            norm2 = Norm(norms, stat)
            var_in, root_out, shift_made = (
                sem("mlp_" + n) for n in ("var_in", "root_out", "shift_made"))
            mlp1 = Linear(products, [hl[:]], [w_in[:]], HID)
            mlp2 = Linear(products, [z[:, :, 0:P], z[:, :, P:HID]], [w_gain[:, 0, :], w_gain[:, 1, :]], D)
            with nc.Block() as block:

                @block.sync
                def _(sp):
                    sp.dma_start(w_in[:], t["w_mlp1"]).then_inc(mlp_loaded, 16)
                    sp.dma_start(w_out[:], t["w_mlp2"].rearrange("(s k) f -> k s f", s=2)).then_inc(mlp_loaded, 16)
                    sp.dma_start(b_in[:], bc(t["b_mlp1"], [NB, HID])).then_inc(mlp_loaded, 16)
                    sp.dma_start(cols[:], t["mlp_cols"]).then_inc(mlp_loaded, 16)
                    sp.dma_start(b_out[:], bc(t["b_mlp2"], [NB, D])).then_inc(mlp_loaded, 16)
                    sp.wait_ge(x3_ready, 1)
                    sp.dma_start(nodes(h_rows[0:N, :]), h[:].rearrange("b a d -> b (a d)")).then_inc(x3_put, 16)
                    sp.wait_ge(x3_put, 16)

                @block.vector
                def _(dve):
                    v = nc.vector
                    link = Chain(dve, mchain)
                    link(v.memset(attr[:], 1.0))
                    dve.wait_ge(mlp_loaded, 80)
                    link(v.memset(zero_bias[:], 0.0))
                    link(v.tensor_tensor(w_gain[:], w_out[:], bc(cols[:, 0, :].unsqueeze(2), [P, 2, D]), ALU.mult))
                    dve.wait_ge(shift_made, 1)
                    link(v.tensor_tensor(b_out[:], b_out[:], ps_shift[0:NB, 0:D], ALU.add))
                    mlp1.dve(dve, nc, ps_out, b_in, z)
                    dve.sem_inc(msilu_in, 1)
                    shape = [NB, NA, HID]
                    dve.wait_ge(msilu_out, 1)
                    link(v.tensor_reduce(share[:, 0, :], z[:], AX, ALU.add))
                    link(v.tensor_scalar(share[:, 0, :], share[:, 0, :], 1.0 / HID, None, ALU.mult))
                    v.tensor_tensor(z[:], z[:], bc(share[:, 0, :].unsqueeze(2), shape), ALU.subtract).then_inc(z_ready, 1)
                    dve.wait_ge(z_ready, 1)
                    link(v.tensor_tensor(scratch[:], z[:], z[:], ALU.mult))
                    link(v.tensor_reduce(share[:, 1, :], scratch[:], AX, ALU.add))
                    v.tensor_scalar(share[:, 1, :], share[:, 1, :], 1.0 / HID, EPS, ALU.mult, ALU.add).then_inc(var_in, 1)
                    mlp2.dve(dve, nc, ps_out, zero_bias, y)
                    dve.wait_ge(root_out, 1)
                    link(v.reciprocal(share[:, 1, :], share[:, 0, :]))
                    link(v.tensor_tensor(y[:], y[:], bc(share[:, 1, :].unsqueeze(2), [NB, NA, D]), ALU.mult))
                    link(v.tensor_tensor(y[:], y[:], bc(b_out[:].unsqueeze(1), [NB, NA, D]), ALU.add))
                    link(v.tensor_tensor(h[:], h[:], y[:], ALU.add))
                    norm2.dve(dve, nc, link, h[:], scratch[:, :, 0:D])
                    dve.sem_inc(x3_ready, 1)
                    source_rows.split_rows(dve, nc, h[:], parts, y[:], LAYERS + 1)

                @block.scalar
                def _(act):
                    mlp1.act(act, nc, ps_turn, held)
                    act.wait_ge(msilu_in, 1)
                    nc.scalar.activation(z[:], z[:], ACT.Silu).then_inc(msilu_out, 1)
                    mlp2.act(act, nc, ps_turn, held)
                    act.wait_ge(var_in, 1)
                    nc.scalar.activation(share[:, 0, :], share[:, 1, :], ACT.Sqrt).then_inc(root_out, 1)
                    norm2.act(act, nc)

                @block.tensor
                def _(pe):
                    pe.wait_ge(mlp_loaded, 80)
                    for s in range(2):
                        ins = nc.tensor.matmul(ps_shift[0:NB, 0:D], bc(cols[:, 1, s:s + 1], [P, NB]), w_out[:, s, :],
                                               start=(s == 0), stop=(s == 1))
                    ins.then_inc(shift_made, 1)
                    mlp1.pe(pe, nc, ps_turn, ps_out, held, ident)
                    pe.wait_ge(z_ready, 1)
                    mlp2.pe(pe, nc, ps_turn, ps_out, held, ident)

        with ExitStack() as ctx:
            sb, ps = tiles(ctx, "last")
            agg = sb("agg", [NB, NA, 2 * D])
            run_sum = sb("run_sum", [P, D * W1])
            sum3 = run_sum[:].rearrange("p (f t) -> p f t", t=W1)
            (e_zeroed, e_masks, e_scanned, e_rows, e_stored, e_chain, e_w, e_made, e_turned) = (
                sem("edge_" + n) for n in ("zeroed", "masks", "scanned", "rows", "stored", "chain", "w",
                                           "made", "turned"))
            e_loaded = [sem(f"edge_loaded_k{k}") for k in range(2)]
            source_rows.xt, source_rows.tp = PICKED_LAST, TC - PICKED_LAST
            L = LAYERS
            sum_rows = nc.dram_tensor("sum_rows", [EP, D], F32).ap()
            with ExitStack() as ctx2:
                sb, ps = tiles(ctx2, "last_edges")
                hots = sb("hots", [NB, RING, source_rows.xt * P], BF16)
                ps_pick = ps("ps_pick", [P, 1, source_rows.xt // PAIR, 512])
                got = sb("got", [P, 2, TC, D])
                msg = sb("msg", [P, TC, D])
                turned = sb("turned", [P, D * W1])
                mask_sum = sb("mask_sum", [P, D * W1], BF16)
                both = sb("both", [P, TC, D])
                w_edge = sb("w_edge", [K10 + 1, D])
                ps_edge = ps("ps_edge", [P, 4, 512])
                in3, ms3 = (a[:].rearrange("p (f t) -> p f t", t=W1) for a in (turned, mask_sum))
                ps_flat = ps_edge[:].rearrange("p b x -> p (b x)")[:, 0:TC * D].rearrange("p (t f) -> p t f", f=D)
                rows_by_part = sum_rows.rearrange("(p t) d -> p t d", t=T)

                with nc.Block() as block:

                    @block.sync
                    def _(sp):
                        sp.sem_inc(e_made, 2)
                        sp.dma_start(w_edge[:], t["w_edge"]).then_inc(e_w, 16)
                        for k in range(2):
                            sp.wait_ge(e_made, 1 + k)
                            sp.dma_start(attr[0:K10, k, :, :], t["edge10"][:, k * TC:(k + 1) * TC, :]).then_inc(e_loaded[k], 16)
                        with sp.Fori(0, NCH // 2 - 1) as g:
                            for k in range(2):
                                sp.wait_ge(source_rows.used[k], g + (L * (NCH // 2) + 2))
                                source_rows.load_index(sp, t["src_pad"], by_tile, index, tile_src, k, g + 1, L)
                                sp.wait_ge(e_made, g * 2 + (k + 3))
                                sp.dma_start(attr[0:K10, k, :, :], t["edge10"][:, bass.ds((g * 2 + (2 + k)) * TC, TC), :]
                                             ).then_inc(e_loaded[k], 16)

                    @block.gpsimd
                    def _(pool):
                        source_rows.gather(pool, h_rows, index, got, L)

                    @block.scalar
                    def _(act):
                        def step(i, k, g, first=False):
                            nc.scalar.activation(ms3, bc(keep[:, bass.ds(i, 1), :], [P, D, W1]),
                                                 ACT.Copy).then_inc(e_masks, 1)
                            act.wait_ge(source_rows.used[k], g + (L * (NCH // 2) + 2))
                            nc.scalar.activation(in3[:, :, 1:W1], msg[:].rearrange("p t f -> p f t"),
                                                 ACT.Relu).then_inc(e_turned, 1)
                            act.wait_ge(e_scanned, i + 1)
                            if not first:
                                act.wait_ge(e_stored, i * 16)
                            nc.scalar.activation(both[:].rearrange("p t f -> p f t"), sum3[:, :, 1:W1],
                                                 ACT.Copy).then_inc(e_rows, 1)
                            act.wait_ge(e_rows, i + 1)
                            act.dma_start(rows_by_part[:, bass.ds(i * TC, TC), :], both[:]).then_inc(e_stored, 16)

                        step(0, 0, 0, first=True)
                        with act.Fori(0, NCH // 2 - 1) as g:
                            step(g * 2 + 1, 1, g)
                            step(g * 2 + 2, 0, g + 1)
                        step(NCH - 1, 1, NCH // 2 - 1)
                        act.wait_ge(e_stored, 16 * NCH)

                    @block.vector
                    def _(dve):
                        v = nc.vector
                        v.memset(run_sum[:], 0.0).then_inc(e_zeroed, 1)
                        dve.wait_ge(e_zeroed, 1)

                        def hots_of(i, k, g, a0, a1):
                            source_rows.make_hots(dve, nc, hots, tile_src, node_id, i + L * NCH, k, g, L, a0, a1)

                        def add_parts(i, k, g):
                            source_rows.add_parts(dve, nc, ps_pick, got, i + L * NCH, k, g, L, 1)

                        def message(i, k, g):
                            source_rows.wait_gathered(dve, k, g, L)
                            dve.wait_ge(source_rows.picked, i + (L * NCH + 3))
                            dve.wait_ge(e_made, i + 3)
                            v.tensor_tensor(msg[:], got[:, k, :, :], ps_flat, ALU.add).then_inc(source_rows.used[k], 1)

                        def scan(i):
                            dve.wait_ge(e_masks, i + 1)
                            dve.wait_ge(e_turned, i + 1)
                            Chain(dve, e_chain, i)(v.tensor_copy(in3[:, :, 0:1], sum3[:, :, TC:W1]))
                            v.tensor_tensor_scan(run_sum[:], mask_sum[:], turned[:], 0.0, ALU.mult,
                                                 ALU.add).then_inc(e_scanned, 1)
                            dve.wait_ge(e_scanned, i + 1)

                        def step(i, k, g, g_next):
                            hots_of(i + 1, 1 - k, g_next, 0, 5)
                            add_parts(i, k, g)
                            hots_of(i + 1, 1 - k, g_next, 5, 10)
                            message(i, k, g)
                            hots_of(i + 1, 1 - k, g_next, 10, 18)
                            scan(i)
                            hots_of(i + 1, 1 - k, g_next, 18, NA)

                        hots_of(0, 0, 0, 0, NA)
                        with dve.Fori(0, NCH // 2 - 1) as g:
                            step(g * 2, 0, g, g)
                            step(g * 2 + 1, 1, g, g + 1)
                        step(NCH - 2, 0, NCH // 2 - 1, NCH // 2 - 1)
                        add_parts(NCH - 1, 1, NCH // 2 - 1)
                        message(NCH - 1, 1, NCH // 2 - 1)
                        scan(NCH - 1)

                    @block.tensor
                    def _(pe):
                        pe.wait_ge(e_w, 16)
                        with pe.Fori(0, NCH // 2) as g:
                            for k in range(2):
                                c = g * 2 + k
                                source_rows.pick(pe, nc, ps_pick, hots, parts, c + L * NCH, k, 1)
                                pe.wait_ge(e_loaded[k], g * 16 + 16)
                                pe.wait_ge(source_rows.used[1 - k], g + (L * (NCH // 2) + 1 + k))
                                for j in range(TC):
                                    ins = nc.tensor.matmul(ps_edge[:, j // 8, (j % 8) * D:(j % 8 + 1) * D],
                                                           attr[:, k, j, :], w_edge[:], start=True, stop=True)
                                ins.then_inc(e_made, 1)

            with ExitStack() as ctx2:
                sb, ps = tiles(ctx2, "last_nodes")
                y = sb("y", [NB, NA, D])
                y2 = sb("y2", [NB, NA, D])
                scratch = sb("scratch", [NB, NA, D])
                heldA = sb("heldA", [P, NA * NB])
                tails = sb("tails", [P, P])
                tails_t = sb("tails_t", [P, P])
                carry_t = sb("carry_t", [P, P])
                carry = sb("carry", [P, P])
                w1 = sb("w1", [D, D])
                w2 = sb("w2", [D, D])
                vec = sb("vec", [NB, 4, D])
                ones = sb("ones", [NB, NB])
                bn = sb("bn", [NB, 4, D])
                ps_turn = ps("ps_turn", [P, 2, 512])
                ps_out = ps("ps_out", [P, 2, 512])
                ps_carry = ps("ps_carry", [P, 2, 512])
                ps_bn = ps("ps_bn", [P, 2, 512])
                held = [heldA]
                (f_loaded, fchain, f_in, f_hid, f_out, f_sum, f_root, f_root_out, f_done, f_put) = (
                    sem("last_" + n) for n in ("loaded", "chain", "in", "hid", "out", "sum", "root", "root_out",
                                               "done", "put"))
                l1 = Linear(products, [y2[:]], [w1[:]], D)
                l2 = Linear(products, [y[:]], [w2[:]], D)
                norm3 = Norm(norms, stat)
                with nc.Block() as block:

                    @block.sync
                    def _(sp):
                        sp.dma_start(w1[:], t["w_last1"]).then_inc(f_loaded, 16)
                        sp.dma_start(w2[:], t["w_last2"]).then_inc(f_loaded, 16)
                        sp.dma_start(vec[:], bc(t["last_vecs"].unsqueeze(0), [NB, 4, D])).then_inc(f_loaded, 16)
                        sp.wait_ge(f_done, 1)
                        sp.dma_start(nodes(out), h[:].rearrange("b a d -> b (a d)")).then_inc(f_put, 16)
                        sp.wait_ge(f_put, 16)

                    @block.gpsimd
                    def _(pool):
                        for i, (a0, n) in enumerate(pieces(NA, TG)):
                            for a in range(a0, a0 + n):
                                pool.indirect_dma_start(agg[:, a, D:2 * D], None, sum_rows,
                                                        bass.IndirectOffsetOnAxis(ap=end_row[:, a:a + 1], axis=0)
                                                        ).then_inc(ends_got[i], 16)
                        for i, (a0, n) in enumerate(pieces(NA, TG)):
                            pool.wait_ge(ends_got[i], (LAYERS + 1) * 16 * n)

                    @block.vector
                    def _(dve):
                        v = nc.vector
                        link = Chain(dve, fchain)
                        v.memset(tails[:, 0:D], 0.0).then_inc(fix.tails_ready, 1)
                        v.tensor_copy(tails[:, D:2 * D].unsqueeze(2), sum3[:, :, TC:W1]).then_inc(fix.tails_ready, 1)
                        fix.scan(dve, nc, ps_carry, tails_t, carry_t, carry, carry_mask, L)
                        for i, (a0, n) in enumerate(pieces(NA, TG)):
                            dve.wait_ge(ends_got[i], (LAYERS + 1) * 16 * n)
                            fix.add(dve, nc, ps_carry, agg, None, None, i, L)
                        link(v.tensor_tensor(y2[:], agg[:, :, D:2 * D], bc(has_in[:].unsqueeze(2), [NB, NA, D]), ALU.mult))
                        v.tensor_tensor(y2[:], y2[:], h[:], ALU.add).then_inc(f_in, 1)
                        dve.wait_ge(f_loaded, 48)
                        l1.dve(dve, nc, ps_out, vec[:, 0, :], y)
                        v.tensor_scalar(y[:], y[:], 0.0, None, ALU.max).then_inc(f_hid, 1)
                        l2.dve(dve, nc, ps_out, vec[:, 1, :], y2)
                        link(v.memset(ones[:], 1.0))
                        v.tensor_scalar(y2[:], y2[:], 0.0, None, ALU.max).then_inc(f_out, 1)
                        dve.wait_ge(f_sum, 1)
                        link(v.tensor_scalar(bn[:, 0, :], ps_bn[0:NB, 0, 0:D], 1.0 / N, None, ALU.mult))
                        link(v.tensor_tensor(y2[:], y2[:], bc(bn[:, 0, :].unsqueeze(1), [NB, NA, D]), ALU.subtract))
                        v.tensor_tensor(scratch[:], y2[:], y2[:], ALU.mult).then_inc(f_out, 1)
                        dve.wait_ge(f_sum, 2)
                        v.tensor_scalar(bn[:, 1, :], ps_bn[0:NB, 1, 0:D], 1.0 / N, EPS, ALU.mult, ALU.add).then_inc(f_root, 1)
                        dve.wait_ge(f_root_out, 1)
                        link(v.reciprocal(bn[:, 3, :], bn[:, 2, :]))
                        link(v.tensor_tensor(bn[:, 3, :], bn[:, 3, :], vec[:, 2, :], ALU.mult))
                        link(v.tensor_tensor(y2[:], y2[:], bc(bn[:, 3, :].unsqueeze(1), [NB, NA, D]), ALU.mult))
                        link(v.tensor_tensor(y2[:], y2[:], bc(vec[:, 3, :].unsqueeze(1), [NB, NA, D]), ALU.add))
                        link(v.tensor_tensor(h[:], h[:], y2[:], ALU.add))
                        norm3.dve(dve, nc, link, h[:], scratch[:])
                        dve.sem_inc(f_done, 1)

                    @block.scalar
                    def _(act):
                        l1.act(act, nc, ps_turn, held)
                        l2.act(act, nc, ps_turn, held)
                        act.wait_ge(f_root, 1)
                        nc.scalar.activation(bn[:, 2, :], bn[:, 1, :], ACT.Sqrt).then_inc(f_root_out, 1)
                        norm3.act(act, nc)

                    @block.tensor
                    def _(pe):
                        fix.turn(pe, nc, ps_carry, tails, carry_t, ident, L)
                        fix.turn_back(pe, nc, ps_carry, carry_t, ident, L)
                        for i in range(NGT):
                            fix.bring(pe, nc, ps_carry, carry, carry_from, i, L)
                        pe.wait_ge(f_loaded, 48)
                        pe.wait_ge(f_in, 1)
                        l1.pe(pe, nc, ps_turn, ps_out, held, ident)
                        pe.wait_ge(f_hid, 1)
                        l2.pe(pe, nc, ps_turn, ps_out, held, ident)
                        for i, tile in enumerate((y2, scratch)):
                            pe.wait_ge(f_out, i + 1)
                            for a in range(NA):
                                ins = nc.tensor.matmul(ps_bn[0:NB, i, 0:D], ones[:], tile[:, a, :], start=(a == 0),
                                                       stop=(a == NA - 1))
                            ins.then_inc(f_sum, 1)


def kernel(**inputs):
    import numpy as np
    import concourse.bacc as bacc
    from concourse.bass_utils import run_bass_kernel_spmd

    a = {k: np.asarray(v) for k, v in inputs.items()}

    def lay(ap):
        return np.ascontiguousarray(ap)

    def edges(v, fill):
        padded = np.full((EP,) + v.shape[1:], fill, v.dtype)
        padded[:E] = v
        return padded

    attr = edges(a["edge_attr_10"], 0)
    w1 = a["L1_gnn_W1"]
    arrays = {
        "x": a["x"], "node_vec": a["node_vec"],
        "src_pad": edges(a["src"], N).reshape(P, T), "dst_pad": edges(a["dst"], N).reshape(P, T),
        "src_turned": edges(a["src"], N).reshape(P, T).T.reshape(P, T),
        "edge64": edges(a["edge_attr_64"], 0), "edge10": attr.reshape(P, T, K10).transpose(2, 1, 0),
        "w_curv": a["L0_gnn_W_curv"].reshape(1, D), "b_curv": a["L0_gnn_b_curv"].reshape(1, D),
        "w_lin0": a["L0_gnn_W_lin"].T, "b_lin0": a["L0_gnn_b_lin"].reshape(1, D),
        "w_l1x": w1[0:D], "w_l1v": w1[D:2 * D], "w_l1u": w1[2 * D:3 * D], "b_l1h": a["L1_gnn_b1"].reshape(1, D),
        "w_l1o": a["L1_gnn_W2"], "b_l1o": a["L1_gnn_b2"].reshape(1, D), "u0": a["L1_gnn_u"][0].reshape(D, 1),
        "w_adapt": a["L2_gnn_adapter_w"].T, "b_adapt": a["L2_gnn_adapter_b"].reshape(1, D),
        "w_agg": a["L2_gnn_conv_wl"].transpose(0, 2, 1).reshape(-1, D), "w_self": a["L2_gnn_conv_wr"].transpose(0, 2, 1).reshape(-1, D),
        "conv_vecs": np.stack([a["L2_gnn_conv_bl"], a["L2_gnn_ln_g"], a["L2_gnn_ln_b"]], 1),
        "w_mlp1": a["L2_gnn_mlp_w1"].T, "w_mlp2": a["L2_gnn_mlp_w2"].T, "b_mlp2": a["L2_gnn_mlp_b2"].reshape(1, D),
        "b_mlp1": a["L2_gnn_mlp_b1"].reshape(1, -1),
        "mlp_cols": np.stack([a["L2_gnn_mlp_ln_g"], a["L2_gnn_mlp_ln_b"]]).reshape(2, 2, P).transpose(2, 0, 1),
        "w_edge": np.concatenate([a["L3_gnn_W_edge"], a["L3_gnn_b_edge"][None]]),
        "w_last1": a["L3_gnn_W1"], "w_last2": a["L3_gnn_W2"],
        "last_vecs": np.stack([a["L3_gnn_b1"], a["L3_gnn_b2"], a["L3_gnn_bn_gamma"], a["L3_gnn_bn_beta"]]),
    }
    arrays = {"in_" + k: lay(v) for k, v in arrays.items()}
    nc = bacc.Bacc("TRN2", target_bir_lowering=False, num_devices=1)
    t = {k[3:]: nc.dram_tensor(k, v.shape, mybir.dt.from_np(v.dtype), kind="ExternalInput").ap() for k, v in arrays.items()}
    out = nc.dram_tensor("out_0", (N, D), F32, kind="ExternalOutput").ap()
    program(nc, t, out)
    return run_bass_kernel_spmd(nc, [arrays], core_ids=[0]).results[0]["out_0"]
```
